# Optimizing a Trainium2 kernel written in Bass

```python
import numpy as np
import jax
import jax.numpy as jnp

def _softmax(x, axis=-1):
    return jax.nn.softmax(x, axis=axis)

def _gelu(x):
    return jax.nn.gelu(x, approximate=True)

def _silu(x):
    return jax.nn.silu(x)

def _sigmoid(x):
    return jax.nn.sigmoid(x)

def _layernorm(x, axis=-1, eps=1e-05):
    m = jnp.mean(x, axis=axis, keepdims=True)
    v = jnp.var(x, axis=axis, keepdims=True)
    return (x - m) / jnp.sqrt(v + eps)

def _scatter_add(tgt, idx, src, axis=0):
    return tgt.at[idx].add(src)

def _segment_sum(src, seg, n):
    return jax.ops.segment_sum(src, seg, n)
kernel_name = 'mk_vit_tower_cls_d1_tok_img512_r4_ab0b83'

def setup_inputs(seed: int=0):
    np.random.seed(seed)
    _w = jnp.asarray

    def _rec_inputs():
        import jax
        import jax.numpy as jnp
        _rk = jax.random.key(seed)
        x = 7.57192e-06 + 1.00007 * jax.random.normal(jax.random.fold_in(_rk, 1), (64, 3, 224, 224), jnp.float32)
        cls_tok = 0.02 * jax.random.normal(jax.random.fold_in(_rk, 5), (1, 1, 128), jnp.float32)
        return (x, cls_tok)
    x, cls_tok = _rec_inputs()

    def _L0_tok_setup():
        import jax, jax.numpy as jnp
        import numpy as np
        DEPTH = 4
        HEADS = 8
        DIM = 128
        HID = 256
        P = 16
        IMG = 224
        GRID = IMG // P
        NPATCH = GRID * GRID
        NTOK = NPATCH + 1
        BATCH = 64
        EPS = 1e-05

        def layernorm(x, w, b):
            mu = jnp.mean(x, axis=-1, keepdims=True)
            var = jnp.mean(jnp.square(x - mu), axis=-1, keepdims=True)
            return (x - mu) * jax.lax.rsqrt(var + EPS) * w + b
        key = jax.random.key(seed)
        ks = jax.random.split(key, 12)
        s = 0.02
        inp = {'x': jax.random.normal(ks[0], (BATCH, 3, IMG, IMG), jnp.float32), 'conv_w': jax.random.normal(ks[1], (3 * P * P, DIM), jnp.float32) * s, 'conv_b': jnp.zeros((DIM,), jnp.float32), 'cls_token': jax.random.normal(ks[2], (1, 1, DIM), jnp.float32) * s, 'pos_embed': jax.random.normal(ks[3], (1, NTOK, DIM), jnp.float32) * s, 'ln1_w': jnp.ones((DEPTH, DIM), jnp.float32), 'ln1_b': jnp.zeros((DEPTH, DIM), jnp.float32), 'qkv_w': jax.random.normal(ks[4], (DEPTH, DIM, 3 * DIM), jnp.float32) * s, 'qkv_b': jnp.zeros((DEPTH, 3 * DIM), jnp.float32), 'proj_w': jax.random.normal(ks[5], (DEPTH, DIM, DIM), jnp.float32) * s, 'proj_b': jnp.zeros((DEPTH, DIM), jnp.float32), 'ln2_w': jnp.ones((DEPTH, DIM), jnp.float32), 'ln2_b': jnp.zeros((DEPTH, DIM), jnp.float32), 'fc1_w': jax.random.normal(ks[6], (DEPTH, DIM, HID), jnp.float32) * s, 'fc1_b': jnp.zeros((DEPTH, HID), jnp.float32), 'fc2_w': jax.random.normal(ks[7], (DEPTH, HID, DIM), jnp.float32) * s, 'fc2_b': jnp.zeros((DEPTH, DIM), jnp.float32), 'norm_w': jnp.ones((DIM,), jnp.float32), 'norm_b': jnp.zeros((DIM,), jnp.float32)}
        return inp
    _L0_tok_all = _L0_tok_setup()
    _L0_tok_in = {k: v for k, v in _L0_tok_all.items() if k in ('conv_w', 'conv_b', 'cls_token', 'pos_embed', 'ln1_w', 'ln1_b', 'qkv_w', 'qkv_b', 'proj_w', 'proj_b', 'ln2_w', 'ln2_b', 'fc1_w', 'fc1_b', 'fc2_w', 'fc2_b', 'norm_w', 'norm_b')}
    del _L0_tok_all

    def _L0_attn_setup():
        import jax, jax.numpy as jnp
        import numpy as np
        NUM_HEADS = 8
        TOPK_RATIO = 0.1
        key = jax.random.key(seed)
        ks = jax.random.split(key, 8)
        B, N, D = (1, 128, 128)
        f = lambda k, s, sc=1.0: jax.random.normal(k, s, dtype=jnp.float32) * sc
        return {'x': f(ks[0], (B, N, D)), 'Wq': f(ks[1], (D, D), 0.02), 'Wk': f(ks[2], (D, D), 0.02), 'Wv': f(ks[3], (D, D), 0.02), 'Wo': f(ks[4], (D, D), 0.02), 'pW1': f(ks[5], (64, 1), 0.5), 'pb1': jnp.zeros((64,), jnp.float32), 'pW2': f(ks[6], (1, 64), 0.5), 'pb2': jnp.zeros((1,), jnp.float32)}
    _L0_attn_all = _L0_attn_setup()
    _L0_attn_in = {k: v for k, v in _L0_attn_all.items() if k in ('Wq', 'Wk', 'Wv', 'Wo', 'pW1', 'pb1', 'pW2', 'pb2')}
    del _L0_attn_all

    def _L0_ffn_setup():
        import jax, jax.numpy as jnp
        import numpy as np
        from jax import lax
        N_HEADS = 8
        D_KEYS = 128
        HALF = D_KEYS // 2
        N_KEYS = 64
        TOP_K = 8
        D_MODEL = 128

        def _forward(queries, Wq, bq, keys, w_down, w_up):
            N, T, D = queries.shape
            x = queries.reshape(-1, D)
            q = (x @ Wq + bq).reshape(-1, N_HEADS, D_KEYS)
            q1, q2 = (q[..., :HALF], q[..., HALF:])
            s1 = jnp.einsum('bhc,hnc->bhn', q1, keys[:, 0])
            s2 = jnp.einsum('bhc,hnc->bhn', q2, keys[:, 1])
            s1t, i1 = lax.top_k(s1, TOP_K)
            s2t, i2 = lax.top_k(s2, TOP_K)
            all_scores = (s1t[..., :, None] + s2t[..., None, :]).reshape(-1, N_HEADS, TOP_K * TOP_K)
            all_idx = (i1[..., :, None] * N_KEYS + i2[..., None, :]).reshape(-1, N_HEADS, TOP_K * TOP_K)
            scores, best = lax.top_k(all_scores, TOP_K)
            indices = jnp.take_along_axis(all_idx, best, axis=-1)
            w_d = w_down[indices]
            w_u = w_up[indices]
            inner = jnp.einsum('bd,bhkd->bhk', x, w_d)
            vals = jax.nn.relu(inner) * jax.nn.softmax(scores, axis=-1)
            out = jnp.einsum('bhk,bhkd->bd', vals, w_u)
            return out.reshape(N, T, D)
        key = jax.random.key(seed)
        ks = jax.random.split(key, 6)
        N, T = (2, 256)
        queries = jax.random.normal(ks[0], (N, T, D_MODEL), dtype=jnp.float32)
        Wq = jax.random.normal(ks[1], (D_MODEL, N_HEADS * D_KEYS), dtype=jnp.float32) / np.sqrt(D_MODEL)
        bq = jnp.zeros((N_HEADS * D_KEYS,), dtype=jnp.float32)
        bound = 1.0 / np.sqrt(HALF)
        keys = jax.random.uniform(ks[2], (N_HEADS, 2, N_KEYS, HALF), dtype=jnp.float32, minval=-bound, maxval=bound)
        w_down = jax.random.normal(ks[3], (N_KEYS * N_KEYS, D_MODEL), dtype=jnp.float32) * 0.02
        w_up = jax.random.normal(ks[4], (N_KEYS * N_KEYS, D_MODEL), dtype=jnp.float32) * 0.02
        return {'queries': queries, 'Wq': Wq, 'bq': bq, 'keys': keys, 'w_down': w_down, 'w_up': w_up}
    _L0_ffn_all = _L0_ffn_setup()
    _L0_ffn_in = {k: v for k, v in _L0_ffn_all.items() if k in ('Wq', 'bq', 'keys', 'w_down', 'w_up')}
    del _L0_ffn_all
    return {'x': x, 'cls_tok': cls_tok, 'L0_tok_conv_w': _L0_tok_in['conv_w'], 'L0_tok_conv_b': _L0_tok_in['conv_b'], 'L0_tok_cls_token': _L0_tok_in['cls_token'], 'L0_tok_pos_embed': _L0_tok_in['pos_embed'], 'L0_tok_ln1_w': _L0_tok_in['ln1_w'], 'L0_tok_ln1_b': _L0_tok_in['ln1_b'], 'L0_tok_qkv_w': _L0_tok_in['qkv_w'], 'L0_tok_qkv_b': _L0_tok_in['qkv_b'], 'L0_tok_proj_w': _L0_tok_in['proj_w'], 'L0_tok_proj_b': _L0_tok_in['proj_b'], 'L0_tok_ln2_w': _L0_tok_in['ln2_w'], 'L0_tok_ln2_b': _L0_tok_in['ln2_b'], 'L0_tok_fc1_w': _L0_tok_in['fc1_w'], 'L0_tok_fc1_b': _L0_tok_in['fc1_b'], 'L0_tok_fc2_w': _L0_tok_in['fc2_w'], 'L0_tok_fc2_b': _L0_tok_in['fc2_b'], 'L0_tok_norm_w': _L0_tok_in['norm_w'], 'L0_tok_norm_b': _L0_tok_in['norm_b'], 'L0_attn_Wq': _L0_attn_in['Wq'], 'L0_attn_Wk': _L0_attn_in['Wk'], 'L0_attn_Wv': _L0_attn_in['Wv'], 'L0_attn_Wo': _L0_attn_in['Wo'], 'L0_attn_pW1': _L0_attn_in['pW1'], 'L0_attn_pb1': _L0_attn_in['pb1'], 'L0_attn_pW2': _L0_attn_in['pW2'], 'L0_attn_pb2': _L0_attn_in['pb2'], 'L0_ffn_Wq': _L0_ffn_in['Wq'], 'L0_ffn_bq': _L0_ffn_in['bq'], 'L0_ffn_keys': _L0_ffn_in['keys'], 'L0_ffn_w_down': _L0_ffn_in['w_down'], 'L0_ffn_w_up': _L0_ffn_in['w_up']}

def reference(x, cls_tok, L0_tok_conv_w, L0_tok_conv_b, L0_tok_cls_token, L0_tok_pos_embed, L0_tok_ln1_w, L0_tok_ln1_b, L0_tok_qkv_w, L0_tok_qkv_b, L0_tok_proj_w, L0_tok_proj_b, L0_tok_ln2_w, L0_tok_ln2_b, L0_tok_fc1_w, L0_tok_fc1_b, L0_tok_fc2_w, L0_tok_fc2_b, L0_tok_norm_w, L0_tok_norm_b, L0_attn_Wq, L0_attn_Wk, L0_attn_Wv, L0_attn_Wo, L0_attn_pW1, L0_attn_pb1, L0_attn_pW2, L0_attn_pb2, L0_ffn_Wq, L0_ffn_bq, L0_ffn_keys, L0_ffn_w_down, L0_ffn_w_up):
    import jax
    import jax.numpy as jnp

    def _L0_tok_ref(x, conv_w, conv_b, cls_token, pos_embed, ln1_w, ln1_b, qkv_w, qkv_b, proj_w, proj_b, ln2_w, ln2_b, fc1_w, fc1_b, fc2_w, fc2_b, norm_w, norm_b):
        import jax, jax.numpy as jnp
        import numpy as np
        DEPTH = 4
        HEADS = 8
        DIM = 128
        HID = 256
        P = 16
        IMG = 224
        GRID = IMG // P
        NPATCH = GRID * GRID
        NTOK = NPATCH + 1
        BATCH = 64
        EPS = 1e-05

        def layernorm(x, w, b):
            mu = jnp.mean(x, axis=-1, keepdims=True)
            var = jnp.mean(jnp.square(x - mu), axis=-1, keepdims=True)
            return (x - mu) * jax.lax.rsqrt(var + EPS) * w + b
        B = x.shape[0]
        hd = DIM // HEADS
        scale = hd ** (-0.5)
        patches = x.reshape(B, 3, GRID, P, GRID, P)
        patches = patches.transpose(0, 2, 4, 1, 3, 5).reshape(B, NPATCH, 3 * P * P)
        tok = patches @ conv_w + conv_b
        cls = jnp.broadcast_to(cls_token, (B, 1, DIM))
        h = jnp.concatenate([cls, tok], axis=1) + pos_embed
        for i in range(DEPTH):
            y = layernorm(h, ln1_w[i], ln1_b[i])
            qkv = (y @ qkv_w[i] + qkv_b[i]).reshape(B, NTOK, 3, HEADS, hd)
            qkv = qkv.transpose(2, 0, 3, 1, 4)
            q, k, v = (qkv[0], qkv[1], qkv[2])
            attn = jax.nn.softmax(jnp.einsum('bhnd,bhmd->bhnm', q, k) * scale, axis=-1)
            o = jnp.einsum('bhnm,bhmd->bhnd', attn, v)
            o = o.transpose(0, 2, 1, 3).reshape(B, NTOK, DIM)
            h = h + (o @ proj_w[i] + proj_b[i])
            y = layernorm(h, ln2_w[i], ln2_b[i])
            y = jax.nn.gelu(y @ fc1_w[i] + fc1_b[i], approximate=False)
            h = h + (y @ fc2_w[i] + fc2_b[i])
        return layernorm(h, norm_w, norm_b)

    def _L0_attn_ref(x, Wq, Wk, Wv, Wo, pW1, pb1, pW2, pb2):
        import jax, jax.numpy as jnp
        import numpy as np
        NUM_HEADS = 8
        TOPK_RATIO = 0.1
        B, N, D = x.shape
        H = NUM_HEADS
        dh = D // H

        def heads(y):
            return y.reshape(B, N, H, dh).transpose(0, 2, 1, 3)
        Q = heads(x @ Wq.T)
        K = heads(x @ Wk.T)
        V = heads(x @ Wv.T)
        alpha = jnp.einsum('bhnd,bhsd->bhns', Q, K) * dh ** 0.25
        mag = jnp.abs(alpha)
        hid = jax.nn.silu(jax.lax.stop_gradient(mag)[..., None] * pW1[:, 0] + pb1)
        phase = hid @ pW2[0] + pb2[0]
        re = alpha * jnp.cos(phase)
        im = alpha * jnp.sin(phase)
        babs = jnp.sqrt(re * re + im * im)
        probs = babs / (babs.sum(-1, keepdims=True) + 1e-08)
        k = max(1, int(TOPK_RATIO * N))
        tp, ti = jax.lax.top_k(probs, k)
        tp = tp / (tp.sum(-1, keepdims=True) + 1e-08)
        Vg = jax.vmap(jax.vmap(lambda v, i: v[i]))(V, ti)
        out = jnp.einsum('bhnk,bhnkd->bhnd', tp, Vg)
        out = out.transpose(0, 2, 1, 3).reshape(B, N, D)
        return out @ Wo.T

    def _L0_ffn_ref(queries, Wq, bq, keys, w_down, w_up):
        import jax, jax.numpy as jnp
        import numpy as np
        from jax import lax
        N_HEADS = 8
        D_KEYS = 128
        HALF = D_KEYS // 2
        N_KEYS = 64
        TOP_K = 8
        D_MODEL = 128

        def _forward(queries, Wq, bq, keys, w_down, w_up):
            N, T, D = queries.shape
            x = queries.reshape(-1, D)
            q = (x @ Wq + bq).reshape(-1, N_HEADS, D_KEYS)
            q1, q2 = (q[..., :HALF], q[..., HALF:])
            s1 = jnp.einsum('bhc,hnc->bhn', q1, keys[:, 0])
            s2 = jnp.einsum('bhc,hnc->bhn', q2, keys[:, 1])
            s1t, i1 = lax.top_k(s1, TOP_K)
            s2t, i2 = lax.top_k(s2, TOP_K)
            all_scores = (s1t[..., :, None] + s2t[..., None, :]).reshape(-1, N_HEADS, TOP_K * TOP_K)
            all_idx = (i1[..., :, None] * N_KEYS + i2[..., None, :]).reshape(-1, N_HEADS, TOP_K * TOP_K)
            scores, best = lax.top_k(all_scores, TOP_K)
            indices = jnp.take_along_axis(all_idx, best, axis=-1)
            w_d = w_down[indices]
            w_u = w_up[indices]
            inner = jnp.einsum('bd,bhkd->bhk', x, w_d)
            vals = jax.nn.relu(inner) * jax.nn.softmax(scores, axis=-1)
            out = jnp.einsum('bhk,bhkd->bd', vals, w_u)
            return out.reshape(N, T, D)
        return _forward(queries, Wq, bq, keys, w_down, w_up)
    h = _L0_tok_ref(x, L0_tok_conv_w, L0_tok_conv_b, L0_tok_cls_token, L0_tok_pos_embed, L0_tok_ln1_w, L0_tok_ln1_b, L0_tok_qkv_w, L0_tok_qkv_b, L0_tok_proj_w, L0_tok_proj_b, L0_tok_ln2_w, L0_tok_ln2_b, L0_tok_fc1_w, L0_tok_fc1_b, L0_tok_fc2_w, L0_tok_fc2_b, L0_tok_norm_w, L0_tok_norm_b)
    h = jnp.concatenate([jnp.broadcast_to(cls_tok, (h.shape[0], 1, h.shape[2])), h], axis=1)
    h = h + _L0_attn_ref(_layernorm(h, axis=-1), L0_attn_Wq, L0_attn_Wk, L0_attn_Wv, L0_attn_Wo, L0_attn_pW1, L0_attn_pb1, L0_attn_pW2, L0_attn_pb2)
    h = h + _L0_ffn_ref(_layernorm(h, axis=-1), L0_ffn_Wq, L0_ffn_bq, L0_ffn_keys, L0_ffn_w_down, L0_ffn_w_up)
    return h

_drawn_inputs = setup_inputs


def setup_inputs(seed=0):
    import zlib

    import numpy as np

    out = dict(_drawn_inputs(seed))
    spreads = {'L0_tok_conv_b': (0.0, 0.1),
     'L0_tok_ln1_w': (1.0, 0.6),
     'L0_tok_ln1_b': (0.0, 0.489),
     'L0_tok_qkv_b': (0.0, 0.1),
     'L0_tok_proj_b': (0.0, 0.1),
     'L0_tok_ln2_w': (1.0, 0.6),
     'L0_tok_ln2_b': (0.0, 0.667),
     'L0_tok_fc1_b': (0.0, 0.1),
     'L0_tok_fc2_b': (0.0, 0.1),
     'L0_tok_norm_w': (1.0, 0.2),
     'L0_tok_norm_b': (0.0, 0.1),
     'L0_attn_pb1': (0.0, 0.8),
     'L0_ffn_bq': (0.0, 0.8)}
    factors = {'cls_tok': 8.0,
     'L0_tok_cls_token': 8.0,
     'L0_attn_Wq': 5.531,
     'L0_attn_Wk': 5.282,
     'L0_attn_pW1': 8.0,
     'L0_attn_pW2': 8.0,
     'L0_ffn_Wq': 8.0,
     'L0_ffn_keys': 8.0,
     'L0_ffn_w_down': 8.0,
     'L0_ffn_w_up': 8.0}
    for name, (base, spread) in spreads.items():
        noise = np.random.default_rng([zlib.crc32(name.encode()), seed]).standard_normal(out[name].shape)
        drawn = base * np.exp(spread * noise) if base else spread * noise
        out[name] = jnp.asarray(drawn.astype(out[name].dtype))
    for name, factor in factors.items():
        out[name] = (out[name] * factor).astype(out[name].dtype)
    return out
```

```python
from contextlib import ExitStack

import concourse.bass as bass
from concourse import mybir

ALU = mybir.AluOpType
ACT = mybir.ActivationFunctionType
AX = mybir.AxisListType
F32 = mybir.dt.float32

DIM = 128
HEADS = 8
HD = DIM // HEADS
HID = 256
PATCHES = 196
TOK = PATCHES + 1
C = 99
W = 2 * C
KC = 3 * 16 * 16 // 128
G = 4
EPS = 1e-5
QW, KW, VW, PW, F1W, F2W = 0, 256, 512, 640, 768, 1024
VB, PB, F2B = 1280, 1408, 1536
LN1W, LN1B, LN2W, LN2B, QB, KB, F1B = 1664, 1665, 1666, 1667, 1668, 1670, 1672
NW = 1674


class Count:

    made = []

    def __init__(self, sem, per):
        self.sem, self.per = sem, per
        Count.made.append(self)

    def after(self, it, k):
        return it * self.per + (k + 1)


def start(nc):
    with nc.Block() as block:
        @block.gpsimd
        def _(pool):
            for count in Count.made:
                pool.sem_inc(count.sem, 1)
    Count.made.clear()


def build_tower(nc, ctx, B, DEPTH, x_in, base_in, convw_in, layer_in, h, ident):
    NG = B // G
    sb = lambda name, shape: ctx.enter_context(nc.sbuf_tensor(name, shape, F32))
    sem = lambda name: ctx.enter_context(nc.semaphore(name))

    XB = 3
    with ExitStack() as c2:
        xbuf = c2.enter_context(nc.sbuf_tensor("xbuf", [128, XB, KC, W], F32))
        convw = c2.enter_context(nc.sbuf_tensor("convw", [128, KC, DIM], F32))
        base = c2.enter_context(nc.sbuf_tensor("base", [C, 2, 2, DIM], F32))
        emb = [c2.enter_context(nc.psum_tensor(f"emb{i}", [C, 2, DIM], F32)) for i in range(2)]
        x_loaded = [sem(f"x_loaded{i}") for i in range(XB)]
        consts_loaded, x_pad, emb_done, emb_taken, base_done = (
            sem(n) for n in ("consts_loaded", "x_pad", "emb_done", "emb_taken", "base_done"))
        block = c2.enter_context(nc.Block())

        @block.sync
        def _(sp):
            sp.wait_ge(x_pad, 1)
            sp.dma_start(convw[:], convw_in).then_inc(consts_loaded, 16)
            sp.dma_start(base[:], base_in).then_inc(consts_loaded, 16)
            for i in range(B):
                if i >= XB:
                    sp.wait_ge(emb_done, i - XB + 1)
                sp.dma_start(xbuf[:, i % XB, :, 0:PATCHES], x_in[i]).then_inc(x_loaded[i % XB], 16)

        @block.tensor
        def _(pe):
            pe.wait_ge(consts_loaded, 32)
            for i in range(B):
                pe.wait_ge(x_loaded[i % XB], 16 * (i // XB + 1))
                if i >= 2:
                    pe.wait_ge(emb_taken, i - 1)
                for c in range(2):
                    for k in range(KC):
                        mm = nc.tensor.matmul(emb[i % 2][:, c, :], xbuf[:, i % XB, k, c * C:c * C + C],
                                              convw[:, k, :], start=(k == 0), stop=(k == KC - 1))
                mm.then_inc(emb_done, 1)

        @block.vector
        def _(dve):
            nc.vector.memset(xbuf[:, :, :, PATCHES:W], 0.0).then_inc(x_pad, 1)
            dve.wait_ge(consts_loaded, 32)
            nc.vector.tensor_tensor(base[:, 0], base[:, 0], base[:, 1], ALU.add).then_inc(base_done, 1)
            dve.wait_ge(base_done, 1)
            for i in range(B):
                dve.wait_ge(emb_done, i + 1)
                nc.vector.tensor_tensor(h[:, i], emb[i % 2][:], base[:, 0], ALU.add).then_inc(emb_taken, 1)

    with ExitStack() as c2:
        sb = lambda name, shape: c2.enter_context(nc.sbuf_tensor(name, shape, F32))
        wts = sb("wts", [128, NW])
        stats = sb("stats", [C, G, 2, 6])
        mv = sb("mv", [C, G, 2, 2])
        rstd = sb("rstd", [C, G, 2])
        neghalf = sb("neghalf", [C, G, 2])
        z = sb("z", [C, G, 2, DIM])
        yT = sb("yT", [128, G, W])
        qT = sb("qT", [128, 2, G, W])
        kT = sb("kT", [128, 2, G, W])
        vaug = sb("vaug", [C, G, 2, HEADS, HD + 1])
        negmax = sb("negmax", [C, 2, 2, 2, 4, 32])
        probs = sb("probs", [C, 4, 2, 2, W])
        rsum = sb("rsum", [C, 2, HEADS])
        o = sb("o", [C, G, 2, DIM])
        oT = sb("oT", [128, G, W])
        gT = sb("gT", [128, G // 2, 2, 2, W])
        SC = [c2.enter_context(nc.psum_tensor(f"SC{i}", [C, 512], F32)) for i in range(2)]
        ST = [c2.enter_context(nc.psum_tensor(f"ST{i}", [C, 2, 512], F32)) for i in range(2)]
        WK = [c2.enter_context(nc.psum_tensor(f"WK{i}", [128, 512], F32)) for i in range(2)]

        uses = []
        for ln in ("ln1", "ln2"):
            for a in range(G // 2):
                uses.append((ln, a))
                if ln == "ln1":
                    uses += [("q0", a), ("q1", a), ("k0", a), ("k1", a), ("v", a)]
                else:
                    uses += [("f1_0", a), ("f1_1", a)]
            if ln == "ln1":
                for j in range(G + 1):
                    if j >= 1:
                        uses.append(("av", j - 1))
                    if j < G:
                        uses.append(("max", j))
                for a in range(G // 2):
                    uses += [("oT", a), ("proj", a)]
        uses += [("f2", a) for a in range(G // 2)]
        assert len(uses) % 2 == 0
        place = {u: (n % 2, n // 2) for n, u in enumerate(uses)}

        work_ready = [Count(sem(f"work_ready{b}"), len(uses) // 2) for b in range(2)]
        work_taken = [Count(sem(f"work_taken{b}"), len(uses) // 2) for b in range(2)]
        wts_loaded = sem("wts_loaded")
        filled = sem("filled")
        spare = sem("spare")
        stats_done = Count(sem("stats_done"), 2 * 2 * G)
        mv_done = Count(sem("mv_done"), 2)
        veps_done = Count(sem("veps_done"), 2)
        rstd_done = Count(sem("rstd_done"), 2)
        z_done = Count(sem("z_done"), 2 * G)
        bias_added = Count(sem("bias_added"), 2)
        scores_ready = Count(sem("scores_ready"), G * HEADS)
        max_done = Count(sem("max_done"), G * HEADS)
        st_ready = Count(sem("st_ready"), G * 4)
        exp_done = Count(sem("exp_done"), G * 4)
        av_done = Count(sem("av_done"), G * 3)
        rsum_done = Count(sem("rsum_done"), G)
        start(nc)
        block = c2.enter_context(nc.Block())

        def steps(eng):
            with eng.Fori(0, DEPTH) as layer:
                eng.wait_ge(wts_loaded, layer * 16 + 16)
                eng.sem_inc(spare, 1)
                with eng.Fori(0, NG) as g:
                    yield layer * NG + g, g * G

        def ready(eng, it, use):
            b, n = place[use]
            eng.wait_ge(work_ready[b].sem, work_ready[b].after(it, n + 1))
            return WK[b]

        def taken(eng, it, use):
            b, n = place[use]
            eng.wait_ge(work_taken[b].sem, work_taken[b].after(it, n + 1))

        def free(eng, it, use):
            b, n = place[use]
            eng.wait_ge(work_taken[b].sem, work_taken[b].after(it, n))
            return WK[b]

        def signal_ready(use):
            return work_ready[place[use][0]].sem

        def signal_taken(use):
            return work_taken[place[use][0]].sem

        @block.sync
        def _(sp):
            lastb, lastn = place[("f2", G // 2 - 1)]
            with sp.Fori(0, DEPTH) as layer:
                for b in range(2):
                    sp.wait_ge(work_taken[b].sem, work_taken[b].after(layer * NG, 0))
                sp.dma_start(wts[:], layer_in[layer]).then_inc(wts_loaded, 16)

        @block.tensor
        def _(pe):
            pe.wait_ge(filled, 4)

            def norm_transposed(it, n, a):
                ps = free(pe, it, (f"ln{n + 1}", a))
                for j in (2 * a, 2 * a + 1):
                    pe.wait_ge(z_done.sem, z_done.after(it, n * G + j + 1))
                    for c in range(2):
                        mm = nc.tensor.transpose(ps[:, (j % 2) * W + c * C:(j % 2) * W + c * C + C], z[:, j, c, :], ident[0:C, 0:C])
                mm.then_inc(signal_ready((f"ln{n + 1}", a)), 1)

            def scores(it, j, hd):
                g, half = hd % 4, hd // 4
                u = j * HEADS + hd
                if u >= 2:
                    pe.wait_ge(max_done.sem, max_done.after(it, u - 1))
                if hd == 0 and j % 2 == 0:
                    for q in ("k0", "k1"):
                        taken(pe, it, (q, j // 2))
                for qc in range(2):
                    mm = nc.tensor.matmul(SC[u % 2][:, qc * W:qc * W + W],
                                          qT[32 * g:32 * g + HD, half, j, qc * C:qc * C + C],
                                          kT[32 * g:32 * g + HD, half, j, :], start=True, stop=True)
                mm.then_inc(scores_ready.sem, 1)

            def scores_t(it, j, p):
                u = j * 4 + p
                if u >= 2:
                    pe.wait_ge(exp_done.sem, exp_done.after(it, u - 1))
                if p == 0:
                    taken(pe, it, ("max", j))
                for hh in range(2):
                    hd = 2 * p + hh
                    g, half = hd % 4, hd // 4
                    for kc in range(2):
                        mm = nc.tensor.matmul(ST[u % 2][:, hh, kc * W:kc * W + W],
                                              kT[32 * g:32 * g + HD + 1, half, j, kc * C:kc * C + C],
                                              qT[32 * g:32 * g + HD + 1, half, j, :], start=True, stop=True)
                mm.then_inc(st_ready.sem, 1)

            def attend(it, j, p):
                if p == 0:
                    free(pe, it, ("av", j))
                    if j % 2 == 0:
                        taken(pe, it, ("v", j // 2))
                ps = WK[place[("av", j)][0]]
                pe.wait_ge(exp_done.sem, exp_done.after(it, 4 * j + p + 1))
                for hh in range(2):
                    hd = 2 * p + hh
                    for qc in range(2):
                        col = (qc * HEADS + hd) * (HD + 1)
                        for kc in range(2):
                            keys = C if kc == 0 else TOK - C
                            mm = nc.tensor.matmul(ps[0:C, col:col + HD + 1],
                                                  probs[0:keys, p, hh, kc, qc * C:qc * C + C],
                                                  vaug[0:keys, j, kc, hd, :], start=(kc == 0), stop=(kc == 1))
                if p == 3:
                    mm.then_inc(signal_ready(("av", j)), 1)
                else:
                    mm.then_inc(av_done.sem, 1)

            for it, img in steps(pe):
                for a in range(G // 2):
                    norm_transposed(it, 0, a)
                    pair = slice(2 * a, 2 * a + 2)
                    taken(pe, it, ("ln1", a))
                    for n, (name, col) in enumerate((("q0", QW), ("q1", QW + 128), ("k0", KW), ("k1", KW + 128))):
                        ps = free(pe, it, (name, a))
                        nc.tensor.matmul(ps[:, 0:2 * W], wts[:, col:col + 128], yT[:, pair, :],
                                         start=True, stop=True).then_inc(signal_ready((name, a)), 1)
                    ps = free(pe, it, ("v", a))
                    for j in (2 * a, 2 * a + 1):
                        for c in range(2):
                            n = (j % 2) * 2 + c
                            mm = nc.tensor.matmul(ps[0:C, n * 128:n * 128 + 128], yT[:, j, c * C:c * C + C],
                                                  wts[:, VW:VW + 128], start=True, stop=True)
                    mm.then_inc(signal_ready(("v", a)), 1)
                for j in range(G + 1):
                    for p in range(4):
                        if j < G:
                            scores(it, j, 2 * p)
                            scores(it, j, 2 * p + 1)
                        if j >= 1:
                            scores_t(it, j - 1, p)
                            if p >= 1:
                                attend(it, j - 1, p - 1)
                    if j >= 1:
                        attend(it, j - 1, 3)
                    if j < G:
                        ps = free(pe, it, ("max", j))
                        pe.wait_ge(max_done.sem, max_done.after(it, HEADS * (j + 1)))
                        for half in range(2):
                            for qc in range(2):
                                mm = nc.tensor.transpose(ps[:, half * W + qc * C:half * W + qc * C + C],
                                                         negmax[:, j % 2, qc, half].rearrange("p g e -> p (g e)"),
                                                         ident[0:C, 0:C])
                        mm.then_inc(signal_ready(("max", j)), 1)
                for a in range(G // 2):
                    ps = free(pe, it, ("oT", a))
                    for j in (2 * a, 2 * a + 1):
                        taken(pe, it, ("av", j))
                        for c in range(2):
                            mm = nc.tensor.transpose(ps[:, (j % 2) * W + c * C:(j % 2) * W + c * C + C], o[:, j, c, :], ident[0:C, 0:C])
                    mm.then_inc(signal_ready(("oT", a)), 1)
                    taken(pe, it, ("oT", a))
                    ps = free(pe, it, ("proj", a))
                    for j in (2 * a, 2 * a + 1):
                        for c in range(2):
                            n = (j % 2) * 2 + c
                            mm = nc.tensor.matmul(ps[0:C, n * 128:n * 128 + 128], oT[:, j, c * C:c * C + C],
                                                  wts[:, PW:PW + 128], start=True, stop=True)
                    mm.then_inc(signal_ready(("proj", a)), 1)
                for a in range(G // 2):
                    norm_transposed(it, 1, a)
                    taken(pe, it, ("ln2", a))
                    for hh in range(2):
                        ps = free(pe, it, (f"f1_{hh}", a))
                        nc.tensor.matmul(ps[:, 0:2 * W], wts[:, F1W + 128 * hh:F1W + 128 * hh + 128],
                                         yT[:, 2 * a:2 * a + 2, :], start=True, stop=True).then_inc(signal_ready((f"f1_{hh}", a)), 1)
                for a in range(G // 2):
                    ps = free(pe, it, ("f2", a))
                    taken(pe, it, ("f1_1", a))
                    taken(pe, it, ("f1_0", a))
                    for jj in range(2):
                        for c in range(2):
                            n = jj * 2 + c
                            for hh in range(2):
                                mm = nc.tensor.matmul(ps[0:C, n * 128:n * 128 + 128], gT[:, a, hh, jj, c * C:c * C + C],
                                                      wts[:, F2W + 128 * hh:F2W + 128 * hh + 128],
                                                      start=(hh == 0), stop=(hh == 1))
                    mm.then_inc(signal_ready(("f2", a)), 1)

        @block.scalar
        def _(act):
            def flat(t):
                return t.rearrange("p a b -> p (a b)")

            for it, img in steps(act):
                for a in range(G // 2):
                    pair = slice(2 * a, 2 * a + 2)
                    ps = ready(act, it, ("ln1", a))
                    nc.scalar.activation(flat(yT[:, pair, :]), ps[:, 0:2 * W], ACT.Identity,
                                         scale=wts[:, LN1W:LN1W + 1], bias=wts[:, LN1B:LN1B + 1]).then_inc(signal_taken(("ln1", a)), 1)
                    for half in range(2):
                        ps = ready(act, it, (f"k{half}", a))
                        nc.scalar.activation(flat(kT[:, half, pair, :]), ps[:, 0:2 * W], ACT.Identity,
                                             bias=wts[:, KB + half:KB + half + 1]).then_inc(signal_taken((f"k{half}", a)), 1)
                for j in range(G):
                    for p in range(4):
                        u = 4 * j + p
                        act.wait_ge(st_ready.sem, st_ready.after(it, u + 1))
                        if j >= 1:
                            if p < 3:
                                act.wait_ge(av_done.sem, av_done.after(it, 3 * (j - 1) + p + 1))
                            else:
                                ready(act, it, ("av", j - 1))
                        nc.scalar.activation(probs[:, p].rearrange("p h k w -> p h (k w)"), ST[u % 2][:, :, 0:2 * W],
                                             ACT.Exp).then_inc(exp_done.sem, 1)
                for a in range(G // 2):
                    ps = ready(act, it, ("oT", a))
                    nc.scalar.copy(flat(oT[:, 2 * a:2 * a + 2, :]), ps[:, 0:2 * W]).then_inc(signal_taken(("oT", a)), 1)
                for a in range(G // 2):
                    ps = ready(act, it, ("ln2", a))
                    nc.scalar.activation(flat(yT[:, 2 * a:2 * a + 2, :]), ps[:, 0:2 * W], ACT.Identity,
                                         scale=wts[:, LN2W:LN2W + 1], bias=wts[:, LN2B:LN2B + 1]).then_inc(signal_taken(("ln2", a)), 1)
                    for hh in range(2):
                        ps = ready(act, it, (f"f1_{hh}", a))
                        nc.scalar.activation(flat(gT[:, a, hh]), ps[:, 0:2 * W], ACT.Gelu,
                                             bias=wts[:, F1B + hh:F1B + hh + 1]).then_inc(signal_taken((f"f1_{hh}", a)), 1)



        @block.vector
        def _(dve):
            nc.vector.memset(negmax[:], 0.0).then_inc(filled, 1)
            nc.vector.memset(vaug[:], 1.0).then_inc(filled, 1)

            def normalise(it, img, n):
                for j in range(G):
                    for c in range(2):
                        nc.vector.bn_stats(stats[:, j, c, :], h[:, img + j, c, :]).then_inc(stats_done.sem, 1)
                for j in range(G):
                    for c in range(2):
                        dve.wait_ge(stats_done.sem, stats_done.after(it, 2 * G * n + 2 * j + c + 1))
                        dve.sem_inc(spare, 1)
                        agg = nc.vector.bn_aggr(mv[:, j, c, :], stats[:, j, c, :])
                agg.then_inc(mv_done.sem, 1)
                dve.wait_ge(rstd_done.sem, rstd_done.after(it, n + 1))
                for j in range(G):
                    for c in range(2):
                        zz = nc.vector.tensor_scalar(z[:, j, c, :], h[:, img + j, c, :], mv[:, j, c, 0:1],
                                                     rstd[:, j, c:c + 1], ALU.subtract, ALU.mult)
                    zz.then_inc(z_done.sem, 1)

            def add_to_h(it, img, name, n, a):
                if a == 0:
                    dve.wait_ge(bias_added.sem, bias_added.after(it, n + 1))
                ps = ready(dve, it, (name, a))
                hp = h[:, bass.ds(img + 2 * a, 2), :, :].rearrange("p i c d -> p (i c d)")
                nc.vector.tensor_tensor(hp, hp, ps[0:C, :], ALU.add).then_inc(signal_taken((name, a)), 1)

            for it, img in steps(dve):
                dve.sem_inc(spare, 1)
                normalise(it, img, 0)
                for a in range(G // 2):
                    pair = slice(2 * a, 2 * a + 2)
                    for half in range(2):
                        ps = ready(dve, it, (f"q{half}", a))
                        nc.vector.tensor_scalar(qT[:, half, pair, :].rearrange("p a b -> p (a b)"), ps[:, 0:2 * W],
                                                wts[:, QB + half:QB + half + 1], float(HD) ** -0.5, ALU.add, ALU.mult
                                                ).then_inc(signal_taken((f"q{half}", a)), 1)
                    ps = ready(dve, it, ("v", a))
                    for jj in range(2):
                        vv = nc.vector.tensor_tensor(
                            vaug[:, 2 * a + jj, :, :, 0:HD],
                            ps[0:C, jj * 256:jj * 256 + 256].rearrange("p (n h e) -> p n h e", n=2, h=HEADS),
                            wts[0:C, VB:VB + 128].rearrange("p (n h e) -> p n h e", n=1, h=HEADS).to_broadcast([C, 2, HEADS, HD]),
                            ALU.add)
                    vv.then_inc(signal_taken(("v", a)), 1)
                for j in range(G + 1):
                    if j < G:
                        for hd in range(HEADS):
                            u = j * HEADS + hd
                            g, half = hd % 4, hd // 4
                            dve.wait_ge(scores_ready.sem, scores_ready.after(it, u + 1))
                            if hd == 0 and j >= 2:
                                ready(dve, it, ("max", j - 2))
                            nc.vector.tensor_reduce(negmax[:, j % 2, :, half, g, HD:HD + 1],
                                                    SC[u % 2][:, 0:2 * W].rearrange("p (q k) -> p q k", q=2)[:, :, 0:TOK],
                                                    axis=AX.X, op=ALU.max, negate=True).then_inc(max_done.sem, 1)
                    if j >= 1:
                        ps = ready(dve, it, ("av", j - 1))
                        pv = ps[0:C, 0:2 * HEADS * (HD + 1)].rearrange("p (n e) -> p n e", e=HD + 1)
                        nc.vector.reciprocal(rsum[:].rearrange("p q h -> p (q h)"), pv[:, :, HD]).then_inc(rsum_done.sem, 1)
                        dve.wait_ge(rsum_done.sem, rsum_done.after(it, j))
                        nc.vector.tensor_tensor(o[:, j - 1].rearrange("p q (h e) -> p (q h) e", e=HD), pv[:, :, 0:HD],
                                                rsum[:].rearrange("p q (h e) -> p (q h) e", e=1).to_broadcast([C, 2 * HEADS, HD]),
                                                ALU.mult).then_inc(signal_taken(("av", j - 1)), 1)
                    if j < G:
                        ps = ready(dve, it, ("max", j))
                        qv = qT[:, :, j, :]
                        nc.vector.tensor_tensor(qv, qv, ps[:, 0:2 * W].rearrange("p (h w) -> p h w", h=2), ALU.add
                                                ).then_inc(signal_taken(("max", j)), 1)
                for a in range(G // 2):
                    add_to_h(it, img, "proj", 0, a)
                taken(dve, it, ("proj", G // 2 - 1))
                dve.sem_inc(spare, 1)
                normalise(it, img, 1)
                for a in range(G // 2):
                    add_to_h(it, img, "f2", 1, a)

        @block.gpsimd
        def _(pool):
            nc.gpsimd.memset(neghalf[:], -0.5).then_inc(filled, 1)
            nc.gpsimd.memset(rstd[:], 0.0).then_inc(filled, 1)
            pool.wait_ge(filled, 4)
            for it, img in steps(pool):
                for n, col in ((0, PB), (1, F2B)):
                    pool.wait_ge(mv_done.sem, mv_done.after(it, n + 1))
                    pool.sem_inc(spare, 1)
                    nc.gpsimd.tensor_scalar(rstd[:], mv[:, :, :, 1], EPS, None, ALU.add).then_inc(veps_done.sem, 1)
                    pool.wait_ge(veps_done.sem, veps_done.after(it, n + 1))
                    nc.gpsimd.tensor_tensor(rstd[:], rstd[:], neghalf[:], ALU.pow).then_inc(rstd_done.sem, 1)
                    pool.wait_ge(z_done.sem, z_done.after(it, G * n + G))
                    pool.sem_inc(spare, 1)
                    hp = h[:, bass.ds(img, G), :, :].rearrange("p i c d -> p (i c) d")
                    nc.gpsimd.tensor_tensor(hp, hp, wts[0:C, col:col + 128].rearrange("p (n d) -> p n d", n=1)
                                            .to_broadcast([C, 2 * G, DIM]), ALU.add).then_inc(bias_added.sem, 1)



def build_norm(nc, B, normw_in, cls_in, h):
    with ExitStack() as ctx:
        sb = lambda name, shape: ctx.enter_context(nc.sbuf_tensor(name, shape, F32))
        sem = lambda name: ctx.enter_context(nc.semaphore(name))
        wb = sb("norm_wb", [C, 2, DIM])
        stats = sb("n_stats", [C, G, 2, 6])
        mv = sb("n_mv", [C, G, 2, 2])
        rstd = sb("n_rstd", [C, G, 2])
        neghalf = sb("n_neghalf", [C, G, 2])
        z = sb("n_z", [C, 2, G, 2, DIM])
        loaded, spare, filled, cls_stored = sem("norm_loaded"), sem("n_spare"), sem("n_filled"), sem("cls_stored")
        stats_done = Count(sem("n_stats_done"), 2 * G)
        mv_done = Count(sem("n_mv_done"), 1)
        veps_done = Count(sem("n_veps_done"), 1)
        rstd_done = Count(sem("n_rstd_done"), 1)
        z_done = Count(sem("n_z_done"), 1)
        scaled = Count(sem("n_scaled"), 1)
        shifted = Count(sem("n_shifted"), 1)
        start(nc)
        block = ctx.enter_context(nc.Block())

        @block.sync
        def _(sp):
            sp.dma_start(wb[:], normw_in).then_inc(loaded, 16)
            sp.wait_ge(shifted.sem, shifted.after(B // G, 0))
            sp.dma_start(h[C - 1:C, :, 1, :], cls_in).then_inc(cls_stored, 16)
            sp.wait_ge(cls_stored, 16)

        @block.vector
        def _(dve):
            dve.wait_ge(loaded, 16)
            with dve.Fori(0, B // G) as it:
                for j in range(G):
                    for c in range(2):
                        nc.vector.bn_stats(stats[:, j, c, :], h[:, it * G + j, c, :]).then_inc(stats_done.sem, 1)
                dve.wait_ge(stats_done.sem, stats_done.after(it, 2 * G))
                dve.sem_inc(spare, 1)
                for j in range(G):
                    for c in range(2):
                        agg = nc.vector.bn_aggr(mv[:, j, c, :], stats[:, j, c, :])
                agg.then_inc(mv_done.sem, 1)
                dve.wait_ge(rstd_done.sem, rstd_done.after(it, 1))
                for j in range(G):
                    for c in range(2):
                        zz = nc.vector.tensor_scalar(z[:, 0, j, c, :], h[:, it * G + j, c, :], mv[:, j, c, 0:1],
                                                     rstd[:, j, c:c + 1], ALU.subtract, ALU.mult)
                zz.then_inc(z_done.sem, 1)
                dve.wait_ge(z_done.sem, z_done.after(it, 1))
                row = lambda n: wb[:, n:n + 1, :].to_broadcast([C, 2 * G, DIM])
                nc.vector.tensor_tensor(z[:, 1].rearrange("p j c d -> p (j c) d"), z[:, 0].rearrange("p j c d -> p (j c) d"),
                                        row(0), ALU.mult).then_inc(scaled.sem, 1)
                dve.wait_ge(scaled.sem, scaled.after(it, 1))
                nc.vector.tensor_tensor(h[:, bass.ds(it * G, G), :, :].rearrange("p j c d -> p (j c) d"),
                                        z[:, 1].rearrange("p j c d -> p (j c) d"), row(1), ALU.add).then_inc(shifted.sem, 1)

        @block.gpsimd
        def _(pool):
            nc.gpsimd.memset(neghalf[:], -0.5).then_inc(filled, 1)
            pool.wait_ge(filled, 1)
            with pool.Fori(0, B // G) as it:
                pool.wait_ge(mv_done.sem, mv_done.after(it, 1))
                pool.sem_inc(spare, 1)
                nc.gpsimd.tensor_scalar(rstd[:], mv[:, :, :, 1], EPS, None, ALU.add).then_inc(veps_done.sem, 1)
                pool.wait_ge(veps_done.sem, veps_done.after(it, 1))
                nc.gpsimd.tensor_tensor(rstd[:], rstd[:], neghalf[:], ALU.pow).then_inc(rstd_done.sem, 1)


AQ, AK, AV, AO = 0, 128, 256, 384
AMASK = 640
ANW = 648
TOPK = W // 10
SEG = 2 * HEADS


def build_attention(nc, B, attw_in, h, ident):
    A = 2
    with ExitStack() as ctx:
        sb = lambda name, shape: ctx.enter_context(nc.sbuf_tensor(name, shape, F32))
        sem = lambda name: ctx.enter_context(nc.semaphore(name))
        wts = sb("a_wts", [128, ANW])
        stats = sb("a_stats", [C, A, 2, 6])
        mv = sb("a_mv", [C, A, 2, 2])
        rstd = sb("a_rstd", [C, A, 2])
        neghalf = sb("a_neghalf", [C, A, 2])
        z = sb("a_z", [C, A, 2, DIM])
        zT = sb("a_zT", [128, A, W])
        qm = sb("a_qm", [128, HEADS, A, W])
        kT = sb("a_kT", [128, A, W])
        v = sb("a_v", [C, A, 2, 144])
        mag = sb("a_mag", [C, A, SEG, W])
        left = sb("a_left", [C, 2, SEG, W])
        top = sb("a_top", [C, SEG, 24])
        total = sb("a_total", [C, A, SEG])
        small = sb("a_small", [C, 6, SEG])
        wgt = sb("a_wgt", [C, SEG, W])
        wT = sb("a_wT", [C, 2, 2, W])
        oT = sb("a_oT", [128, 2, W])
        SC = [ctx.enter_context(nc.psum_tensor(f"a_SC{i}", [C, 512], F32)) for i in range(2)]
        WT = [ctx.enter_context(nc.psum_tensor(f"a_WT{i}", [C, 512], F32)) for i in range(2)]
        OT = ctx.enter_context(nc.psum_tensor("a_OT", [128, 512], F32))
        PR = ctx.enter_context(nc.psum_tensor("a_PR", [C, 512], F32))
        WK = [ctx.enter_context(nc.psum_tensor(f"a_WK{i}", [128, 512], F32)) for i in range(2)]
        uses = ["z", "q", "k", "v"]
        place = {u: (n % 2, n // 2) for n, u in enumerate(uses)}
        work_ready = [Count(sem(f"a_work_ready{b}"), 2) for b in range(2)]
        work_taken = [Count(sem(f"a_work_taken{b}"), 2) for b in range(2)]
        loaded, spare, filled = sem("a_loaded"), sem("a_spare"), sem("a_filled")
        stats_done = Count(sem("a_stats_done"), 2 * A)
        mv_done = Count(sem("a_mv_done"), 1)
        veps_done = Count(sem("a_veps_done"), 1)
        rstd_done = Count(sem("a_rstd_done"), 1)
        z_done = Count(sem("a_z_done"), 1)
        scores_ready = Count(sem("a_scores_ready"), A * HEADS)
        mag_done = Count(sem("a_mag_done"), A * HEADS)
        found = Count(sem("a_found"), A * 3)
        cleared = Count(sem("a_cleared"), A * 4)
        coef_done = Count(sem("a_coef_done"), A * 7)
        wgt_done = Count(sem("a_wgt_done"), A)
        scaled = Count(sem("a_scaled"), A)
        wT_ready = Count(sem("a_wT_ready"), A * HEADS)
        wT_taken = Count(sem("a_wT_taken"), A * HEADS)
        av_done = Count(sem("a_av_done"), A * HEADS)
        oT_taken = Count(sem("a_oT_taken"), A)
        proj_ready = Count(sem("a_proj_ready"), A)
        added = Count(sem("a_added"), A)
        start(nc)
        block = ctx.enter_context(nc.Block())
        steps = lambda eng: eng.Fori(0, B // A)

        def ready(eng, it, use):
            b, n = place[use]
            eng.wait_ge(work_ready[b].sem, work_ready[b].after(it, n + 1))
            return WK[b]

        def taken(eng, it, use):
            b, n = place[use]
            eng.wait_ge(work_taken[b].sem, work_taken[b].after(it, n + 1))

        def free(eng, it, use):
            b, n = place[use]
            eng.wait_ge(work_taken[b].sem, work_taken[b].after(it, n))
            return WK[b]

        def upto(eng, count, it, k):
            eng.wait_ge(count.sem, count.after(it, k))

        @block.sync
        def _(sp):
            sp.dma_start(wts[:], attw_in).then_inc(loaded, 16)

        @block.tensor
        def _(pe):
            pe.wait_ge(loaded, 16)
            with steps(pe) as it:
                ps = free(pe, it, "z")
                upto(pe, z_done, it, 1)
                for j in range(A):
                    for c in range(2):
                        mm = nc.tensor.transpose(ps[:, j * W + c * C:j * W + c * C + C], z[:, j, c, :], ident[0:C, 0:C])
                mm.then_inc(work_ready[place["z"][0]].sem, 1)
                taken(pe, it, "z")
                for name, col in (("q", AQ), ("k", AK)):
                    ps = free(pe, it, name)
                    nc.tensor.matmul(ps[:, 0:A * W], wts[:, col:col + 128], zT[:], start=True, stop=True
                                     ).then_inc(work_ready[place[name][0]].sem, 1)
                ps = free(pe, it, "v")
                for j in range(A):
                    for c in range(2):
                        n = 2 * j + c
                        mm = nc.tensor.matmul(ps[0:C, n * 128:n * 128 + 128], zT[:, j, c * C:c * C + C],
                                              wts[:, AV:AV + 128], start=True, stop=True)
                mm.then_inc(work_ready[place["v"][0]].sem, 1)
                taken(pe, it, "q")
                taken(pe, it, "k")
                for j in range(A):
                    for hd in range(HEADS):
                        u = j * HEADS + hd
                        if u >= 2:
                            upto(pe, mag_done, it, u - 1)
                        for c in range(2):
                            mm = nc.tensor.matmul(SC[u % 2][:, c * W:c * W + W], qm[:, hd, j, c * C:c * C + C],
                                                  kT[:, j, :], start=True, stop=True)
                        mm.then_inc(scores_ready.sem, 1)
                for j in range(A):
                    upto(pe, scaled, it, j + 1)
                    taken(pe, it, "v")
                    upto(pe, oT_taken, it, j)

                    def turn(hd):
                        u = j * HEADS + hd
                        if u >= 2:
                            upto(pe, wT_taken, it, u - 1)
                        for kc in range(2):
                            for c in range(2):
                                mm = nc.tensor.transpose(WT[u % 2][:, kc * W + c * C:kc * W + c * C + C],
                                                         wgt[:, c * HEADS + hd, kc * C:kc * C + C], ident[0:C, 0:C])
                        mm.then_inc(wT_ready.sem, 1)

                    def attend(hd):
                        u = j * HEADS + hd
                        g, half = hd % 4, hd // 4
                        upto(pe, wT_taken, it, u + 1)
                        for kc in range(2):
                            mm = nc.tensor.matmul(OT[32 * g:32 * g + 32, half * W:half * W + W],
                                                  v[:, j, kc, HD * hd:HD * hd + 32], wT[:, u % 2, kc, :],
                                                  start=(kc == 0), stop=(kc == 1))
                        mm.then_inc(av_done.sem, 1)

                    turn(0)
                    for hd in range(1, HEADS):
                        turn(hd)
                        attend(hd - 1)
                    attend(HEADS - 1)
                    upto(pe, oT_taken, it, j + 1)
                    upto(pe, added, it, j)
                    for c in range(2):
                        for half in range(2):
                            mm = nc.tensor.matmul(PR[:, c * 128:c * 128 + 128], oT[:, half, c * C:c * C + C],
                                                  wts[:, AO + 128 * half:AO + 128 * half + 128],
                                                  start=(half == 0), stop=(half == 1))
                    mm.then_inc(proj_ready.sem, 1)

        @block.scalar
        def _(act):
            act.wait_ge(loaded, 16)
            with steps(act) as it:
                ps = ready(act, it, "z")
                nc.scalar.copy(zT[:].rearrange("p a w -> p (a w)"), ps[:, 0:A * W]).then_inc(work_taken[place["z"][0]].sem, 1)
                ps = ready(act, it, "q")
                for hd in range(HEADS):
                    cp = nc.scalar.activation(qm[:, hd].rearrange("p a w -> p (a w)"), ps[:, 0:A * W], ACT.Identity,
                                              scale=wts[:, AMASK + hd:AMASK + hd + 1])
                cp.then_inc(work_taken[place["q"][0]].sem, 1)
                for j in range(A):
                    for hd in range(HEADS):
                        u = j * HEADS + hd
                        upto(act, scores_ready, it, u + 1)
                        for c in range(2):
                            seg = c * HEADS + hd
                            ab = nc.scalar.activation(mag[:, j, seg, :], SC[u % 2][:, c * W:c * W + W], ACT.Abs,
                                                      accum_out=total[:, j, seg:seg + 1])
                        ab.then_inc(mag_done.sem, 1)
                for j in range(A):
                    for hd in range(HEADS):
                        u = j * HEADS + hd
                        upto(act, wT_ready, it, u + 1)
                        if u >= 2:
                            upto(act, av_done, it, u - 1)
                        nc.scalar.copy(wT[:, u % 2].rearrange("p k w -> p (k w)"), WT[u % 2][:, 0:2 * W]).then_inc(wT_taken.sem, 1)
                    upto(act, av_done, it, HEADS * (j + 1))
                    if j >= 1:
                        upto(act, proj_ready, it, j)
                    nc.scalar.copy(oT[:].rearrange("p k w -> p (k w)"), OT[:, 0:2 * W]).then_inc(oT_taken.sem, 1)

        @block.vector
        def _(dve):
            nc.vector.memset(v[:], 0.0).then_inc(filled, 1)
            dve.wait_ge(filled, 2)
            with steps(dve) as it:
                for j in range(A):
                    for c in range(2):
                        nc.vector.bn_stats(stats[:, j, c, :], h[:, it * A + j, c, :]).then_inc(stats_done.sem, 1)
                upto(dve, stats_done, it, 2 * A)
                dve.sem_inc(spare, 1)
                for j in range(A):
                    for c in range(2):
                        agg = nc.vector.bn_aggr(mv[:, j, c, :], stats[:, j, c, :])
                agg.then_inc(mv_done.sem, 1)
                upto(dve, rstd_done, it, 1)
                for j in range(A):
                    for c in range(2):
                        zz = nc.vector.tensor_scalar(z[:, j, c, :], h[:, it * A + j, c, :], mv[:, j, c, 0:1],
                                                     rstd[:, j, c:c + 1], ALU.subtract, ALU.mult)
                zz.then_inc(z_done.sem, 1)
                ps = ready(dve, it, "k")
                nc.vector.tensor_copy(kT[:].rearrange("p a w -> p (a w)"), ps[:, 0:A * W]).then_inc(work_taken[place["k"][0]].sem, 1)
                ps = ready(dve, it, "v")
                nc.vector.tensor_copy(v[:, :, :, 0:DIM].rearrange("p a c d -> p (a c) d"),
                                      ps[0:C, :].rearrange("p (n d) -> p n d", d=DIM)).then_inc(work_taken[place["v"][0]].sem, 1)
                for j in range(A):
                    upto(dve, mag_done, it, HEADS * (j + 1))
                    if j >= 1:
                        upto(dve, coef_done, it, 7 * j)
                    src = mag[:, j]
                    lf = left[:, j % 2]
                    dve.sem_inc(spare, 1)
                    for r in range(3):
                        for s in range(SEG):
                            mx = nc.vector.max(top[:, s, 8 * r:8 * r + 8], src[:, s, :])
                        mx.then_inc(found.sem, 1)
                        upto(dve, found, it, 3 * j + r + 1)
                        if r == 2:
                            nc.vector.memset(top[:, :, TOPK:24], 0.0).then_inc(cleared.sem, 1)
                            upto(dve, cleared, it, 4 * j + 3)
                        dve.sem_inc(spare, 1)
                        for s in range(SEG):
                            mr = nc.vector.match_replace(lf[:, s, :], top[:, s, 8 * r:8 * r + 8], src[:, s, :], 0.0)
                        mr.then_inc(cleared.sem, 1)
                        upto(dve, cleared, it, 4 * j + r + 1 + (r == 2))
                        dve.sem_inc(spare, 1)
                        src = lf
                    steps_ = [
                        lambda: nc.vector.tensor_reduce(small[:, 0:1, :].rearrange("p o s -> p (o s)"), top[:, :, 0:TOPK], axis=AX.X, op=ALU.add),
                        lambda: nc.vector.tensor_scalar(small[:, 1, :], total[:, j, :], 1e-8, None, ALU.add),
                        lambda: nc.vector.reciprocal(small[:, 2, :], small[:, 1, :]),
                        lambda: nc.vector.tensor_tensor(small[:, 3, :], small[:, 0, :], small[:, 2, :], ALU.mult),
                        lambda: nc.vector.tensor_scalar(small[:, 4, :], small[:, 3, :], 1e-8, None, ALU.add),
                        lambda: nc.vector.reciprocal(small[:, 1, :], small[:, 4, :]),
                        lambda: nc.vector.tensor_tensor(small[:, 5, :], small[:, 1, :], small[:, 2, :], ALU.mult),
                    ]
                    if j >= 1:
                        upto(dve, scaled, it, j)
                    for n, step in enumerate(steps_):
                        step().then_inc(coef_done.sem, 1)
                        upto(dve, coef_done, it, 7 * j + n + 1)
                    if j >= 1:
                        upto(dve, wT_ready, it, HEADS * j)
                    nc.vector.tensor_tensor(wgt[:], mag[:, j], lf, ALU.subtract).then_inc(wgt_done.sem, 1)
                for j in range(A):
                    upto(dve, proj_ready, it, j + 1)
                    hp = h[:, bass.ds(it * A + j, 1), :, :].rearrange("p i c d -> p (i c d)")
                    nc.vector.tensor_tensor(hp, hp, PR[:, 0:2 * DIM], ALU.add).then_inc(added.sem, 1)

        @block.gpsimd
        def _(pool):
            nc.gpsimd.memset(neghalf[:], -0.5).then_inc(filled, 1)
            pool.wait_ge(filled, 2)
            with steps(pool) as it:
                upto(pool, mv_done, it, 1)
                pool.sem_inc(spare, 1)
                nc.gpsimd.tensor_scalar(rstd[:], mv[:, :, :, 1], EPS, None, ALU.add).then_inc(veps_done.sem, 1)
                upto(pool, veps_done, it, 1)
                nc.gpsimd.tensor_tensor(rstd[:], rstd[:], neghalf[:], ALU.pow).then_inc(rstd_done.sem, 1)
                for j in range(A):
                    upto(pool, wgt_done, it, j + 1)
                    nc.gpsimd.tensor_tensor(wgt[:], wgt[:], small[:, 5:6, :].rearrange("p o s -> p s o").to_broadcast([C, SEG, W]),
                                            ALU.mult).then_inc(scaled.sem, 1)


FK = 64
TK = 8
NP = 32
TG = 36
GROUPS = ((0, 32), (32, 64), (64, C))
UNIT = 16


def build_ffn(nc, B, ffnq_in, ffnk_in, ffnb_in, iota_in, wdown_in, wup_in, h, ident):
    BF16 = mybir.dt.bfloat16
    U32 = mybir.dt.uint32
    R = SEG * TK
    units = []
    for g, (t0, t1) in enumerate(GROUPS):
        for t in range(t0, t1, UNIT):
            units.append((g, t, min(t + UNIT, t1)))
    per_group = [sum(1 for u in units if u[0] == g) for g in range(len(GROUPS))]
    with ExitStack() as ctx:
        sb = lambda name, shape, dt=F32: ctx.enter_context(nc.sbuf_tensor(name, shape, dt))
        sem = lambda name: ctx.enter_context(nc.semaphore(name))
        bank = lambda name: ctx.enter_context(nc.psum_tensor(name, [128, 512], F32))
        wd = sb("f_wd", [DIM, NP, 128])
        wu = sb("f_wu", [128, NP, DIM])
        wc = sb("f_wc", [128, 2 * HEADS * FK])
        bc = sb("f_bc", [C, 2 * HEADS * FK])
        iota = sb("f_iota", [128, 128, TG], BF16)
        stats = sb("f_stats", [C, 2, 6])
        mv = sb("f_mv", [C, 2, 2])
        rstd = sb("f_rstd", [C, 2])
        neghalf = sb("f_neghalf", [C, 2])
        z = sb("f_z", [C, 2, DIM])
        zT = sb("f_zT", [128, W])
        sc = sb("f_sc", [C, 2, HEADS, 2, FK])
        top = sb("f_top", [C, SEG, 2, TK])
        topi = sb("f_topi", [C, SEG, 2, TK], U32)
        topf = sb("f_topf", [C, SEG, 2, TK])
        pairs = sb("f_pairs", [C, SEG, TK, TK])
        best = sb("f_best", [C, SEG, TK])
        besti = sb("f_besti", [C, SEG, TK], U32)
        rank = sb("f_rank", [C, 2, SEG, TK], U32)
        rankf = sb("f_rankf", [C, 2, SEG, TK])
        pick = sc[:].rearrange("p c h s k -> p (c h s k)").rearrange("p (d s k a) -> p d s k a", d=2, s=SEG, k=TK)
        got = sb("f_got", [C, 2, SEG, TK])
        goti = sb("f_goti", [C, 3, R], U32)
        gotf = sb("f_gotf", [C, 2, R])
        cols = sb("f_cols", [C, 3, R])
        ex = sb("f_ex", [C, 3, SEG, TK])
        esum = sb("f_esum", [C, 2, SEG])
        idx = sb("f_idx", [128, 2, GROUPS[-1][0] + TG], BF16)
        part = sb("f_part", [128, 3, GROUPS[-1][0] + TG], BF16)
        rest = sb("f_rest", [128, 2, GROUPS[-1][0] + TG])
        hotc = sb("f_hotc", [128, NP, TG], BF16)
        outT = sb("f_outT", [128, W])
        WK = [bank(f"f_WK{i}") for i in range(2)]
        IN = [bank(f"f_IN{i}") for i in range(2)]
        AA = [bank(f"f_AA{i}") for i in range(2)]
        OT = bank("f_OT")
        BK = OT[:, 256:512]
        SLOTS = (AA, IN)
        uses = ["z", "s0", "s1", "s2", "s3", "idx"]
        place = {u: (n % 2, n // 2) for n, u in enumerate(uses)}
        work_ready = [Count(sem(f"f_work_ready{b}"), 3) for b in range(2)]
        work_taken = [Count(sem(f"f_work_taken{b}"), 3) for b in range(2)]
        loaded, big_loaded, spare, filled = sem("f_loaded"), sem("f_big_loaded"), sem("f_spare"), sem("f_filled")
        comp_ready, comp_taken = sem("f_comp_ready"), sem("f_comp_taken")
        dve_step = Count(sem("f_dve_step"), 17)
        stats_done = Count(sem("f_stats_done"), 2)
        mv_done = Count(sem("f_mv_done"), 1)
        veps_done = Count(sem("f_veps_done"), 1)
        rstd_done = Count(sem("f_rstd_done"), 1)
        z_done = Count(sem("f_z_done"), 1)
        diff_done = Count(sem("f_diff_done"), 1)
        exp_done = Count(sem("f_exp_done"), 1)
        cols_done = Count(sem("f_cols_done"), 1)
        inner_ready = Count(sem("f_inner_ready"), 16)
        inner_taken = Count(sem("f_inner_taken"), 16)
        hot_done = Count(sem("f_hot_done"), len(GROUPS))
        hotc_done = Count(sem("f_hotc_done"), len(GROUPS))
        hotp_done = Count(sem("f_hotp_done"), 3 * len(GROUPS))
        aa_ready = [Count(sem(f"f_aa_ready{i}"), len(units[i::2])) for i in range(2)]
        aa_taken = [Count(sem(f"f_aa_taken{i}"), len(units[i::2])) for i in range(2)]
        out_ready = Count(sem("f_out_ready"), 1)
        out_taken = Count(sem("f_out_taken"), 1)
        back_ready = Count(sem("f_back_ready"), 1)
        added = Count(sem("f_added"), 1)
        start(nc)

        def upto(eng, count, it, k):
            eng.wait_ge(count.sem, count.after(it, k))

        def ready(eng, it, use):
            b, n = place[use]
            upto(eng, work_ready[b], it, n + 1)
            return WK[b]

        def taken(eng, it, use):
            b, n = place[use]
            upto(eng, work_taken[b], it, n + 1)

        def free(eng, it, use):
            b, n = place[use]
            upto(eng, work_taken[b], it, n)
            return WK[b]

        with ExitStack() as c2:
            qt = c2.enter_context(nc.sbuf_tensor("f_qt", [FK, 2 * HEADS, DIM], F32))
            kt = c2.enter_context(nc.sbuf_tensor("f_kt", [FK, 2 * HEADS, FK], F32))
            bt = c2.enter_context(nc.sbuf_tensor("f_bt", [FK, 2 * HEADS, C], F32))
            numbers = c2.enter_context(nc.sbuf_tensor("f_numbers", [128, 128], F32))
            block = c2.enter_context(nc.Block())

            @block.sync
            def _(sp):
                sp.dma_start(qt[:], ffnq_in).then_inc(loaded, 16)
                sp.dma_start(kt[:], ffnk_in).then_inc(loaded, 16)
                sp.dma_start(bt[:], ffnb_in).then_inc(loaded, 16)
                sp.dma_start(numbers[:], iota_in).then_inc(big_loaded, 16)
                sp.dma_start(wd[:], wdown_in).then_inc(big_loaded, 16)
                sp.dma_start(wu[:], wup_in).then_inc(big_loaded, 16)

            @block.tensor
            def _(pe):
                pe.wait_ge(loaded, 48)
                for n in range(2):
                    for s in range(8):
                        mm = nc.tensor.matmul(IN[n][:, s * FK:s * FK + FK], qt[:, 8 * n + s, :], kt[:, 8 * n + s, :],
                                              start=True, stop=True)
                    mm.then_inc(comp_ready, 1)
                for n in range(2):
                    for s in range(8):
                        mm = nc.tensor.matmul(AA[n][0:C, s * FK:s * FK + FK], bt[:, 8 * n + s, :], kt[:, 8 * n + s, :],
                                              start=True, stop=True)
                    mm.then_inc(comp_ready, 1)

            @block.vector
            def _(dve):
                for n in range(4):
                    dve.wait_ge(comp_ready, n + 1)
                    src = (IN + AA)[n]
                    dst = (wc, bc)[n // 2]
                    rows = (128, C)[n // 2]
                    nc.vector.tensor_copy(dst[:, (n % 2) * 512:(n % 2) * 512 + 512], src[0:rows, :]).then_inc(comp_taken, 1)
                dve.wait_ge(big_loaded, 48)
                nc.vector.tensor_copy(iota[:], numbers[:].rearrange("p (i o) -> p i o", o=1).to_broadcast([128, 128, TG]))
                nc.vector.memset(idx[:], 0.0).then_inc(filled, 1)
                nc.vector.memset(part[:], 0.0).then_inc(filled, 1)
                dve.wait_ge(comp_taken, 4)

        hot = sb("f_hot", [128, 2, 128, TG], BF16)
        act_in = sb("f_act", [128, NP, W])
        hotp = sb("f_hotp", [128, 2, 3, NP, TG], BF16)
        block = ctx.enter_context(nc.Block())

        @block.tensor
        def _(pe):
            pe.wait_ge(big_loaded, 48)
            with pe.Fori(0, B) as it:
                ps = free(pe, it, "z")
                upto(pe, z_done, it, 1)
                for c in range(2):
                    mm = nc.tensor.transpose(ps[:, c * C:c * C + C], z[:, c, :], ident[0:C, 0:C])
                mm.then_inc(work_ready[place["z"][0]].sem, 1)
                taken(pe, it, "z")
                for n in range(4):
                    ps = free(pe, it, f"s{n}")
                    c, f = n // 2, n % 2
                    nc.tensor.matmul(ps[0:C, :], zT[:, c * C:c * C + C], wc[:, 512 * f:512 * f + 512],
                                     start=True, stop=True).then_inc(work_ready[place[f"s{n}"][0]].sem, 1)
                for n in range(NP // 2):
                    if n >= 2:
                        upto(pe, inner_taken, it, n - 1)
                    for m in range(2):
                        mm = nc.tensor.matmul(IN[n % 2][:, m * W:m * W + W], wd[:, 2 * n + m, :], zT[:],
                                              start=True, stop=True)
                    mm.then_inc(inner_ready.sem, 1)
                ps = free(pe, it, "idx")
                upto(pe, cols_done, it, 1)
                for n in range(3):
                    mm = nc.tensor.transpose(ps[:, n * C:n * C + C], cols[:, n, :], ident[0:C, 0:C])
                mm.then_inc(work_ready[place["idx"][0]].sem, 1)
                for u, (g, t0, t1) in enumerate(units):
                    if u == sum(per_group[:g]):
                        upto(pe, hotp_done, it, 3 * g + 3)
                    upto(pe, aa_taken[u % 2], it, u // 2)
                    if u == 1:
                        upto(pe, inner_taken, it, 16)
                    for t in range(t0, t1):
                        for c in range(2):
                            col = (t - t0) * NP
                            tt = t - GROUPS[g][0]
                            for pt in range(3):
                                mm = nc.tensor.matmul(SLOTS[u % 2][c][:, col:col + NP], hot[64 * c:64 * c + 64, g % 2, :, tt],
                                                      hotp[64 * c:64 * c + 64, g % 2, pt, :, tt],
                                                      start=(pt == 0), stop=(pt == 2))
                    mm.then_inc(aa_ready[u % 2].sem, 1)
                upto(pe, out_taken, it, 0)
                for i in range(2):
                    upto(pe, aa_taken[i], it, aa_taken[i].per)
                for n in range(NP):
                    mm = nc.tensor.matmul(OT[:, 0:W], wu[:, n, :], act_in[:, n, :], start=(n == 0), stop=(n == NP - 1))
                mm.then_inc(out_ready.sem, 1)
                upto(pe, out_taken, it, 1)
                upto(pe, added, it, 0)
                for c in range(2):
                    mm = nc.tensor.transpose(BK[0:C, c * 128:c * 128 + 128], outT[:, c * C:c * C + C], ident[:])
                mm.then_inc(back_ready.sem, 1)

        @block.scalar
        def _(act):
            with act.Fori(0, B) as it:
                ps = ready(act, it, "z")
                nc.scalar.copy(zT[:], ps[:, 0:W]).then_inc(work_taken[place["z"][0]].sem, 1)
                for n in range(NP // 2):
                    upto(act, inner_ready, it, n + 1)
                    if n == 0:
                        upto(act, out_ready, it, 0)
                    nc.scalar.activation(act_in[:, 2 * n:2 * n + 2, :].rearrange("p n w -> p (n w)"), IN[n % 2][:, 0:2 * W],
                                         ACT.Relu).then_inc(inner_taken.sem, 1)
                upto(act, diff_done, it, 1)
                nc.scalar.activation(ex[:, 1], ex[:, 0], ACT.Exp).then_inc(exp_done.sem, 1)
                upto(act, out_ready, it, 1)
                nc.scalar.copy(outT[:], OT[:, 0:W]).then_inc(out_taken.sem, 1)

        @block.vector
        def _(dve):
            V = nc.vector
            dve.wait_ge(filled, 2)
            dve.wait_ge(big_loaded, 48)
            with dve.Fori(0, B) as it:
                n_step = [0]

                def then(ins):
                    n_step[0] += 1
                    ins.then_inc(dve_step.sem, 1)
                    upto(dve, dve_step, it, n_step[0])
                    dve.sem_inc(spare, 1)

                for c in range(2):
                    V.bn_stats(stats[:, c, :], h[:, it, c, :]).then_inc(stats_done.sem, 1)
                upto(dve, stats_done, it, 2)
                dve.sem_inc(spare, 1)
                for c in range(2):
                    agg = V.bn_aggr(mv[:, c, :], stats[:, c, :])
                agg.then_inc(mv_done.sem, 1)
                upto(dve, rstd_done, it, 1)
                for c in range(2):
                    zz = V.tensor_scalar(z[:, c, :], h[:, it, c, :], mv[:, c, 0:1], rstd[:, c:c + 1], ALU.subtract, ALU.mult)
                zz.then_inc(z_done.sem, 1)
                for n in range(4):
                    c, f = n // 2, n % 2
                    ps = ready(dve, it, f"s{n}")
                    V.tensor_tensor(sc[:, c, 4 * f:4 * f + 4].rearrange("p h s k -> p (h s k)"), ps[0:C, :],
                                    bc[:, 512 * f:512 * f + 512], ALU.add).then_inc(work_taken[place[f"s{n}"][0]].sem, 1)
                taken(dve, it, "s2")
                taken(dve, it, "s3")
                dve.sem_inc(spare, 1)
                segs = [(c, hd, side) for c in range(2) for hd in range(HEADS) for side in range(2)]
                for c, hd, side in segs:
                    last = V.max(top[:, c * HEADS + hd, side, :], sc[:, c, hd, side, :])
                then(last)
                for c, hd, side in segs:
                    last = V.max_index(topi[:, c * HEADS + hd, side, :], top[:, c * HEADS + hd, side, :], sc[:, c, hd, side, :])
                then(last)
                V.tensor_copy(topf[:], topi[:])
                then(V.tensor_tensor(pairs[:],
                                     top[:, :, 0, :].rearrange("p s (a o) -> p s a o", o=1).to_broadcast([C, SEG, TK, TK]),
                                     top[:, :, 1:2, :].to_broadcast([C, SEG, TK, TK]), ALU.add))
                for s in range(SEG):
                    last = V.max(best[:, s, :], pairs[:, s].rearrange("p a b -> p (a b)"))
                then(last)
                for s in range(SEG):
                    V.max_index(besti[:, s, :], best[:, s, :], pairs[:, s].rearrange("p a b -> p (a b)"))
                V.tensor_tensor(ex[:, 0], best[:], best[:, :, 0:1].to_broadcast([C, SEG, TK]), ALU.subtract).then_inc(diff_done.sem, 1)
                upto(dve, diff_done, it, 1)
                V.tensor_scalar(rank[:, 0], besti[:], 3, None, ALU.logical_shift_right)
                then(V.tensor_scalar(rank[:, 1], besti[:], 7, None, ALU.bitwise_and))
                then(V.tensor_copy(rankf[:], rank[:]))
                for side in range(2):
                    for a in range(TK):
                        last = V.scalar_tensor_tensor(pick[:, side, :, :, a], rankf[:, side], float(a),
                                                      topf[:, :, side, a:a + 1].to_broadcast([C, SEG, TK]),
                                                      ALU.is_equal, ALU.mult)
                then(last)
                then(V.tensor_reduce(got[:].rearrange("p d s k -> p (d s k)"), pick.rearrange("p d s k a -> p (d s k) a"),
                                     axis=AX.X, op=ALU.add))
                then(V.tensor_copy(goti[:, 0, :], got[:, 1].rearrange("p s k -> p (s k)")))
                V.tensor_scalar(goti[:, 1, :], goti[:, 0, :], 1, None, ALU.logical_shift_right)
                then(V.tensor_scalar(goti[:, 2, :], goti[:, 0, :], 1, None, ALU.bitwise_and))
                V.tensor_copy(cols[:, 1, :], goti[:, 1, :])
                then(V.tensor_copy(gotf[:, 0, :], goti[:, 2, :]))
                V.scalar_tensor_tensor(cols[:, 0, :], gotf[:, 0, :], float(FK), got[:, 0].rearrange("p s k -> p (s k)"),
                                       ALU.mult, ALU.add)
                upto(dve, exp_done, it, 1)
                then(V.tensor_reduce(esum[:, 0, :], ex[:, 1], axis=AX.X, op=ALU.add))
                then(V.reciprocal(esum[:, 1, :], esum[:, 0, :]))
                V.tensor_tensor(cols[:, 2, :].rearrange("p (s k) -> p s k", k=TK), ex[:, 1],
                                esum[:, 1, :].rearrange("p (s o) -> p s o", o=1).to_broadcast([C, SEG, TK]),
                                ALU.mult).then_inc(cols_done.sem, 1)
                ps = ready(dve, it, "idx")
                V.tensor_copy(idx[:, :, 0:C], ps[:, 0:2 * C].rearrange("p (n t) -> p n t", n=2))
                wt = ps[:, 2 * C:3 * C]
                then(V.tensor_copy(part[:, 0, 0:C], wt))
                then(V.tensor_tensor(rest[:, 0, 0:C], wt, part[:, 0, 0:C], ALU.subtract))
                then(V.tensor_copy(part[:, 1, 0:C], rest[:, 0, 0:C]))
                then(V.tensor_tensor(rest[:, 1, 0:C], rest[:, 0, 0:C], part[:, 1, 0:C], ALU.subtract))
                V.tensor_copy(part[:, 2, 0:C], rest[:, 1, 0:C]).then_inc(work_taken[place["idx"][0]].sem, 1)
                taken(dve, it, "idx")
                def one_hots(g):
                    t0 = GROUPS[g][0]
                    if g >= 2:
                        done = sum(per_group[:g - 1]) - 1
                        upto(dve, aa_ready[done % 2], it, done // 2 + 1)
                    V.tensor_tensor(hot[:, g % 2], idx[:, 0:1, t0:t0 + TG].to_broadcast([128, 128, TG]), iota[:],
                                    ALU.is_equal).then_inc(hot_done.sem, 1)
                    V.tensor_tensor(hotc[:], idx[:, 1:2, t0:t0 + TG].to_broadcast([128, NP, TG]), iota[:, 0:NP, :],
                                    ALU.is_equal).then_inc(hotc_done.sem, 1)
                    upto(dve, hotc_done, it, g + 1)
                    for pt in range(3):
                        V.tensor_tensor(hotp[:, g % 2, pt], hotc[:], part[:, pt:pt + 1, t0:t0 + TG].to_broadcast([128, NP, TG]),
                                        ALU.mult).then_inc(hotp_done.sem, 1)
                    upto(dve, hotp_done, it, 3 * g + 3)

                def weigh(g):
                    if g == 0:
                        upto(dve, inner_taken, it, 16)
                    for u, (gu, t0, t1) in enumerate(units):
                        if gu != g:
                            continue
                        upto(dve, aa_ready[u % 2], it, u // 2 + 1)
                        for c in range(2):
                            sl = act_in[:, :, c * C + t0:c * C + t1]
                            last = V.tensor_tensor(sl, sl, SLOTS[u % 2][c][:, 0:(t1 - t0) * NP].rearrange("p (t n) -> p n t", n=NP),
                                                   ALU.mult)
                        last.then_inc(aa_taken[u % 2].sem, 1)

                one_hots(0)
                for g in range(1, len(GROUPS)):
                    one_hots(g)
                    weigh(g - 1)
                weigh(len(GROUPS) - 1)
                upto(dve, back_ready, it, 1)
                hp = h[:, bass.ds(it, 1), :, :].rearrange("p i c d -> p (i c d)")
                V.tensor_tensor(hp, hp, BK[0:C, 0:2 * DIM], ALU.add).then_inc(added.sem, 1)
                upto(dve, added, it, 1)
                dve.sem_inc(spare, 1)
                dve_step.used = n_step[0]
            assert dve_step.used == dve_step.per

        @block.gpsimd
        def _(pool):
            nc.gpsimd.memset(neghalf[:], -0.5).then_inc(filled, 1)
            pool.wait_ge(filled, 3)
            with pool.Fori(0, B) as it:
                upto(pool, mv_done, it, 1)
                pool.sem_inc(spare, 1)
                nc.gpsimd.tensor_scalar(rstd[:], mv[:, :, 1], EPS, None, ALU.add).then_inc(veps_done.sem, 1)
                upto(pool, veps_done, it, 1)
                nc.gpsimd.tensor_tensor(rstd[:], rstd[:], neghalf[:], ALU.pow).then_inc(rstd_done.sem, 1)


def build(nc, B, DEPTH, x_in, base_in, convw_in, layer_in, ident_in, normw_in, cls_in, attw_in, ffnq_in, ffnk_in, ffnb_in, iota_in, wdown_in, wup_in, out, stage=9):
    with ExitStack() as ctx:
        h = ctx.enter_context(nc.sbuf_tensor("h", [C, B, 2, DIM], F32))
        ident = ctx.enter_context(nc.sbuf_tensor("ident", [128, 128], F32))
        ident_loaded = ctx.enter_context(nc.semaphore("ident_loaded"))
        with nc.Block() as block:
            @block.sync
            def _(sp):
                sp.dma_start(ident[:], ident_in).then_inc(ident_loaded, 16)
                sp.wait_ge(ident_loaded, 16)
        with ExitStack() as c2:
            build_tower(nc, c2, B, DEPTH, x_in, base_in, convw_in, layer_in, h, ident)
        if stage >= 2:
            build_norm(nc, B, normw_in, cls_in, h)
            build_attention(nc, B, attw_in, h, ident)
        if stage >= 3:
            build_ffn(nc, B, ffnq_in, ffnk_in, ffnb_in, iota_in, wdown_in, wup_in, h, ident)
        with ExitStack() as c2:
            stored = c2.enter_context(nc.semaphore("stored"))
            block = c2.enter_context(nc.Block())

            @block.sync
            def _(sp):
                first = 2 + C
                sp.dma_start(out[:, 2:first].rearrange("b p d -> p b d"), h[:, :, 0, :]).then_inc(stored, 16)
                sp.dma_start(out[:, first:W].rearrange("b p d -> p b d"), h[0:W - first, :, 1, :]).then_inc(stored, 16)
                for slot, row in ((C - 2, 1), (C - 1, 0)):
                    sp.dma_start(out[:, row:row + 1].rearrange("b p d -> p b d"), h[slot:slot + 1, :, 1, :]).then_inc(stored, 16)
                sp.wait_ge(stored, 64)


def lay_out(inputs, B):
    import numpy as np
    f = np.float32
    x = np.asarray(inputs["x"])[:B]
    x = x.reshape(B, 3, 14, 16, 14, 16).transpose(0, 1, 3, 5, 2, 4).reshape(B, KC, 128, PATCHES)
    x = np.ascontiguousarray(x.transpose(0, 2, 1, 3))
    cw = np.asarray(inputs["L0_tok_conv_w"]).reshape(KC, 128, DIM).transpose(1, 0, 2)
    pos = np.asarray(inputs["L0_tok_pos_embed"])[0]
    base = np.zeros((2, W, DIM), f)
    base[0, :PATCHES] = pos[1:]
    base[0, PATCHES] = pos[0]
    base[1, :PATCHES] = np.asarray(inputs["L0_tok_conv_b"])
    base[1, PATCHES] = np.asarray(inputs["L0_tok_cls_token"])[0, 0]
    base = base.reshape(2, 2, C, DIM).transpose(2, 0, 1, 3)
    g = lambda n: np.asarray(inputs["L0_tok_" + n])
    L = g("qkv_w").shape[0]
    wt = np.zeros((L, 128, NW), f)
    rows = np.arange(4)[:, None] * 32 + np.arange(HD)[None, :]
    for half in range(2):
        cols = rows.reshape(-1)
        for w0, bcol, part in ((QW, QB, 0), (KW, KB, 1)):
            src = part * DIM + half * 64
            wt[:, :, w0 + half * 128 + cols] = g("qkv_w")[:, :, src:src + 64]
            wt[:, cols, bcol + half] = g("qkv_b")[:, src:src + 64]
        wt[:, np.arange(4) * 32 + HD, KB + half] = 1.0
    wt[:, :, VW:VW + 128] = g("qkv_w")[:, :, 256:]
    wt[:, :, PW:PW + 128] = g("proj_w")
    wt[:, :, F1W:F1W + 256] = g("fc1_w")
    wt[:, :, F2W:F2W + 256] = g("fc2_w").reshape(L, 2, 128, DIM).transpose(0, 2, 1, 3).reshape(L, 128, 256)
    wt[:, :, VB:VB + 128] = g("qkv_b")[:, None, 256:]
    wt[:, :, PB:PB + 128] = g("proj_b")[:, None]
    wt[:, :, F2B:F2B + 128] = g("fc2_b")[:, None]
    for col, n in ((LN1W, "ln1_w"), (LN1B, "ln1_b"), (LN2W, "ln2_w"), (LN2B, "ln2_b")):
        wt[:, :, col] = g(n)
    wt[:, :, F1B:F1B + 2] = g("fc1_b").reshape(L, 2, 128).transpose(0, 2, 1)
    nw = np.stack([g("norm_w"), g("norm_b")])
    normw = np.ascontiguousarray(np.broadcast_to(nw, (C, 2, DIM)))
    cls = np.ascontiguousarray(np.broadcast_to(np.asarray(inputs["cls_tok"])[0], (B, DIM)))[None]
    a = lambda n: np.asarray(inputs["L0_attn_" + n])
    at = np.zeros((128, ANW), f)
    at[:, AQ:AQ + 128], at[:, AK:AK + 128], at[:, AV:AV + 128] = a("Wq").T, a("Wk").T, a("Wv").T
    for hd in range(HEADS):
        gr, half = hd % 4, hd // 4
        at[32 * gr:32 * gr + HD, AO + 128 * half:AO + 128 * half + 128] = a("Wo").T[HD * hd:HD * hd + HD]
        at[HD * hd:HD * hd + HD, AMASK + hd] = 2.0
    q = lambda n: np.asarray(inputs["L0_ffn_" + n])
    SH = 2 * HEADS
    fq = np.ascontiguousarray(q("Wq").reshape(DIM, SH, FK).transpose(2, 1, 0))
    fk = np.ascontiguousarray(q("keys").reshape(SH, FK, FK).transpose(2, 0, 1))
    fb = np.ascontiguousarray(np.broadcast_to(q("bq").reshape(SH, FK).T[:, :, None], (FK, SH, C)))
    iota = np.ascontiguousarray(np.broadcast_to(np.arange(128, dtype=f), (128, 128)))
    wd = q("w_down").reshape(FK, NP, 2, DIM).transpose(3, 1, 2, 0).reshape(DIM, NP, 128)
    wu = q("w_up").reshape(FK, NP, 2, DIM).transpose(2, 0, 1, 3).reshape(128, NP, DIM)
    return {"ffnq_in": fq, "ffnk_in": fk, "ffnb_in": fb, "iota_in": iota, "wdown_in": np.ascontiguousarray(wd),
            "wup_in": np.ascontiguousarray(wu), "normw_in": normw, "cls_in": cls, "attw_in": at, "x_in": x, "base_in": np.ascontiguousarray(base), "convw_in": np.ascontiguousarray(cw),
            "layer_in": wt, "ident_in": np.eye(128, dtype=f)}


def kernel(**inputs):
    import concourse.bacc as bacc
    from concourse.bass_utils import run_bass_kernel_spmd

    B = inputs["x"].shape[0]
    arrays = lay_out(inputs, B)
    nc = bacc.Bacc("TRN2", target_bir_lowering=False, num_devices=1)
    aps = {name: nc.dram_tensor(name, a.shape, mybir.dt.from_np(a.dtype), kind="ExternalInput").ap()
           for name, a in arrays.items()}
    out = nc.dram_tensor("out", (B, W, DIM), F32, kind="ExternalOutput").ap()
    build(nc, B, inputs["L0_tok_qkv_w"].shape[0], out=out, **aps)
    return run_bass_kernel_spmd(nc, [arrays], core_ids=[0]).results[0]["out"]
```

```python
from contextlib import ExitStack

import concourse.bass as bass
from concourse import mybir

ALU = mybir.AluOpType
ACT = mybir.ActivationFunctionType
AX = mybir.AxisListType
F32 = mybir.dt.float32

DIM = 128
HEADS = 8
HD = DIM // HEADS
HID = 256
PATCHES = 196
TOK = PATCHES + 1
C = 99
W = 2 * C
KC = 3 * 16 * 16 // 128
G = 4
EPS = 1e-5
PARTS = 3
QPARTS, KPARTS = (0, 0, 0, 1, 1, 2), (0, 1, 2, 0, 1, 0)
STACK = len(QPARTS) * HD
QW, KW, VW, PW, F1W, F2W = 0, 128, 256, 384, 640, 896
VB, PB, F2B = 1152, 1280, 1408
LN1W, LN1B, LN2W, LN2B, QB, KB, F1B = 1536, 1537, 1538, 1539, 1540, 1541, 1542
NW = 1544


class Count:

    made = []

    def __init__(self, sem, per):
        self.sem, self.per = sem, per
        Count.made.append(self)

    def after(self, it, k):
        return it * self.per + (k + 1)


def start(nc):
    with nc.Block() as block:
        @block.gpsimd
        def _(pool):
            for count in Count.made:
                pool.sem_inc(count.sem, 1)
    Count.made.clear()


def build_tower(nc, ctx, B, DEPTH, x_in, base_in, convw_in, layer_in, h, ident):
    NG = B // G
    sb = lambda name, shape: ctx.enter_context(nc.sbuf_tensor(name, shape, F32))
    sem = lambda name: ctx.enter_context(nc.semaphore(name))

    XB = 3
    with ExitStack() as c2:
        xbuf = c2.enter_context(nc.sbuf_tensor("xbuf", [128, XB, KC, W], F32))
        convw = c2.enter_context(nc.sbuf_tensor("convw", [128, KC, DIM], F32))
        base = c2.enter_context(nc.sbuf_tensor("base", [C, 2, 2, DIM], F32))
        emb = [c2.enter_context(nc.psum_tensor(f"emb{i}", [C, 2, DIM], F32)) for i in range(2)]
        x_loaded = [sem(f"x_loaded{i}") for i in range(XB)]
        consts_loaded, x_pad, emb_done, emb_taken, base_done = (
            sem(n) for n in ("consts_loaded", "x_pad", "emb_done", "emb_taken", "base_done"))
        block = c2.enter_context(nc.Block())

        @block.sync
        def _(sp):
            sp.wait_ge(x_pad, 1)
            sp.dma_start(convw[:], convw_in).then_inc(consts_loaded, 16)
            sp.dma_start(base[:], base_in).then_inc(consts_loaded, 16)
            for i in range(B):
                if i >= XB:
                    sp.wait_ge(emb_done, i - XB + 1)
                sp.dma_start(xbuf[:, i % XB, :, 0:PATCHES], x_in[i]).then_inc(x_loaded[i % XB], 16)

        @block.tensor
        def _(pe):
            pe.wait_ge(consts_loaded, 32)
            for i in range(B):
                pe.wait_ge(x_loaded[i % XB], 16 * (i // XB + 1))
                if i >= 2:
                    pe.wait_ge(emb_taken, i - 1)
                for c in range(2):
                    for k in range(KC):
                        mm = nc.tensor.matmul(emb[i % 2][:, c, :], xbuf[:, i % XB, k, c * C:c * C + C],
                                              convw[:, k, :], start=(k == 0), stop=(k == KC - 1))
                mm.then_inc(emb_done, 1)

        @block.vector
        def _(dve):
            nc.vector.memset(xbuf[:, :, :, PATCHES:W], 0.0).then_inc(x_pad, 1)
            dve.wait_ge(consts_loaded, 32)
            nc.vector.tensor_tensor(base[:, 0], base[:, 0], base[:, 1], ALU.add).then_inc(base_done, 1)
            dve.wait_ge(base_done, 1)
            for i in range(B):
                dve.wait_ge(emb_done, i + 1)
                nc.vector.tensor_tensor(h[:, i], emb[i % 2][:], base[:, 0], ALU.add).then_inc(emb_taken, 1)

    BF16 = mybir.dt.bfloat16
    with ExitStack() as c2:
        sb = lambda name, shape, dt=F32: c2.enter_context(nc.sbuf_tensor(name, shape, dt))
        wts = sb("wts", [128, NW])
        identb = sb("identb", [128, 128], BF16)
        stats = sb("stats", [C, G, 2, 6])
        mv = sb("mv", [C, G, 2, 2])
        rstd = sb("rstd", [C, G, 2])
        neghalf = sb("neghalf", [C, G, 2])
        z = sb("z", [C, G, 2, DIM])
        yT = sb("yT", [128, G, W])
        parts = sb("parts", [128, 2, PARTS, G, W], BF16)
        rest = sb("rest", [128, 2, 2, W])
        qs = sb("qs", [STACK + PARTS, HEADS, G, W], BF16)
        ks = sb("ks", [STACK + PARTS, HEADS, G, W], BF16)
        vaug = sb("vaug", [C, G, 2, HEADS, 32])
        negmax = sb("negmax", [C, G, 2, HEADS])
        mrest = sb("mrest", [C, 2, 2, HEADS])
        mparts = sb("mparts", [C, G, 2, PARTS, HEADS], BF16)
        mrows = sb("mrows", [PARTS * HEADS, G, W], BF16)
        probs = sb("probs", [C, 4, 2, 2, W])
        oraw = sb("oraw", [128, 2, 2, W])
        rsum = sb("rsum", [C, 2, 2, 4])
        o = sb("o", [C, G, 2, DIM])
        oT = sb("oT", [128, G, W])
        gT = sb("gT", [128, G // 2, 2, 2, W])
        PAIR = [c2.enter_context(nc.psum_tensor(f"PAIR{i}", [C, 2, 512], F32)) for i in range(3)]
        WK = [c2.enter_context(nc.psum_tensor(f"WK{i}", [128, 512], F32)) for i in range(2)]

        LAG = 2
        plan = []
        for a in range(G // 2):
            plan += [("ln1", a), ("q", a), ("k", a), ("v", a)]
        for j in range(G + LAG + 1):
            i = j - LAG
            for p in range(4):
                if j < G:
                    plan.append(("S", j, p))
                if 0 <= i < G:
                    plan.append(("ST", i, p))
                if p == 0 and 0 <= i - 1:
                    plan.append(("av", i - 1, 1))
                if p == 1 and 1 <= j <= G:
                    plan.append(("max", j - 1))
                if p == 2 and 0 <= i < G:
                    plan.append(("av", i, 0))
                if p == 3 and 0 <= i - 1:
                    plan.append(("turn", i - 1))
        for a in range(G // 2):
            plan += [("oT", a), ("proj", a)]
        for a in range(G // 2):
            plan += [("ln2", a), ("f1", a, 0), ("f1", a, 1)]
        plan += [("f2", a) for a in range(G // 2)]
        paired = [u for u in plan if u[0] in ("S", "ST")]
        seat = {u: (n % 3, n // 3) for n, u in enumerate(paired)}
        uses = [u for u in plan if u[0] not in ("S", "ST") and not (u[0] == "av" and u[2] == 1)]
        assert len(uses) % 2 == 0
        place = {u: (n % 2, n // 2) for n, u in enumerate(uses)}

        work_ready = [Count(sem(f"work_ready{b}"), len(uses) // 2) for b in range(2)]
        work_taken = [Count(sem(f"work_taken{b}"), len(uses) // 2) for b in range(2)]
        wts_loaded = sem("wts_loaded")
        filled = sem("filled")
        spare = sem("spare")
        stats_done = Count(sem("stats_done"), 2 * 2 * G)
        mv_done = Count(sem("mv_done"), 2)
        veps_done = Count(sem("veps_done"), 2)
        rstd_done = Count(sem("rstd_done"), 2)
        z_done = Count(sem("z_done"), 2 * G)
        bias_added = Count(sem("bias_added"), 2)
        high_done = Count(sem("high_done"), G)
        rest_done = Count(sem("rest_done"), G)
        mid_done = Count(sem("mid_done"), G)
        low_done = Count(sem("low_done"), G)
        stacked = [Count(sem(f"stacked{a}"), 16 * 2 * len(QPARTS)) for a in range(G // 2)]
        pair_ready = [Count(sem(f"pair_ready{b}"), len(paired[b::3])) for b in range(3)]
        pair_taken = [Count(sem(f"pair_taken{b}"), len(paired[b::3])) for b in range(3)]
        msplit = Count(sem("msplit"), G * 5)
        max_stacked = [Count(sem(f"max_stacked{j}"), 16) for j in range(G)]
        av_half = Count(sem("av_half"), G)
        rsum_done = Count(sem("rsum_done"), G)
        start(nc)
        block = c2.enter_context(nc.Block())

        def steps(eng):
            with eng.Fori(0, DEPTH) as layer:
                eng.wait_ge(wts_loaded, layer * 16 + 16)
                eng.sem_inc(spare, 1)
                with eng.Fori(0, NG) as g:
                    yield layer * NG + g, g * G

        def upto(eng, count, it, k):
            eng.wait_ge(count.sem, count.after(it, k))

        def ready(eng, it, *use):
            b, n = place[use]
            upto(eng, work_ready[b], it, n + 1)
            return WK[b]

        def taken(eng, it, *use):
            b, n = place[use]
            upto(eng, work_taken[b], it, n + 1)

        def free(eng, it, *use):
            b, n = place[use]
            upto(eng, work_taken[b], it, n)
            return WK[b]

        def is_ready(*use):
            return work_ready[place[use][0]].sem

        def is_taken(*use):
            return work_taken[place[use][0]].sem

        def seat_ready(eng, it, *use):
            b, n = seat[use]
            upto(eng, pair_ready[b], it, n + 1)
            return PAIR[b]

        def seat_taken(eng, it, *use):
            b, n = seat[use]
            upto(eng, pair_taken[b], it, n + 1)

        def seat_free(eng, it, *use):
            b, n = seat[use]
            upto(eng, pair_taken[b], it, n)
            return PAIR[b]

        flat = lambda t: t.rearrange("p a b -> p (a b)")

        @block.sync
        def _(sp):
            with sp.Fori(0, DEPTH) as layer:
                for b in range(2):
                    upto(sp, work_taken[b], layer * NG, 0)
                sp.dma_start(wts[:], layer_in[layer]).then_inc(wts_loaded, 16)
                with sp.Fori(0, NG) as g:
                    it = layer * NG + g
                    for a in range(G // 2):
                        upto(sp, low_done, it, 2 * a + 2)
                        upto(sp, mid_done, it, 2 * a + 2)
                        for b in range(3):
                            upto(sp, pair_ready[b], it, 0)
                        for t, (dst, which) in enumerate(((qs, QPARTS), (ks, KPARTS))):
                            for r, part in enumerate(which):
                                sp.dma_start(dst[HD * r:HD * r + HD, :, 2 * a:2 * a + 2, :].rearrange("d h j w -> d h (j w)"),
                                             flat(parts[:, t, part, 2 * a:2 * a + 2, :])).then_inc(stacked[a].sem, 16)
                    for j in range(G):
                        taken(sp, it, "max", j)
                        sp.dma_start(qs[STACK:STACK + PARTS, :, j, :],
                                     mrows[:, j, :]).then_inc(max_stacked[j].sem, 16)

        @block.tensor
        def _(pe):
            pe.wait_ge(filled, 6)

            def norm_transposed(it, n, a):
                ps = free(pe, it, f"ln{n + 1}", a)
                for j in (2 * a, 2 * a + 1):
                    upto(pe, z_done, it, n * G + j + 1)
                    for c in range(2):
                        mm = nc.tensor.transpose(ps[:, (j % 2) * W + c * C:(j % 2) * W + c * C + C], z[:, j, c, :], ident[0:C, 0:C])
                mm.then_inc(is_ready(f"ln{n + 1}", a), 1)

            def project(it, name, a, col):
                ps = free(pe, it, name, a)
                taken(pe, it, "ln1", a)
                nc.tensor.matmul(ps[:, 0:2 * W], wts[:, col:col + 128], yT[:, 2 * a:2 * a + 2, :],
                                 start=True, stop=True).then_inc(is_ready(name, a), 1)

            def project_rows(it, name, a, src, col):
                ps = free(pe, it, name, a)
                for j in (2 * a, 2 * a + 1):
                    for c in range(2):
                        n = (j % 2) * 2 + c
                        mm = nc.tensor.matmul(ps[0:C, n * 128:n * 128 + 128], src[:, j, c * C:c * C + C],
                                              wts[:, col:col + 128], start=True, stop=True)
                mm.then_inc(is_ready(name, a), 1)

            def scores(it, j, p):
                if p == 0 and j % 2 == 0:
                    upto(pe, stacked[j // 2], it, stacked[j // 2].per)
                ps = seat_free(pe, it, "S", j, p)
                for hh in range(2):
                    for qc in range(2):
                        mm = nc.tensor.matmul(ps[:, hh, qc * W:qc * W + W], qs[0:STACK, 2 * p + hh, j, qc * C:qc * C + C],
                                              ks[0:STACK, 2 * p + hh, j, :], start=True, stop=True)
                mm.then_inc(pair_ready[seat["S", j, p][0]].sem, 1)

            def scores_transposed(it, j, p):
                if p == 0:
                    upto(pe, max_stacked[j], it, 16)
                ps = seat_free(pe, it, "ST", j, p)
                for hh in range(2):
                    for kc in range(2):
                        mm = nc.tensor.matmul(ps[:, hh, kc * W:kc * W + W], ks[:, 2 * p + hh, j, kc * C:kc * C + C],
                                              qs[:, 2 * p + hh, j, :], start=True, stop=True)
                mm.then_inc(pair_ready[seat["ST", j, p][0]].sem, 1)

            def attend(it, j, half):
                if half == 0:
                    free(pe, it, "av", j, 0)
                    if j % 2 == 0:
                        taken(pe, it, "v", j // 2)
                ps = WK[place[("av", j, 0)][0]]
                seat_taken(pe, it, "ST", j, 2 * half)
                seat_taken(pe, it, "ST", j, 2 * half + 1)
                for kc in range(2):
                    keys = C if kc == 0 else TOK - C
                    for g in range(4):
                        hd = 4 * half + g
                        mm = nc.tensor.matmul(ps[32 * g:32 * g + 32, half * W:half * W + W], vaug[0:keys, j, kc, hd, :],
                                              probs[0:keys, hd // 2, hd % 2, kc, :], start=(kc == 0), stop=(kc == 1),
                                              skip_group_check=True)
                mm.then_inc(av_half.sem if half == 0 else is_ready("av", j, 0), 1)

            def turn(it, j):
                ps = free(pe, it, "turn", j)
                taken(pe, it, "av", j, 0)
                for qc in range(2):
                    for half in range(2):
                        n = 2 * qc + half
                        mm = nc.tensor.transpose(ps[0:C, n * 128:n * 128 + 128], oraw[:, j % 2, half, qc * C:qc * C + C], ident[:])
                mm.then_inc(is_ready("turn", j), 1)

            def turn_max(it, j):
                ps = free(pe, it, "max", j)
                upto(pe, msplit, it, 5 * j + 5)
                for qc in range(2):
                    mm = nc.tensor.transpose(ps[:].bitcast(BF16)[0:PARTS * HEADS, qc * 100:qc * 100 + C],
                                             mparts[:, j, qc].rearrange("p n h -> p (n h)"), identb[0:C, 0:C])
                mm.then_inc(is_ready("max", j), 1)

            for it, img in steps(pe):
                for step in plan:
                    what, a = step[0], step[1]
                    if what == "ln1":
                        norm_transposed(it, 0, a)
                    elif what == "q":
                        project(it, "q", a, QW)
                    elif what == "k":
                        project(it, "k", a, KW)
                    elif what == "v":
                        project_rows(it, "v", a, yT, VW)
                    elif what == "S":
                        scores(it, a, step[2])
                    elif what == "ST":
                        scores_transposed(it, a, step[2])
                    elif what == "av":
                        attend(it, a, step[2])
                    elif what == "turn":
                        turn(it, a)
                    elif what == "max":
                        turn_max(it, a)
                    elif what == "oT":
                        ps = free(pe, it, "oT", a)
                        for j in (2 * a, 2 * a + 1):
                            taken(pe, it, "turn", j)
                            for c in range(2):
                                mm = nc.tensor.transpose(ps[:, (j % 2) * W + c * C:(j % 2) * W + c * C + C], o[:, j, c, :], ident[0:C, 0:C])
                        mm.then_inc(is_ready("oT", a), 1)
                    elif what == "proj":
                        taken(pe, it, "oT", a)
                        project_rows(it, "proj", a, oT, PW)
                    elif what == "ln2":
                        norm_transposed(it, 1, a)
                    elif what == "f1":
                        hh = step[2]
                        ps = free(pe, it, "f1", a, hh)
                        taken(pe, it, "ln2", a)
                        nc.tensor.matmul(ps[:, 0:2 * W], wts[:, F1W + 128 * hh:F1W + 128 * hh + 128],
                                         yT[:, 2 * a:2 * a + 2, :], start=True, stop=True).then_inc(is_ready("f1", a, hh), 1)
                    elif what == "f2":
                        ps = free(pe, it, "f2", a)
                        taken(pe, it, "f1", a, 0)
                        taken(pe, it, "f1", a, 1)
                        for jj in range(2):
                            for c in range(2):
                                n = jj * 2 + c
                                for hh in range(2):
                                    mm = nc.tensor.matmul(ps[0:C, n * 128:n * 128 + 128], gT[:, a, hh, jj, c * C:c * C + C],
                                                          wts[:, F2W + 128 * hh:F2W + 128 * hh + 128],
                                                          start=(hh == 0), stop=(hh == 1))
                        mm.then_inc(is_ready("f2", a), 1)

        @block.scalar
        def _(act):
            A = nc.scalar

            def norm(it, n, a, w, b):
                ps = ready(act, it, f"ln{n}", a)
                A.activation(flat(yT[:, 2 * a:2 * a + 2, :]), ps[:, 0:2 * W], ACT.Identity,
                             scale=wts[:, w:w + 1], bias=wts[:, b:b + 1]).then_inc(is_taken(f"ln{n}", a), 1)

            for it, img in steps(act):
                for a in range(G // 2):
                    norm(it, 1, a, LN1W, LN1B)
                    for t, (name, b) in enumerate((("q", QB), ("k", KB))):
                        ps = ready(act, it, name, a)
                        if a == 0:
                            for s in stacked:
                                upto(act, s, it, 0)
                        A.activation(flat(parts[:, t, 0, 2 * a:2 * a + 2, :]), ps[:, 0:2 * W], ACT.Identity,
                                     bias=wts[:, b:b + 1]).then_inc(high_done.sem, 1)
                for j in range(G + LAG + 1):
                    i = j - LAG
                    for p in range(4):
                        if 0 <= i < G:
                            ps = seat_ready(act, it, "ST", i, p)
                            if i >= 1 and p == 0:
                                upto(act, av_half, it, i)
                            if i >= 1 and p == 2:
                                ready(act, it, "av", i - 1, 0)
                            A.activation(probs[:, p].rearrange("p h k w -> p h (k w)"), ps[:, :, 0:2 * W], ACT.Exp,
                                         scale=float(HD) ** -0.5).then_inc(pair_taken[seat["ST", i, p][0]].sem, 1)
                        if p == 0 and 0 <= i - 1:
                            ps = ready(act, it, "av", i - 1, 0)
                            if i >= 3:
                                ready(act, it, "turn", i - 3)
                            A.copy(oraw[:, (i - 1) % 2].rearrange("p h w -> p (h w)"), ps[:, 0:2 * W]
                                   ).then_inc(is_taken("av", i - 1, 0), 1)
                        if p == 1 and 1 <= j <= G:
                            ps = ready(act, it, "max", j - 1)
                            if j == 1:
                                for s in max_stacked:
                                    upto(act, s, it, 0)
                            A.copy(mrows[:, j - 1].rearrange("p (q w) -> p q w", q=2),
                                   ps[:].bitcast(BF16)[0:PARTS * HEADS, 0:200].rearrange("p (q w) -> p q w", q=2)[:, :, 0:C]
                                   ).then_inc(is_taken("max", j - 1), 1)
                for a in range(G // 2):
                    ps = ready(act, it, "oT", a)
                    A.copy(flat(oT[:, 2 * a:2 * a + 2, :]), ps[:, 0:2 * W]).then_inc(is_taken("oT", a), 1)
                for a in range(G // 2):
                    norm(it, 2, a, LN2W, LN2B)
                    for hh in range(2):
                        ps = ready(act, it, "f1", a, hh)
                        A.activation(flat(gT[:, a, hh]), ps[:, 0:2 * W], ACT.Gelu,
                                     bias=wts[:, F1B + hh:F1B + hh + 1]).then_inc(is_taken("f1", a, hh), 1)

        @block.vector
        def _(dve):
            V = nc.vector
            V.memset(ks[STACK:STACK + PARTS], 1.0).then_inc(filled, 1)
            V.memset(vaug[:, :, :, :, 0:HD + 1], 1.0).then_inc(filled, 1)
            V.memset(vaug[:, :, :, :, HD + 1:32], 0.0).then_inc(filled, 1)
            V.tensor_copy(identb[:], ident[:]).then_inc(filled, 1)

            def normalise(it, img, n):
                for j in range(G):
                    for c in range(2):
                        V.bn_stats(stats[:, j, c, :], h[:, img + j, c, :]).then_inc(stats_done.sem, 1)
                for j in range(G):
                    for c in range(2):
                        upto(dve, stats_done, it, 2 * G * n + 2 * j + c + 1)
                        dve.sem_inc(spare, 1)
                        agg = V.bn_aggr(mv[:, j, c, :], stats[:, j, c, :])
                agg.then_inc(mv_done.sem, 1)
                upto(dve, rstd_done, it, n + 1)
                for j in range(G):
                    for c in range(2):
                        zz = V.tensor_scalar(z[:, j, c, :], h[:, img + j, c, :], mv[:, j, c, 0:1],
                                             rstd[:, j, c:c + 1], ALU.subtract, ALU.mult)
                    zz.then_inc(z_done.sem, 1)

            def add_to_h(it, img, name, n, a):
                if a == 0:
                    upto(dve, bias_added, it, n + 1)
                ps = ready(dve, it, name, a)
                hp = h[:, bass.ds(img + 2 * a, 2), :, :].rearrange("p i c d -> p (i c d)")
                V.tensor_tensor(hp, hp, ps[0:C, :], ALU.add).then_inc(is_taken(name, a), 1)

            for it, img in steps(dve):
                dve.sem_inc(spare, 1)
                normalise(it, img, 0)
                for a in range(G // 2):
                    pair = slice(2 * a, 2 * a + 2)
                    for t, (name, b) in enumerate((("q", QB), ("k", KB))):
                        n = 2 * a + t
                        upto(dve, high_done, it, n + 1)
                        ps = WK[place[(name, a)][0]]
                        part = lambda i: flat(parts[:, t, i, pair, :])
                        rs = flat(rest[:, t])
                        V.scalar_tensor_tensor(rs, ps[:, 0:2 * W], wts[:, b:b + 1], part(0), ALU.add, ALU.subtract
                                               ).then_inc(is_taken(name, a), 1)
                        taken(dve, it, name, a)
                        V.tensor_copy(part(1), rs).then_inc(mid_done.sem, 1)
                        upto(dve, mid_done, it, n + 1)
                        V.tensor_tensor(part(2), rs, part(1), ALU.subtract).then_inc(low_done.sem, 1)
                        upto(dve, low_done, it, n + 1)
                    ps = ready(dve, it, "v", a)
                    for jj in range(2):
                        vv = V.tensor_tensor(
                            vaug[:, 2 * a + jj, :, :, 0:HD],
                            ps[0:C, jj * 256:jj * 256 + 256].rearrange("p (n h e) -> p n h e", n=2, h=HEADS),
                            wts[0:C, VB:VB + 128].rearrange("p (n h e) -> p n h e", n=1, h=HEADS).to_broadcast([C, 2, HEADS, HD]),
                            ALU.add)
                    vv.then_inc(is_taken("v", a), 1)
                for j in range(G + LAG + 1):
                    if j < G:
                        for p in range(4):
                            ps = seat_ready(dve, it, "S", j, p)
                            V.tensor_reduce(negmax[:, j, :, 2 * p:2 * p + 2].rearrange("p q h -> p h q"),
                                            ps[:, :, 0:2 * W].rearrange("p h (q k) -> p h q k", q=2)[:, :, :, 0:TOK],
                                            axis=AX.X, op=ALU.max, negate=True).then_inc(pair_taken[seat["S", j, p][0]].sem, 1)
                    i = j - LAG - 1
                    if 0 <= i < G:
                        if i >= 1:
                            taken(dve, it, "turn", i - 1)
                        ps = ready(dve, it, "turn", i)
                        pv = ps[0:C, :].rearrange("p (n e) -> p n e", e=32)
                        V.reciprocal(rsum[:].rearrange("p q h g -> p (q h g)"), pv[:, :, HD]).then_inc(rsum_done.sem, 1)
                        upto(dve, rsum_done, it, i + 1)
                        V.tensor_tensor(o[:, i].rearrange("p q (h e) -> p (q h) e", e=HD), pv[:, :, 0:HD],
                                        rsum[:].rearrange("p q h (g o) -> p (q h g) o", o=1).to_broadcast([C, 2 * HEADS, HD]),
                                        ALU.mult).then_inc(is_taken("turn", i), 1)
                for a in range(G // 2):
                    add_to_h(it, img, "proj", 0, a)
                taken(dve, it, "proj", G // 2 - 1)
                dve.sem_inc(spare, 1)
                normalise(it, img, 1)
                for a in range(G // 2):
                    add_to_h(it, img, "f2", 1, a)
                taken(dve, it, "f2", G // 2 - 1)
                dve.sem_inc(spare, 1)

        @block.gpsimd
        def _(pool):
            P = nc.gpsimd
            P.memset(neghalf[:], -0.5).then_inc(filled, 1)
            P.memset(rstd[:], 0.0).then_inc(filled, 1)
            pool.wait_ge(filled, 6)

            def norm(it, img, n, col):
                upto(pool, mv_done, it, n + 1)
                pool.sem_inc(spare, 1)
                P.tensor_scalar(rstd[:], mv[:, :, :, 1], EPS, None, ALU.add).then_inc(veps_done.sem, 1)
                upto(pool, veps_done, it, n + 1)
                P.tensor_tensor(rstd[:], rstd[:], neghalf[:], ALU.pow).then_inc(rstd_done.sem, 1)
                upto(pool, z_done, it, G * n + G)
                pool.sem_inc(spare, 1)
                hp = h[:, bass.ds(img, G), :, :].rearrange("p i c d -> p (i c) d")
                P.tensor_tensor(hp, hp, wts[0:C, col:col + 128].rearrange("p (n d) -> p n d", n=1)
                                .to_broadcast([C, 2 * G, DIM]), ALU.add).then_inc(bias_added.sem, 1)

            for it, img in steps(pool):
                norm(it, img, 0, PB)
                for j in range(G):
                    for p in range(1, 4):
                        seat_taken(pool, it, "S", j, p)
                    pool.sem_inc(spare, 1)
                    m = negmax[:, j]
                    split = [lambda: P.tensor_copy(mparts[:, j, :, 0], m),
                             lambda: P.tensor_tensor(mrest[:, 0], m, mparts[:, j, :, 0], ALU.subtract),
                             lambda: P.tensor_copy(mparts[:, j, :, 1], mrest[:, 0]),
                             lambda: P.tensor_tensor(mrest[:, 1], mrest[:, 0], mparts[:, j, :, 1], ALU.subtract),
                             lambda: P.tensor_copy(mparts[:, j, :, 2], mrest[:, 1])]
                    for n, op in enumerate(split):
                        op().then_inc(msplit.sem, 1)
                        upto(pool, msplit, it, 5 * j + n + 1)
                        pool.sem_inc(spare, 1)
                norm(it, img, 1, F2B)


def build_norm(nc, B, normw_in, cls_in, h):
    with ExitStack() as ctx:
        sb = lambda name, shape: ctx.enter_context(nc.sbuf_tensor(name, shape, F32))
        sem = lambda name: ctx.enter_context(nc.semaphore(name))
        wb = sb("norm_wb", [C, 2, DIM])
        stats = sb("n_stats", [C, G, 2, 6])
        mv = sb("n_mv", [C, G, 2, 2])
        rstd = sb("n_rstd", [C, G, 2])
        neghalf = sb("n_neghalf", [C, G, 2])
        z = sb("n_z", [C, 2, G, 2, DIM])
        loaded, spare, filled, cls_stored = sem("norm_loaded"), sem("n_spare"), sem("n_filled"), sem("cls_stored")
        stats_done = Count(sem("n_stats_done"), 2 * G)
        mv_done = Count(sem("n_mv_done"), 1)
        veps_done = Count(sem("n_veps_done"), 1)
        rstd_done = Count(sem("n_rstd_done"), 1)
        z_done = Count(sem("n_z_done"), 1)
        scaled = Count(sem("n_scaled"), 1)
        shifted = Count(sem("n_shifted"), 1)
        start(nc)
        block = ctx.enter_context(nc.Block())

        @block.sync
        def _(sp):
            sp.dma_start(wb[:], normw_in).then_inc(loaded, 16)
            sp.wait_ge(shifted.sem, shifted.after(B // G, 0))
            sp.dma_start(h[C - 1:C, :, 1, :], cls_in).then_inc(cls_stored, 16)
            sp.wait_ge(cls_stored, 16)

        @block.vector
        def _(dve):
            dve.wait_ge(loaded, 16)
            with dve.Fori(0, B // G) as it:
                for j in range(G):
                    for c in range(2):
                        nc.vector.bn_stats(stats[:, j, c, :], h[:, it * G + j, c, :]).then_inc(stats_done.sem, 1)
                dve.wait_ge(stats_done.sem, stats_done.after(it, 2 * G))
                dve.sem_inc(spare, 1)
                for j in range(G):
                    for c in range(2):
                        agg = nc.vector.bn_aggr(mv[:, j, c, :], stats[:, j, c, :])
                agg.then_inc(mv_done.sem, 1)
                dve.wait_ge(rstd_done.sem, rstd_done.after(it, 1))
                for j in range(G):
                    for c in range(2):
                        zz = nc.vector.tensor_scalar(z[:, 0, j, c, :], h[:, it * G + j, c, :], mv[:, j, c, 0:1],
                                                     rstd[:, j, c:c + 1], ALU.subtract, ALU.mult)
                zz.then_inc(z_done.sem, 1)
                dve.wait_ge(z_done.sem, z_done.after(it, 1))
                row = lambda n: wb[:, n:n + 1, :].to_broadcast([C, 2 * G, DIM])
                nc.vector.tensor_tensor(z[:, 1].rearrange("p j c d -> p (j c) d"), z[:, 0].rearrange("p j c d -> p (j c) d"),
                                        row(0), ALU.mult).then_inc(scaled.sem, 1)
                dve.wait_ge(scaled.sem, scaled.after(it, 1))
                nc.vector.tensor_tensor(h[:, bass.ds(it * G, G), :, :].rearrange("p j c d -> p (j c) d"),
                                        z[:, 1].rearrange("p j c d -> p (j c) d"), row(1), ALU.add).then_inc(shifted.sem, 1)

        @block.gpsimd
        def _(pool):
            nc.gpsimd.memset(neghalf[:], -0.5).then_inc(filled, 1)
            pool.wait_ge(filled, 1)
            with pool.Fori(0, B // G) as it:
                pool.wait_ge(mv_done.sem, mv_done.after(it, 1))
                pool.sem_inc(spare, 1)
                nc.gpsimd.tensor_scalar(rstd[:], mv[:, :, :, 1], EPS, None, ALU.add).then_inc(veps_done.sem, 1)
                pool.wait_ge(veps_done.sem, veps_done.after(it, 1))
                nc.gpsimd.tensor_tensor(rstd[:], rstd[:], neghalf[:], ALU.pow).then_inc(rstd_done.sem, 1)


AQ, AK, AV, AO = 0, 128, 256, 384
AMASK = 640
ANW = 648
TOPK = W // 10
SEG = 2 * HEADS


def build_attention(nc, B, attw_in, h, ident):
    A = 2
    with ExitStack() as ctx:
        sb = lambda name, shape: ctx.enter_context(nc.sbuf_tensor(name, shape, F32))
        sem = lambda name: ctx.enter_context(nc.semaphore(name))
        wts = sb("a_wts", [128, ANW])
        stats = sb("a_stats", [C, A, 2, 6])
        mv = sb("a_mv", [C, A, 2, 2])
        rstd = sb("a_rstd", [C, A, 2])
        neghalf = sb("a_neghalf", [C, A, 2])
        z = sb("a_z", [C, A, 2, DIM])
        zT = sb("a_zT", [128, A, W])
        qm = sb("a_qm", [128, HEADS, A, W])
        kT = sb("a_kT", [128, A, W])
        v = sb("a_v", [C, A, 2, 144])
        mag = sb("a_mag", [C, A, SEG, W])
        left = sb("a_left", [C, 2, SEG, W])
        top = sb("a_top", [C, SEG, 24])
        total = sb("a_total", [C, A, SEG])
        small = sb("a_small", [C, 6, SEG])
        wgt = sb("a_wgt", [C, SEG, W])
        wT = sb("a_wT", [C, 2, 2, W])
        oT = sb("a_oT", [128, 2, W])
        SC = [ctx.enter_context(nc.psum_tensor(f"a_SC{i}", [C, 512], F32)) for i in range(2)]
        WT = [ctx.enter_context(nc.psum_tensor(f"a_WT{i}", [C, 512], F32)) for i in range(2)]
        OT = ctx.enter_context(nc.psum_tensor("a_OT", [128, 512], F32))
        PR = ctx.enter_context(nc.psum_tensor("a_PR", [C, 512], F32))
        WK = [ctx.enter_context(nc.psum_tensor(f"a_WK{i}", [128, 512], F32)) for i in range(2)]
        uses = ["z", "q", "k", "v"]
        place = {u: (n % 2, n // 2) for n, u in enumerate(uses)}
        work_ready = [Count(sem(f"a_work_ready{b}"), 2) for b in range(2)]
        work_taken = [Count(sem(f"a_work_taken{b}"), 2) for b in range(2)]
        loaded, spare, filled = sem("a_loaded"), sem("a_spare"), sem("a_filled")
        stats_done = Count(sem("a_stats_done"), 2 * A)
        mv_done = Count(sem("a_mv_done"), 1)
        veps_done = Count(sem("a_veps_done"), 1)
        rstd_done = Count(sem("a_rstd_done"), 1)
        z_done = Count(sem("a_z_done"), 1)
        scores_ready = Count(sem("a_scores_ready"), A * HEADS)
        mag_done = Count(sem("a_mag_done"), A * HEADS)
        found = Count(sem("a_found"), A * 3)
        cleared = Count(sem("a_cleared"), A * 4)
        coef_done = Count(sem("a_coef_done"), A * 7)
        wgt_done = Count(sem("a_wgt_done"), A)
        scaled = Count(sem("a_scaled"), A)
        wT_ready = Count(sem("a_wT_ready"), A * HEADS)
        wT_taken = Count(sem("a_wT_taken"), A * HEADS)
        av_done = Count(sem("a_av_done"), A * HEADS)
        oT_taken = Count(sem("a_oT_taken"), A)
        proj_ready = Count(sem("a_proj_ready"), A)
        added = Count(sem("a_added"), A)
        start(nc)
        block = ctx.enter_context(nc.Block())
        steps = lambda eng: eng.Fori(0, B // A)

        def ready(eng, it, use):
            b, n = place[use]
            eng.wait_ge(work_ready[b].sem, work_ready[b].after(it, n + 1))
            return WK[b]

        def taken(eng, it, use):
            b, n = place[use]
            eng.wait_ge(work_taken[b].sem, work_taken[b].after(it, n + 1))

        def free(eng, it, use):
            b, n = place[use]
            eng.wait_ge(work_taken[b].sem, work_taken[b].after(it, n))
            return WK[b]

        def upto(eng, count, it, k):
            eng.wait_ge(count.sem, count.after(it, k))

        @block.sync
        def _(sp):
            sp.dma_start(wts[:], attw_in).then_inc(loaded, 16)

        @block.tensor
        def _(pe):
            pe.wait_ge(loaded, 16)
            with steps(pe) as it:
                ps = free(pe, it, "z")
                upto(pe, z_done, it, 1)
                for j in range(A):
                    for c in range(2):
                        mm = nc.tensor.transpose(ps[:, j * W + c * C:j * W + c * C + C], z[:, j, c, :], ident[0:C, 0:C])
                mm.then_inc(work_ready[place["z"][0]].sem, 1)
                taken(pe, it, "z")
                for name, col in (("q", AQ), ("k", AK)):
                    ps = free(pe, it, name)
                    nc.tensor.matmul(ps[:, 0:A * W], wts[:, col:col + 128], zT[:], start=True, stop=True
                                     ).then_inc(work_ready[place[name][0]].sem, 1)
                ps = free(pe, it, "v")
                for j in range(A):
                    for c in range(2):
                        n = 2 * j + c
                        mm = nc.tensor.matmul(ps[0:C, n * 128:n * 128 + 128], zT[:, j, c * C:c * C + C],
                                              wts[:, AV:AV + 128], start=True, stop=True)
                mm.then_inc(work_ready[place["v"][0]].sem, 1)
                taken(pe, it, "q")
                taken(pe, it, "k")
                for j in range(A):
                    for hd in range(HEADS):
                        u = j * HEADS + hd
                        if u >= 2:
                            upto(pe, mag_done, it, u - 1)
                        for c in range(2):
                            mm = nc.tensor.matmul(SC[u % 2][:, c * W:c * W + W], qm[:, hd, j, c * C:c * C + C],
                                                  kT[:, j, :], start=True, stop=True)
                        mm.then_inc(scores_ready.sem, 1)
                for j in range(A):
                    upto(pe, scaled, it, j + 1)
                    taken(pe, it, "v")
                    upto(pe, oT_taken, it, j)

                    def turn(hd):
                        u = j * HEADS + hd
                        if u >= 2:
                            upto(pe, wT_taken, it, u - 1)
                        for kc in range(2):
                            for c in range(2):
                                mm = nc.tensor.transpose(WT[u % 2][:, kc * W + c * C:kc * W + c * C + C],
                                                         wgt[:, c * HEADS + hd, kc * C:kc * C + C], ident[0:C, 0:C])
                        mm.then_inc(wT_ready.sem, 1)

                    def attend(hd):
                        u = j * HEADS + hd
                        g, half = hd % 4, hd // 4
                        upto(pe, wT_taken, it, u + 1)
                        for kc in range(2):
                            mm = nc.tensor.matmul(OT[32 * g:32 * g + 32, half * W:half * W + W],
                                                  v[:, j, kc, HD * hd:HD * hd + 32], wT[:, u % 2, kc, :],
                                                  start=(kc == 0), stop=(kc == 1))
                        mm.then_inc(av_done.sem, 1)

                    turn(0)
                    for hd in range(1, HEADS):
                        turn(hd)
                        attend(hd - 1)
                    attend(HEADS - 1)
                    upto(pe, oT_taken, it, j + 1)
                    upto(pe, added, it, j)
                    for c in range(2):
                        for half in range(2):
                            mm = nc.tensor.matmul(PR[:, c * 128:c * 128 + 128], oT[:, half, c * C:c * C + C],
                                                  wts[:, AO + 128 * half:AO + 128 * half + 128],
                                                  start=(half == 0), stop=(half == 1))
                    mm.then_inc(proj_ready.sem, 1)

        @block.scalar
        def _(act):
            act.wait_ge(loaded, 16)
            with steps(act) as it:
                ps = ready(act, it, "z")
                nc.scalar.copy(zT[:].rearrange("p a w -> p (a w)"), ps[:, 0:A * W]).then_inc(work_taken[place["z"][0]].sem, 1)
                ps = ready(act, it, "q")
                for hd in range(HEADS):
                    cp = nc.scalar.activation(qm[:, hd].rearrange("p a w -> p (a w)"), ps[:, 0:A * W], ACT.Identity,
                                              scale=wts[:, AMASK + hd:AMASK + hd + 1])
                cp.then_inc(work_taken[place["q"][0]].sem, 1)
                for j in range(A):
                    for hd in range(HEADS):
                        u = j * HEADS + hd
                        upto(act, scores_ready, it, u + 1)
                        for c in range(2):
                            seg = c * HEADS + hd
                            ab = nc.scalar.activation(mag[:, j, seg, :], SC[u % 2][:, c * W:c * W + W], ACT.Abs,
                                                      accum_out=total[:, j, seg:seg + 1])
                        ab.then_inc(mag_done.sem, 1)
                for j in range(A):
                    for hd in range(HEADS):
                        u = j * HEADS + hd
                        upto(act, wT_ready, it, u + 1)
                        if u >= 2:
                            upto(act, av_done, it, u - 1)
                        nc.scalar.copy(wT[:, u % 2].rearrange("p k w -> p (k w)"), WT[u % 2][:, 0:2 * W]).then_inc(wT_taken.sem, 1)
                    upto(act, av_done, it, HEADS * (j + 1))
                    if j >= 1:
                        upto(act, proj_ready, it, j)
                    nc.scalar.copy(oT[:].rearrange("p k w -> p (k w)"), OT[:, 0:2 * W]).then_inc(oT_taken.sem, 1)

        @block.vector
        def _(dve):
            nc.vector.memset(v[:], 0.0).then_inc(filled, 1)
            dve.wait_ge(filled, 2)
            with steps(dve) as it:
                for j in range(A):
                    for c in range(2):
                        nc.vector.bn_stats(stats[:, j, c, :], h[:, it * A + j, c, :]).then_inc(stats_done.sem, 1)
                upto(dve, stats_done, it, 2 * A)
                dve.sem_inc(spare, 1)
                for j in range(A):
                    for c in range(2):
                        agg = nc.vector.bn_aggr(mv[:, j, c, :], stats[:, j, c, :])
                agg.then_inc(mv_done.sem, 1)
                upto(dve, rstd_done, it, 1)
                for j in range(A):
                    for c in range(2):
                        zz = nc.vector.tensor_scalar(z[:, j, c, :], h[:, it * A + j, c, :], mv[:, j, c, 0:1],
                                                     rstd[:, j, c:c + 1], ALU.subtract, ALU.mult)
                zz.then_inc(z_done.sem, 1)
                ps = ready(dve, it, "k")
                nc.vector.tensor_copy(kT[:].rearrange("p a w -> p (a w)"), ps[:, 0:A * W]).then_inc(work_taken[place["k"][0]].sem, 1)
                ps = ready(dve, it, "v")
                nc.vector.tensor_copy(v[:, :, :, 0:DIM].rearrange("p a c d -> p (a c) d"),
                                      ps[0:C, :].rearrange("p (n d) -> p n d", d=DIM)).then_inc(work_taken[place["v"][0]].sem, 1)
                for j in range(A):
                    upto(dve, mag_done, it, HEADS * (j + 1))
                    if j >= 1:
                        upto(dve, coef_done, it, 7 * j)
                    src = mag[:, j]
                    lf = left[:, j % 2]
                    dve.sem_inc(spare, 1)
                    for r in range(3):
                        for s in range(SEG):
                            mx = nc.vector.max(top[:, s, 8 * r:8 * r + 8], src[:, s, :])
                        mx.then_inc(found.sem, 1)
                        upto(dve, found, it, 3 * j + r + 1)
                        if r == 2:
                            nc.vector.memset(top[:, :, TOPK:24], 0.0).then_inc(cleared.sem, 1)
                            upto(dve, cleared, it, 4 * j + 3)
                        dve.sem_inc(spare, 1)
                        for s in range(SEG):
                            mr = nc.vector.match_replace(lf[:, s, :], top[:, s, 8 * r:8 * r + 8], src[:, s, :], 0.0)
                        mr.then_inc(cleared.sem, 1)
                        upto(dve, cleared, it, 4 * j + r + 1 + (r == 2))
                        dve.sem_inc(spare, 1)
                        src = lf
                    steps_ = [
                        lambda: nc.vector.tensor_reduce(small[:, 0:1, :].rearrange("p o s -> p (o s)"), top[:, :, 0:TOPK], axis=AX.X, op=ALU.add),
                        lambda: nc.vector.tensor_scalar(small[:, 1, :], total[:, j, :], 1e-8, None, ALU.add),
                        lambda: nc.vector.reciprocal(small[:, 2, :], small[:, 1, :]),
                        lambda: nc.vector.tensor_tensor(small[:, 3, :], small[:, 0, :], small[:, 2, :], ALU.mult),
                        lambda: nc.vector.tensor_scalar(small[:, 4, :], small[:, 3, :], 1e-8, None, ALU.add),
                        lambda: nc.vector.reciprocal(small[:, 1, :], small[:, 4, :]),
                        lambda: nc.vector.tensor_tensor(small[:, 5, :], small[:, 1, :], small[:, 2, :], ALU.mult),
                    ]
                    if j >= 1:
                        upto(dve, scaled, it, j)
                    for n, step in enumerate(steps_):
                        step().then_inc(coef_done.sem, 1)
                        upto(dve, coef_done, it, 7 * j + n + 1)
                    if j >= 1:
                        upto(dve, wT_ready, it, HEADS * j)
                    nc.vector.tensor_tensor(wgt[:], mag[:, j], lf, ALU.subtract).then_inc(wgt_done.sem, 1)
                for j in range(A):
                    upto(dve, proj_ready, it, j + 1)
                    hp = h[:, bass.ds(it * A + j, 1), :, :].rearrange("p i c d -> p (i c d)")
                    nc.vector.tensor_tensor(hp, hp, PR[:, 0:2 * DIM], ALU.add).then_inc(added.sem, 1)

        @block.gpsimd
        def _(pool):
            nc.gpsimd.memset(neghalf[:], -0.5).then_inc(filled, 1)
            pool.wait_ge(filled, 2)
            with steps(pool) as it:
                upto(pool, mv_done, it, 1)
                pool.sem_inc(spare, 1)
                nc.gpsimd.tensor_scalar(rstd[:], mv[:, :, :, 1], EPS, None, ALU.add).then_inc(veps_done.sem, 1)
                upto(pool, veps_done, it, 1)
                nc.gpsimd.tensor_tensor(rstd[:], rstd[:], neghalf[:], ALU.pow).then_inc(rstd_done.sem, 1)
                for j in range(A):
                    upto(pool, wgt_done, it, j + 1)
                    nc.gpsimd.tensor_tensor(wgt[:], wgt[:], small[:, 5:6, :].rearrange("p o s -> p s o").to_broadcast([C, SEG, W]),
                                            ALU.mult).then_inc(scaled.sem, 1)


FK = 64
TK = 8
NP = 32
TG = 36
GROUPS = ((0, 32), (32, 64), (64, C))
UNIT = 16


def build_ffn(nc, B, ffnq_in, ffnk_in, ffnb_in, iota_in, wdown_in, wup_in, h, ident):
    BF16 = mybir.dt.bfloat16
    U32 = mybir.dt.uint32
    R = SEG * TK
    units = []
    for g, (t0, t1) in enumerate(GROUPS):
        for t in range(t0, t1, UNIT):
            units.append((g, t, min(t + UNIT, t1)))
    per_group = [sum(1 for u in units if u[0] == g) for g in range(len(GROUPS))]
    with ExitStack() as ctx:
        sb = lambda name, shape, dt=F32: ctx.enter_context(nc.sbuf_tensor(name, shape, dt))
        sem = lambda name: ctx.enter_context(nc.semaphore(name))
        bank = lambda name: ctx.enter_context(nc.psum_tensor(name, [128, 512], F32))
        wd = sb("f_wd", [DIM, NP, 128])
        wu = sb("f_wu", [128, NP, DIM])
        wc = sb("f_wc", [128, 2 * HEADS * FK])
        bc = sb("f_bc", [C, 2 * HEADS * FK])
        iota = sb("f_iota", [128, 128, TG], BF16)
        stats = sb("f_stats", [C, 2, 6])
        mv = sb("f_mv", [C, 2, 2])
        rstd = sb("f_rstd", [C, 2])
        neghalf = sb("f_neghalf", [C, 2])
        z = sb("f_z", [C, 2, DIM])
        zT = sb("f_zT", [128, W])
        sc = sb("f_sc", [C, 2, HEADS, 2, FK])
        top = sb("f_top", [C, SEG, 2, TK])
        topi = sb("f_topi", [C, SEG, 2, TK], U32)
        topf = sb("f_topf", [C, SEG, 2, TK])
        pairs = sb("f_pairs", [C, SEG, TK, TK])
        best = sb("f_best", [C, SEG, TK])
        besti = sb("f_besti", [C, SEG, TK], U32)
        rank = sb("f_rank", [C, 2, SEG, TK], U32)
        rankf = sb("f_rankf", [C, 2, SEG, TK])
        pick = sc[:].rearrange("p c h s k -> p (c h s k)").rearrange("p (d s k a) -> p d s k a", d=2, s=SEG, k=TK)
        got = sb("f_got", [C, 2, SEG, TK])
        goti = sb("f_goti", [C, 3, R], U32)
        gotf = sb("f_gotf", [C, 2, R])
        cols = sb("f_cols", [C, 3, R])
        ex = sb("f_ex", [C, 3, SEG, TK])
        esum = sb("f_esum", [C, 2, SEG])
        idx = sb("f_idx", [128, 2, GROUPS[-1][0] + TG], BF16)
        part = sb("f_part", [128, 3, GROUPS[-1][0] + TG], BF16)
        rest = sb("f_rest", [128, 2, GROUPS[-1][0] + TG])
        hotc = sb("f_hotc", [128, NP, TG], BF16)
        outT = sb("f_outT", [128, W])
        WK = [bank(f"f_WK{i}") for i in range(2)]
        IN = [bank(f"f_IN{i}") for i in range(2)]
        AA = [bank(f"f_AA{i}") for i in range(2)]
        OT = bank("f_OT")
        BK = OT[:, 256:512]
        SLOTS = (AA, IN)
        uses = ["z", "s0", "s1", "s2", "s3", "idx"]
        place = {u: (n % 2, n // 2) for n, u in enumerate(uses)}
        work_ready = [Count(sem(f"f_work_ready{b}"), 3) for b in range(2)]
        work_taken = [Count(sem(f"f_work_taken{b}"), 3) for b in range(2)]
        loaded, big_loaded, spare, filled = sem("f_loaded"), sem("f_big_loaded"), sem("f_spare"), sem("f_filled")
        comp_ready, comp_taken = sem("f_comp_ready"), sem("f_comp_taken")
        dve_step = Count(sem("f_dve_step"), 18)
        stats_done = Count(sem("f_stats_done"), 2)
        mv_done = Count(sem("f_mv_done"), 1)
        veps_done = Count(sem("f_veps_done"), 1)
        rstd_done = Count(sem("f_rstd_done"), 1)
        z_done = Count(sem("f_z_done"), 1)
        diff_done = Count(sem("f_diff_done"), 1)
        exp_done = Count(sem("f_exp_done"), 1)
        cols_done = Count(sem("f_cols_done"), 1)
        inner_ready = Count(sem("f_inner_ready"), 16)
        inner_taken = Count(sem("f_inner_taken"), 16)
        hot_done = Count(sem("f_hot_done"), len(GROUPS))
        hotc_done = Count(sem("f_hotc_done"), len(GROUPS))
        hotp_done = Count(sem("f_hotp_done"), 3 * len(GROUPS))
        aa_ready = [Count(sem(f"f_aa_ready{i}"), len(units[i::2])) for i in range(2)]
        aa_taken = [Count(sem(f"f_aa_taken{i}"), len(units[i::2])) for i in range(2)]
        out_ready = Count(sem("f_out_ready"), 1)
        out_taken = Count(sem("f_out_taken"), 1)
        back_ready = Count(sem("f_back_ready"), 1)
        added = Count(sem("f_added"), 1)
        start(nc)

        def upto(eng, count, it, k):
            eng.wait_ge(count.sem, count.after(it, k))

        def ready(eng, it, use):
            b, n = place[use]
            upto(eng, work_ready[b], it, n + 1)
            return WK[b]

        def taken(eng, it, use):
            b, n = place[use]
            upto(eng, work_taken[b], it, n + 1)

        def free(eng, it, use):
            b, n = place[use]
            upto(eng, work_taken[b], it, n)
            return WK[b]

        with ExitStack() as c2:
            qt = c2.enter_context(nc.sbuf_tensor("f_qt", [FK, 2 * HEADS, DIM], F32))
            kt = c2.enter_context(nc.sbuf_tensor("f_kt", [FK, 2 * HEADS, FK], F32))
            bt = c2.enter_context(nc.sbuf_tensor("f_bt", [FK, 2 * HEADS, C], F32))
            numbers = c2.enter_context(nc.sbuf_tensor("f_numbers", [128, 128], F32))
            block = c2.enter_context(nc.Block())

            @block.sync
            def _(sp):
                sp.dma_start(qt[:], ffnq_in).then_inc(loaded, 16)
                sp.dma_start(kt[:], ffnk_in).then_inc(loaded, 16)
                sp.dma_start(bt[:], ffnb_in).then_inc(loaded, 16)
                sp.dma_start(numbers[:], iota_in).then_inc(big_loaded, 16)
                sp.dma_start(wd[:], wdown_in).then_inc(big_loaded, 16)
                sp.dma_start(wu[:], wup_in).then_inc(big_loaded, 16)

            @block.tensor
            def _(pe):
                pe.wait_ge(loaded, 48)
                for n in range(2):
                    for s in range(8):
                        mm = nc.tensor.matmul(IN[n][:, s * FK:s * FK + FK], qt[:, 8 * n + s, :], kt[:, 8 * n + s, :],
                                              start=True, stop=True)
                    mm.then_inc(comp_ready, 1)
                for n in range(2):
                    for s in range(8):
                        mm = nc.tensor.matmul(AA[n][0:C, s * FK:s * FK + FK], bt[:, 8 * n + s, :], kt[:, 8 * n + s, :],
                                              start=True, stop=True)
                    mm.then_inc(comp_ready, 1)

            @block.vector
            def _(dve):
                for n in range(4):
                    dve.wait_ge(comp_ready, n + 1)
                    src = (IN + AA)[n]
                    dst = (wc, bc)[n // 2]
                    rows = (128, C)[n // 2]
                    nc.vector.tensor_copy(dst[:, (n % 2) * 512:(n % 2) * 512 + 512], src[0:rows, :]).then_inc(comp_taken, 1)
                dve.wait_ge(big_loaded, 48)
                nc.vector.tensor_copy(iota[:], numbers[:].rearrange("p (i o) -> p i o", o=1).to_broadcast([128, 128, TG]))
                nc.vector.memset(idx[:], 0.0).then_inc(filled, 1)
                nc.vector.memset(part[:], 0.0).then_inc(filled, 1)
                dve.wait_ge(comp_taken, 4)

        hot = sb("f_hot", [128, 2, 128, TG], BF16)
        act_in = sb("f_act", [128, NP, W])
        hotp = sb("f_hotp", [128, 2, 3, NP, TG], BF16)
        block = ctx.enter_context(nc.Block())

        @block.tensor
        def _(pe):
            def scores(fr):
                ps = free(pe, fr, "z")
                upto(pe, z_done, fr, 1)
                for c in range(2):
                    mm = nc.tensor.transpose(ps[:, c * C:c * C + C], z[:, c, :], ident[0:C, 0:C])
                mm.then_inc(work_ready[place["z"][0]].sem, 1)
                taken(pe, fr, "z")
                for n in range(4):
                    ps = free(pe, fr, f"s{n}")
                    c, f = n // 2, n % 2
                    nc.tensor.matmul(ps[0:C, :], zT[:, c * C:c * C + C], wc[:, 512 * f:512 * f + 512],
                                     start=True, stop=True).then_inc(work_ready[place[f"s{n}"][0]].sem, 1)

            def turn_cols(fr):
                ps = free(pe, fr, "idx")
                upto(pe, cols_done, fr, 1)
                for n in range(3):
                    mm = nc.tensor.transpose(ps[:, n * C:n * C + C], cols[:, n, :], ident[0:C, 0:C])
                mm.then_inc(work_ready[place["idx"][0]].sem, 1)

            def inner(it):
                for n in range(NP // 2):
                    upto(pe, inner_taken, it, max(n - 1, 0))
                    for m in range(2):
                        mm = nc.tensor.matmul(IN[n % 2][:, m * W:m * W + W], wd[:, 2 * n + m, :], zT[:],
                                              start=True, stop=True)
                    mm.then_inc(inner_ready.sem, 1)

            def weights(it, g):
                upto(pe, hotp_done, it, 3 * g + 3)
                for u, (gu, t0, t1) in enumerate(units):
                    if gu != g:
                        continue
                    upto(pe, aa_taken[u % 2], it, u // 2)
                    if u == 1:
                        upto(pe, inner_taken, it, NP // 2)
                    for t in range(t0, t1):
                        tt = t - GROUPS[g][0]
                        col = (t - t0) * NP
                        for c in range(2):
                            for pt in range(3):
                                mm = nc.tensor.matmul(SLOTS[u % 2][c][:, col:col + NP], hot[64 * c:64 * c + 64, g % 2, :, tt],
                                                      hotp[64 * c:64 * c + 64, g % 2, pt, :, tt],
                                                      start=(pt == 0), stop=(pt == 2))
                    mm.then_inc(aa_ready[u % 2].sem, 1)

            pe.wait_ge(big_loaded, 48)
            scores(0)
            turn_cols(0)
            with pe.Fori(0, B) as it:
                fr = it + 1
                inner(it)
                weights(it, 0)
                scores(fr)
                for g in range(1, len(GROUPS)):
                    weights(it, g)
                for i in range(2):
                    upto(pe, aa_taken[i], it, aa_taken[i].per)
                upto(pe, added, it, 0)
                for n in range(NP):
                    mm = nc.tensor.matmul(OT[:, 0:W], wu[:, n, :], act_in[:, n, :], start=(n == 0), stop=(n == NP - 1))
                mm.then_inc(out_ready.sem, 1)
                upto(pe, out_taken, it, 1)
                for c in range(2):
                    mm = nc.tensor.transpose(BK[0:C, c * 128:c * 128 + 128], outT[:, c * C:c * C + C], ident[:])
                mm.then_inc(back_ready.sem, 1)
                turn_cols(fr)

        @block.scalar
        def _(act):
            def copy_z(fr):
                ps = ready(act, fr, "z")
                upto(act, inner_ready, fr - 1, NP // 2)
                nc.scalar.copy(zT[:], ps[:, 0:W]).then_inc(work_taken[place["z"][0]].sem, 1)

            def exps(fr):
                upto(act, diff_done, fr, 1)
                nc.scalar.activation(ex[:, 1], ex[:, 0], ACT.Exp).then_inc(exp_done.sem, 1)

            ps = ready(act, 0, "z")
            nc.scalar.copy(zT[:], ps[:, 0:W]).then_inc(work_taken[place["z"][0]].sem, 1)
            exps(0)
            with act.Fori(0, B) as it:
                fr = it + 1
                upto(act, out_ready, it, 0)
                act.sem_inc(spare, 1)
                for n in range(NP // 2):
                    upto(act, inner_ready, it, n + 1)
                    nc.scalar.activation(act_in[:, 2 * n:2 * n + 2, :].rearrange("p n w -> p (n w)"), IN[n % 2][:, 0:2 * W],
                                         ACT.Relu).then_inc(inner_taken.sem, 1)
                copy_z(fr)
                exps(fr)
                upto(act, out_ready, it, 1)
                nc.scalar.copy(outT[:], OT[:, 0:W]).then_inc(out_taken.sem, 1)

        @block.vector
        def _(dve):
            V = nc.vector
            segs = [(c, hd, side) for c in range(2) for hd in range(HEADS) for side in range(2)]
            n_step = [0]

            def then(ins, fr):
                n_step[0] = n_step[0] % dve_step.per + 1
                ins.then_inc(dve_step.sem, 1)
                upto(dve, dve_step, fr, n_step[0])
                dve.sem_inc(spare, 1)

            def statistics(fr, img):
                for c in range(2):
                    V.bn_stats(stats[:, c, :], h[:, img, c, :]).then_inc(stats_done.sem, 1)
                upto(dve, stats_done, fr, 2)
                dve.sem_inc(spare, 1)
                for c in range(2):
                    agg = V.bn_aggr(mv[:, c, :], stats[:, c, :])
                agg.then_inc(mv_done.sem, 1)

            def normalise(fr, img):
                upto(dve, rstd_done, fr, 1)
                for c in range(2):
                    zz = V.tensor_scalar(z[:, c, :], h[:, img, c, :], mv[:, c, 0:1], rstd[:, c:c + 1], ALU.subtract, ALU.mult)
                zz.then_inc(z_done.sem, 1)

            def copy_scores(fr):
                for n in range(4):
                    c, f = n // 2, n % 2
                    ps = ready(dve, fr, f"s{n}")
                    V.tensor_tensor(sc[:, c, 4 * f:4 * f + 4].rearrange("p h s k -> p (h s k)"), ps[0:C, :],
                                    bc[:, 512 * f:512 * f + 512], ALU.add).then_inc(work_taken[place[f"s{n}"][0]].sem, 1)
                taken(dve, fr, "s2")
                taken(dve, fr, "s3")
                dve.sem_inc(spare, 1)

            def best_keys(fr):
                for c, hd, side in segs:
                    last = V.max(top[:, c * HEADS + hd, side, :], sc[:, c, hd, side, :])
                then(last, fr)
                for c, hd, side in segs:
                    last = V.max_index(topi[:, c * HEADS + hd, side, :], top[:, c * HEADS + hd, side, :], sc[:, c, hd, side, :])
                then(last, fr)
                V.tensor_copy(topf[:], topi[:])

            def best_pairs(fr):
                then(V.tensor_tensor(pairs[:],
                                     top[:, :, 0, :].rearrange("p s (a o) -> p s a o", o=1).to_broadcast([C, SEG, TK, TK]),
                                     top[:, :, 1:2, :].to_broadcast([C, SEG, TK, TK]), ALU.add), fr)
                for s in range(SEG):
                    last = V.max(best[:, s, :], pairs[:, s].rearrange("p a b -> p (a b)"))
                then(last, fr)
                V.tensor_tensor(ex[:, 0], best[:], best[:, :, 0:1].to_broadcast([C, SEG, TK]), ALU.subtract).then_inc(diff_done.sem, 1)
                upto(dve, diff_done, fr, 1)
                dve.sem_inc(spare, 1)
                for s in range(SEG):
                    last = V.max_index(besti[:, s, :], best[:, s, :], pairs[:, s].rearrange("p a b -> p (a b)"))
                then(last, fr)

            def experts(fr):
                V.tensor_scalar(rank[:, 0], besti[:], 3, None, ALU.logical_shift_right)
                then(V.tensor_scalar(rank[:, 1], besti[:], 7, None, ALU.bitwise_and), fr)
                then(V.tensor_copy(rankf[:], rank[:]), fr)
                for side in range(2):
                    for a in range(TK):
                        last = V.scalar_tensor_tensor(pick[:, side, :, :, a], rankf[:, side], float(a),
                                                      topf[:, :, side, a:a + 1].to_broadcast([C, SEG, TK]),
                                                      ALU.is_equal, ALU.mult)
                then(last, fr)
                then(V.tensor_reduce(got[:].rearrange("p d s k -> p (d s k)"), pick.rearrange("p d s k a -> p (d s k) a"),
                                     axis=AX.X, op=ALU.add), fr)
                then(V.tensor_copy(goti[:, 0, :], got[:, 1].rearrange("p s k -> p (s k)")), fr)
                V.tensor_scalar(goti[:, 1, :], goti[:, 0, :], 1, None, ALU.logical_shift_right)
                then(V.tensor_scalar(goti[:, 2, :], goti[:, 0, :], 1, None, ALU.bitwise_and), fr)
                V.tensor_copy(cols[:, 1, :], goti[:, 1, :])
                then(V.tensor_copy(gotf[:, 0, :], goti[:, 2, :]), fr)
                V.scalar_tensor_tensor(cols[:, 0, :], gotf[:, 0, :], float(FK), got[:, 0].rearrange("p s k -> p (s k)"),
                                       ALU.mult, ALU.add)
                upto(dve, exp_done, fr, 1)
                then(V.tensor_reduce(esum[:, 0, :], ex[:, 1], axis=AX.X, op=ALU.add), fr)
                then(V.reciprocal(esum[:, 1, :], esum[:, 0, :]), fr)
                V.tensor_tensor(cols[:, 2, :].rearrange("p (s k) -> p s k", k=TK), ex[:, 1],
                                esum[:, 1, :].rearrange("p (s o) -> p s o", o=1).to_broadcast([C, SEG, TK]),
                                ALU.mult).then_inc(cols_done.sem, 1)

            def split_cols(fr):
                ps = ready(dve, fr, "idx")
                V.tensor_copy(idx[:, :, 0:C], ps[:, 0:2 * C].rearrange("p (n t) -> p n t", n=2))
                wt = ps[:, 2 * C:3 * C]
                then(V.tensor_copy(part[:, 0, 0:C], wt), fr)
                then(V.tensor_tensor(rest[:, 0, 0:C], wt, part[:, 0, 0:C], ALU.subtract), fr)
                then(V.tensor_copy(part[:, 1, 0:C], rest[:, 0, 0:C]), fr)
                then(V.tensor_tensor(rest[:, 1, 0:C], rest[:, 0, 0:C], part[:, 1, 0:C], ALU.subtract), fr)
                V.tensor_copy(part[:, 2, 0:C], rest[:, 1, 0:C]).then_inc(work_taken[place["idx"][0]].sem, 1)
                taken(dve, fr, "idx")

            def one_hots(it, g):
                t0 = GROUPS[g][0]
                if g >= 2:
                    done = sum(per_group[:g - 1]) - 1
                    upto(dve, aa_ready[done % 2], it, done // 2 + 1)
                V.tensor_tensor(hot[:, g % 2], idx[:, 0:1, t0:t0 + TG].to_broadcast([128, 128, TG]), iota[:],
                                ALU.is_equal).then_inc(hot_done.sem, 1)
                V.tensor_tensor(hotc[:], idx[:, 1:2, t0:t0 + TG].to_broadcast([128, NP, TG]), iota[:, 0:NP, :],
                                ALU.is_equal).then_inc(hotc_done.sem, 1)
                upto(dve, hotc_done, it, g + 1)
                for pt in range(3):
                    V.tensor_tensor(hotp[:, g % 2, pt], hotc[:], part[:, pt:pt + 1, t0:t0 + TG].to_broadcast([128, NP, TG]),
                                    ALU.mult).then_inc(hotp_done.sem, 1)
                upto(dve, hotp_done, it, 3 * g + 3)

            def weigh(it, g):
                if g == 0:
                    upto(dve, inner_taken, it, NP // 2)
                for u, (gu, t0, t1) in enumerate(units):
                    if gu != g:
                        continue
                    upto(dve, aa_ready[u % 2], it, u // 2 + 1)
                    for c in range(2):
                        sl = act_in[:, :, c * C + t0:c * C + t1]
                        last = V.tensor_tensor(sl, sl, SLOTS[u % 2][c][:, 0:(t1 - t0) * NP].rearrange("p (t n) -> p n t", n=NP),
                                               ALU.mult)
                    last.then_inc(aa_taken[u % 2].sem, 1)

            dve.wait_ge(filled, 2)
            dve.wait_ge(big_loaded, 48)
            statistics(0, 0)
            normalise(0, 0)
            copy_scores(0)
            best_keys(0)
            best_pairs(0)
            experts(0)
            split_cols(0)
            assert n_step[0] == dve_step.per
            with dve.Fori(0, B) as it:
                fr = it + 1
                img = fr % B
                statistics(fr, img)
                one_hots(it, 0)
                normalise(fr, img)
                one_hots(it, 1)
                weigh(it, 0)
                copy_scores(fr)
                one_hots(it, 2)
                weigh(it, 1)
                best_keys(fr)
                weigh(it, 2)
                best_pairs(fr)
                experts(fr)
                upto(dve, back_ready, it, 1)
                hp = h[:, bass.ds(it, 1), :, :].rearrange("p i c d -> p (i c d)")
                V.tensor_tensor(hp, hp, BK[0:C, 0:2 * DIM], ALU.add).then_inc(added.sem, 1)
                split_cols(fr)
                upto(dve, added, it, 1)
                dve.sem_inc(spare, 1)

        @block.gpsimd
        def _(pool):
            def deviations(fr):
                upto(pool, mv_done, fr, 1)
                pool.sem_inc(spare, 1)
                nc.gpsimd.tensor_scalar(rstd[:], mv[:, :, 1], EPS, None, ALU.add).then_inc(veps_done.sem, 1)
                upto(pool, veps_done, fr, 1)
                nc.gpsimd.tensor_tensor(rstd[:], rstd[:], neghalf[:], ALU.pow).then_inc(rstd_done.sem, 1)

            nc.gpsimd.memset(neghalf[:], -0.5).then_inc(filled, 1)
            pool.wait_ge(filled, 3)
            deviations(0)
            with pool.Fori(0, B) as it:
                deviations(it + 1)


def build(nc, B, DEPTH, x_in, base_in, convw_in, layer_in, ident_in, normw_in, cls_in, attw_in, ffnq_in, ffnk_in, ffnb_in, iota_in, wdown_in, wup_in, out, stage=9):
    with ExitStack() as ctx:
        h = ctx.enter_context(nc.sbuf_tensor("h", [C, B, 2, DIM], F32))
        ident = ctx.enter_context(nc.sbuf_tensor("ident", [128, 128], F32))
        ident_loaded = ctx.enter_context(nc.semaphore("ident_loaded"))
        with nc.Block() as block:
            @block.sync
            def _(sp):
                sp.dma_start(ident[:], ident_in).then_inc(ident_loaded, 16)
                sp.wait_ge(ident_loaded, 16)
        with ExitStack() as c2:
            build_tower(nc, c2, B, DEPTH, x_in, base_in, convw_in, layer_in, h, ident)
        if stage >= 2:
            build_norm(nc, B, normw_in, cls_in, h)
            build_attention(nc, B, attw_in, h, ident)
        if stage >= 3:
            build_ffn(nc, B, ffnq_in, ffnk_in, ffnb_in, iota_in, wdown_in, wup_in, h, ident)
        with ExitStack() as c2:
            stored = c2.enter_context(nc.semaphore("stored"))
            block = c2.enter_context(nc.Block())

            @block.sync
            def _(sp):
                first = 2 + C
                sp.dma_start(out[:, 2:first].rearrange("b p d -> p b d"), h[:, :, 0, :]).then_inc(stored, 16)
                sp.dma_start(out[:, first:W].rearrange("b p d -> p b d"), h[0:W - first, :, 1, :]).then_inc(stored, 16)
                for slot, row in ((C - 2, 1), (C - 1, 0)):
                    sp.dma_start(out[:, row:row + 1].rearrange("b p d -> p b d"), h[slot:slot + 1, :, 1, :]).then_inc(stored, 16)
                sp.wait_ge(stored, 64)


def lay_out(inputs, B):
    import numpy as np
    f = np.float32
    x = np.asarray(inputs["x"])[:B]
    x = x.reshape(B, 3, 14, 16, 14, 16).transpose(0, 1, 3, 5, 2, 4).reshape(B, KC, 128, PATCHES)
    x = np.ascontiguousarray(x.transpose(0, 2, 1, 3))
    cw = np.asarray(inputs["L0_tok_conv_w"]).reshape(KC, 128, DIM).transpose(1, 0, 2)
    pos = np.asarray(inputs["L0_tok_pos_embed"])[0]
    base = np.zeros((2, W, DIM), f)
    base[0, :PATCHES] = pos[1:]
    base[0, PATCHES] = pos[0]
    base[1, :PATCHES] = np.asarray(inputs["L0_tok_conv_b"])
    base[1, PATCHES] = np.asarray(inputs["L0_tok_cls_token"])[0, 0]
    base = base.reshape(2, 2, C, DIM).transpose(2, 0, 1, 3)
    g = lambda n: np.asarray(inputs["L0_tok_" + n])
    L = g("qkv_w").shape[0]
    wt = np.zeros((L, 128, NW), f)
    by_dim = np.arange(DIM).reshape(HEADS, HD).T.reshape(-1)
    wt[:, :, QW:QW + 128], wt[:, :, KW:KW + 128] = g("qkv_w")[:, :, by_dim], g("qkv_w")[:, :, DIM + by_dim]
    wt[:, :, QB], wt[:, :, KB] = g("qkv_b")[:, by_dim], g("qkv_b")[:, DIM + by_dim]
    wt[:, :, VW:VW + 128] = g("qkv_w")[:, :, 256:]
    wt[:, :, PW:PW + 128] = g("proj_w")
    wt[:, :, F1W:F1W + 256] = g("fc1_w")
    wt[:, :, F2W:F2W + 256] = g("fc2_w").reshape(L, 2, 128, DIM).transpose(0, 2, 1, 3).reshape(L, 128, 256)
    wt[:, :, VB:VB + 128] = g("qkv_b")[:, None, 256:]
    wt[:, :, PB:PB + 128] = g("proj_b")[:, None]
    wt[:, :, F2B:F2B + 128] = g("fc2_b")[:, None]
    for col, n in ((LN1W, "ln1_w"), (LN1B, "ln1_b"), (LN2W, "ln2_w"), (LN2B, "ln2_b")):
        wt[:, :, col] = g(n)
    wt[:, :, F1B:F1B + 2] = g("fc1_b").reshape(L, 2, 128).transpose(0, 2, 1)
    nw = np.stack([g("norm_w"), g("norm_b")])
    normw = np.ascontiguousarray(np.broadcast_to(nw, (C, 2, DIM)))
    cls = np.ascontiguousarray(np.broadcast_to(np.asarray(inputs["cls_tok"])[0], (B, DIM)))[None]
    a = lambda n: np.asarray(inputs["L0_attn_" + n])
    at = np.zeros((128, ANW), f)
    at[:, AQ:AQ + 128], at[:, AK:AK + 128], at[:, AV:AV + 128] = a("Wq").T, a("Wk").T, a("Wv").T
    for hd in range(HEADS):
        gr, half = hd % 4, hd // 4
        at[32 * gr:32 * gr + HD, AO + 128 * half:AO + 128 * half + 128] = a("Wo").T[HD * hd:HD * hd + HD]
        at[HD * hd:HD * hd + HD, AMASK + hd] = 2.0
    q = lambda n: np.asarray(inputs["L0_ffn_" + n])
    SH = 2 * HEADS
    fq = np.ascontiguousarray(q("Wq").reshape(DIM, SH, FK).transpose(2, 1, 0))
    fk = np.ascontiguousarray(q("keys").reshape(SH, FK, FK).transpose(2, 0, 1))
    fb = np.ascontiguousarray(np.broadcast_to(q("bq").reshape(SH, FK).T[:, :, None], (FK, SH, C)))
    iota = np.ascontiguousarray(np.broadcast_to(np.arange(128, dtype=f), (128, 128)))
    wd = q("w_down").reshape(FK, NP, 2, DIM).transpose(3, 1, 2, 0).reshape(DIM, NP, 128)
    wu = q("w_up").reshape(FK, NP, 2, DIM).transpose(2, 0, 1, 3).reshape(128, NP, DIM)
    return {"ffnq_in": fq, "ffnk_in": fk, "ffnb_in": fb, "iota_in": iota, "wdown_in": np.ascontiguousarray(wd),
            "wup_in": np.ascontiguousarray(wu), "normw_in": normw, "cls_in": cls, "attw_in": at, "x_in": x, "base_in": np.ascontiguousarray(base), "convw_in": np.ascontiguousarray(cw),
            "layer_in": wt, "ident_in": np.eye(128, dtype=f)}


def kernel(**inputs):
    import concourse.bacc as bacc
    from concourse.bass_utils import run_bass_kernel_spmd

    B = inputs["x"].shape[0]
    arrays = lay_out(inputs, B)
    nc = bacc.Bacc("TRN2", target_bir_lowering=False, num_devices=1)
    aps = {name: nc.dram_tensor(name, a.shape, mybir.dt.from_np(a.dtype), kind="ExternalInput").ap()
           for name, a in arrays.items()}
    out = nc.dram_tensor("out", (B, W, DIM), F32, kind="ExternalOutput").ap()
    build(nc, B, inputs["L0_tok_qkv_w"].shape[0], out=out, **aps)
    return run_bass_kernel_spmd(nc, [arrays], core_ids=[0]).results[0]["out"]
```

```python
from contextlib import ExitStack

import concourse.bass as bass
from concourse import mybir

ALU = mybir.AluOpType
ACT = mybir.ActivationFunctionType
AX = mybir.AxisListType
F32 = mybir.dt.float32

DIM = 128
HEADS = 8
HD = DIM // HEADS
HID = 256
PATCHES = 196
TOK = PATCHES + 1
C = 99
W = 2 * C
KC = 3 * 16 * 16 // 128
G = 4
EPS = 1e-5
PARTS = 3
QPARTS, KPARTS = (0, 0, 0, 1, 1, 2), (0, 1, 2, 0, 1, 0)
STACK = len(QPARTS) * HD
QW, KW, VW, PW, F1W, F2W = 0, 128, 256, 384, 640, 896
VB, PB, F2B = 1152, 1280, 1408
LN1W, LN1B, LN2W, LN2B, QB, KB, F1B = 1536, 1537, 1538, 1539, 1540, 1541, 1542
NW = 1544


class Count:

    made = []

    def __init__(self, sem, per):
        self.sem, self.per = sem, per
        Count.made.append(self)

    def after(self, it, k):
        return it * self.per + (k + 1)


def start(nc):
    with nc.Block() as block:
        @block.gpsimd
        def _(pool):
            for count in Count.made:
                pool.sem_inc(count.sem, 1)
    Count.made.clear()


def build_tower(nc, ctx, B, DEPTH, x_in, base_in, convw_in, layer_in, h, ident):
    NG = B // G
    assert B % (2 * G) == 0
    sem = lambda name: ctx.enter_context(nc.semaphore(name))

    XB = 3
    with ExitStack() as c2:
        xbuf = c2.enter_context(nc.sbuf_tensor("xbuf", [128, XB, KC, W], F32))
        convw = c2.enter_context(nc.sbuf_tensor("convw", [128, KC, DIM], F32))
        base = c2.enter_context(nc.sbuf_tensor("base", [C, 2, 2, DIM], F32))
        emb = [c2.enter_context(nc.psum_tensor(f"emb{i}", [C, 2, DIM], F32)) for i in range(2)]
        x_loaded = [sem(f"x_loaded{i}") for i in range(XB)]
        consts_loaded, x_pad, emb_done, emb_taken, base_done = (
            sem(n) for n in ("consts_loaded", "x_pad", "emb_done", "emb_taken", "base_done"))
        block = c2.enter_context(nc.Block())

        @block.sync
        def _(sp):
            sp.wait_ge(x_pad, 1)
            sp.dma_start(convw[:], convw_in).then_inc(consts_loaded, 16)
            sp.dma_start(base[:], base_in).then_inc(consts_loaded, 16)
            for i in range(B):
                if i >= XB:
                    sp.wait_ge(emb_done, i - XB + 1)
                sp.dma_start(xbuf[:, i % XB, :, 0:PATCHES], x_in[i]).then_inc(x_loaded[i % XB], 16)

        @block.tensor
        def _(pe):
            pe.wait_ge(consts_loaded, 32)
            for i in range(B):
                pe.wait_ge(x_loaded[i % XB], 16 * (i // XB + 1))
                if i >= 2:
                    pe.wait_ge(emb_taken, i - 1)
                for c in range(2):
                    for k in range(KC):
                        mm = nc.tensor.matmul(emb[i % 2][:, c, :], xbuf[:, i % XB, k, c * C:c * C + C],
                                              convw[:, k, :], start=(k == 0), stop=(k == KC - 1))
                mm.then_inc(emb_done, 1)

        @block.vector
        def _(dve):
            nc.vector.memset(xbuf[:, :, :, PATCHES:W], 0.0).then_inc(x_pad, 1)
            dve.wait_ge(consts_loaded, 32)
            nc.vector.tensor_tensor(base[:, 0], base[:, 0], base[:, 1], ALU.add).then_inc(base_done, 1)
            dve.wait_ge(base_done, 1)
            for i in range(B):
                dve.wait_ge(emb_done, i + 1)
                nc.vector.tensor_tensor(h[:, i], emb[i % 2][:], base[:, 0], ALU.add).then_inc(emb_taken, 1)

    BF16 = mybir.dt.bfloat16
    NPAIR = 2
    with ExitStack() as c2:
        sb = lambda name, shape, dt=F32: c2.enter_context(nc.sbuf_tensor(name, shape, dt))
        wts = sb("wts", [128, NW])
        identb = sb("identb", [128, 128], BF16)
        stats = sb("stats", [C, 2, G, 2, 6])
        mv = sb("mv", [C, 2, G, 2, 2])
        rstd = sb("rstd", [C, 2, G, 2])
        neghalf = sb("neghalf", [C, G, 2])
        z = sb("z", [C, 2, G, 2, DIM])
        yT = sb("yT", [128, 2, G, W])
        parts = sb("parts", [128, 2, PARTS, G, W], BF16)
        rest = sb("rest", [128, 2, 2, W])
        qs = sb("qs", [STACK + PARTS, 2, HEADS, G, W], BF16)
        ks = sb("ks", [STACK + PARTS, 2, HEADS, G, W], BF16)
        vaug = sb("vaug", [C, 2, G, 2, HEADS, 32])
        negmax = sb("negmax", [C, G, 2, HEADS])
        mrest = sb("mrest", [C, 2, 2, HEADS])
        mparts = sb("mparts", [C, G, 2, PARTS, HEADS], BF16)
        mrows = sb("mrows", [PARTS * HEADS, G, W], BF16)
        probs = sb("probs", [C, 4, 2, 2, W])
        oraw = sb("oraw", [128, 2, 2, W])
        rsum = sb("rsum", [C, 2, 2, 4])
        o = sb("o", [C, G, 2, DIM])
        oT = sb("oT", [128, G, W])
        gT = sb("gT", [128, G // 2, 2, 2, W])
        PAIR = [c2.enter_context(nc.psum_tensor(f"PAIR{i}", [C, 2, 512], F32)) for i in range(NPAIR)]
        FR = [c2.enter_context(nc.psum_tensor(f"FR{i}", [128, 512], F32)) for i in range(2)]
        WK = [c2.enter_context(nc.psum_tensor(f"WK{i}", [128, 512], F32)) for i in range(2)]

        EARLY = 2
        FRONT_AT = {(2, 2): 0, (3, 0): 1, (3, 3): 2}
        plan = []
        late = [("S", j, p) for j in range(EARLY, G) for p in range(4)]
        for i in range(G + 1):
            for p in range(4):
                plan += [late.pop(0)] if late else []
                if i < G:
                    plan.append(("ST", i, p))
                if p == 0 and i >= 1:
                    plan.append(("av", i - 1, 1))
                if p == 1 and i in (1, 2):
                    plan.append(("max", EARLY + i - 1))
                if p == 2 and i < G:
                    plan.append(("av", i, 0))
                if p == 3 and i >= 1:
                    plan.append(("turn", i - 1))
                if (i, p) in FRONT_AT:
                    plan.append(("front", FRONT_AT[i, p]))
        after = [("next S", j, p) for j in range(EARLY) for p in range(4)]
        for a in range(G // 2):
            plan += [("oT", a), ("proj", a)]
        plan += [after.pop(0), after.pop(0)]
        for a in range(G // 2):
            for piece in (("ln2", a), ("f1", a, 0), ("f1", a, 1)):
                plan += [piece, after.pop(0)]
        plan += [("next max", 0), ("f2", 0), ("f2", 1), ("next max", 1)]
        assert EARLY == 2 and G == 4
        SEAT = {"S": 0, "ST": 1}
        uses = [u for u in plan if u[0] not in ("S", "ST", "front", "max", "next S", "next max") and not (u[0] == "av" and u[2] == 1)]
        assert len(uses) % 2 == 0
        place = {u: (n % 2, n // 2) for n, u in enumerate(uses)}
        fuses = [("ln1", a) for a in range(G // 2)] + [(name, a) for a in range(G // 2) for name in ("q", "k", "v")]
        fuses += [("max", j) for j in range(G)]
        fplace = {u: (n % 2, n // 2) for n, u in enumerate(fuses)}

        work_ready = [Count(sem(f"work_ready{b}"), len(uses) // 2) for b in range(2)]
        work_taken = [Count(sem(f"work_taken{b}"), len(uses) // 2) for b in range(2)]
        front_ready = [Count(sem(f"front_ready{b}"), len(fuses) // 2) for b in range(2)]
        front_taken = [Count(sem(f"front_taken{b}"), len(fuses) // 2) for b in range(2)]
        wts_loaded = sem("wts_loaded")
        filled = sem("filled")
        spare = sem("spare")
        stats_done = [Count(sem(f"stats_done{n}"), 2 * G) for n in range(2)]
        mv_done = [Count(sem(f"mv_done{n}"), 1) for n in range(2)]
        veps_done = [Count(sem(f"veps_done{n}"), 1) for n in range(2)]
        rstd_done = [Count(sem(f"rstd_done{n}"), 1) for n in range(2)]
        z_done = [Count(sem(f"z_done{n}"), G) for n in range(2)]
        bias_added = [Count(sem(f"bias_added{n}"), 1) for n in range(2)]
        high_done = Count(sem("high_done"), G)
        rest_done = Count(sem("rest_done"), G)
        mid_done = Count(sem("mid_done"), G)
        low_done = Count(sem("low_done"), G)
        stacked = [Count(sem(f"stacked{a}"), 16 * 2 * len(QPARTS)) for a in range(G // 2)]
        pair_ready = [Count(sem(f"pair_ready{b}"), 4 * G) for b in range(NPAIR)]
        pair_taken = [Count(sem(f"pair_taken{b}"), 4 * G) for b in range(NPAIR)]
        msplit = Count(sem("msplit"), G * 5)
        max_stacked = [Count(sem(f"max_stacked{j}"), 16) for j in range(G)]
        av_half = Count(sem("av_half"), G)
        rsum_done = Count(sem("rsum_done"), G)
        start(nc)
        block = c2.enter_context(nc.Block())

        def steps(eng, front, rest_of_front=None):
            with eng.Fori(0, DEPTH) as layer:
                eng.wait_ge(wts_loaded, layer * 16 + 16)
                eng.sem_inc(spare, 1)
                front(layer * (NG + 1), 0, 0)
                with eng.Fori(0, NG // 2) as pair:
                    for par in range(2):
                        g = pair * 2 + par
                        yield layer * NG + g, layer * (NG + 1) + g, g * G, (g + 1) % NG * G, par
                if rest_of_front:
                    rest_of_front(layer * (NG + 1) + NG, 0)

        def upto(eng, count, it, k):
            eng.wait_ge(count.sem, count.after(it, k))

        def ready(eng, it, *use):
            b, n = place[use]
            upto(eng, work_ready[b], it, n + 1)
            return WK[b]

        def taken(eng, it, *use):
            b, n = place[use]
            upto(eng, work_taken[b], it, n + 1)

        def free(eng, it, *use):
            b, n = place[use]
            upto(eng, work_taken[b], it, n)
            return WK[b]

        def fready(eng, f, *use):
            b, n = fplace[use]
            upto(eng, front_ready[b], f, n + 1)
            return FR[b]

        def ftaken(eng, f, *use):
            b, n = fplace[use]
            upto(eng, front_taken[b], f, n + 1)

        def ffree(eng, f, *use):
            b, n = fplace[use]
            upto(eng, front_taken[b], f, n)
            return FR[b]

        def is_fready(*use):
            return front_ready[fplace[use][0]].sem

        def is_ftaken(*use):
            return front_taken[fplace[use][0]].sem

        def is_ready(*use):
            return work_ready[place[use][0]].sem

        def is_taken(*use):
            return work_taken[place[use][0]].sem

        def seat_ready(eng, it, what, j, p):
            upto(eng, pair_ready[SEAT[what]], it, 4 * j + p + 1)
            return PAIR[SEAT[what]]

        def seat_taken(eng, it, what, j, p):
            upto(eng, pair_taken[SEAT[what]], it, 4 * j + p + 1)

        def seat_free(eng, it, what, j, p):
            upto(eng, pair_taken[SEAT[what]], it, 4 * j + p)
            return PAIR[SEAT[what]]

        flat = lambda t: t.rearrange("p a b -> p (a b)")

        @block.sync
        def _(sp):
            def stack(it, f, par):
                for a in range(G // 2):
                    upto(sp, low_done, f, 2 * a + 2)
                    upto(sp, mid_done, f, 2 * a + 2)
                    upto(sp, pair_ready[0], f, 0)
                    upto(sp, pair_ready[1], it, 0)
                    for t, (dst, which) in enumerate(((qs, QPARTS), (ks, KPARTS))):
                        for r, part in enumerate(which):
                            sp.dma_start(dst[HD * r:HD * r + HD, par, :, 2 * a:2 * a + 2, :].rearrange("d h j w -> d h (j w)"),
                                         flat(parts[:, t, part, 2 * a:2 * a + 2, :])).then_inc(stacked[a].sem, 16)

            def stack_max(f, par, j):
                ftaken(sp, f, "max", j)
                sp.dma_start(qs[STACK:STACK + PARTS, par, :, j, :], mrows[:, j, :]).then_inc(max_stacked[j].sem, 16)

            with sp.Fori(0, DEPTH) as layer:
                for b in range(2):
                    upto(sp, work_taken[b], layer * NG, 0)
                sp.dma_start(wts[:], layer_in[layer]).then_inc(wts_loaded, 16)
                stack(layer * NG, layer * (NG + 1), 0)
                for j in range(EARLY):
                    stack_max(layer * (NG + 1), 0, j)
                with sp.Fori(0, NG // 2) as pair:
                    for par in range(2):
                        it = layer * NG + pair * 2 + par
                        f = layer * (NG + 1) + pair * 2 + par
                        for j in range(EARLY, G):
                            stack_max(f, par, j)
                        stack(it, f + 1, 1 - par)
                        for j in range(EARLY):
                            stack_max(f + 1, 1 - par, j)
                for j in range(EARLY, G):
                    stack_max(layer * (NG + 1) + NG, 0, j)
            for s in stacked:
                upto(sp, s, DEPTH * (NG + 1), 0)
            for s in max_stacked:
                upto(sp, s, DEPTH * (NG + 1), 0)

        @block.tensor
        def _(pe):
            pe.wait_ge(filled, 6)

            def turn_norm(ps, it, n, a, done):
                for j in (2 * a, 2 * a + 1):
                    upto(pe, z_done[n], it, j + 1)
                    for c in range(2):
                        mm = nc.tensor.transpose(ps[:, (j % 2) * W + c * C:(j % 2) * W + c * C + C], z[:, n, j, c, :], ident[0:C, 0:C])
                mm.then_inc(done, 1)

            def rows(ps, a, src, col, done):
                for j in (2 * a, 2 * a + 1):
                    for c in range(2):
                        n = (j % 2) * 2 + c
                        mm = nc.tensor.matmul(ps[0:C, n * 128:n * 128 + 128], src[:, j, c * C:c * C + C],
                                              wts[:, col:col + 128], start=True, stop=True)
                mm.then_inc(done, 1)

            def front(f, piece):
                if piece == 0:
                    for a in range(G // 2):
                        turn_norm(ffree(pe, f, "ln1", a), f, 0, a, is_fready("ln1", a))
                    return
                a = piece - 1
                assert fplace["q", a][0] == fplace["ln1", a][0]
                for name, col in (("q", QW), ("k", KW)):
                    nc.tensor.matmul(ffree(pe, f, name, a)[:, 0:2 * W], wts[:, col:col + 128], yT[:, 0, 2 * a:2 * a + 2, :],
                                     start=True, stop=True).then_inc(is_fready(name, a), 1)
                rows(ffree(pe, f, "v", a), a, yT[:, 0], VW, is_fready("v", a))

            def scores(f, par, j, p):
                if p == 0 and j % 2 == 0:
                    upto(pe, stacked[j // 2], f, stacked[j // 2].per)
                ps = seat_free(pe, f, "S", j, p)
                for hh in range(2):
                    for qc in range(2):
                        mm = nc.tensor.matmul(ps[:, hh, qc * W:qc * W + W], qs[0:STACK, par, 2 * p + hh, j, qc * C:qc * C + C],
                                              ks[0:STACK, par, 2 * p + hh, j, :], start=True, stop=True)
                mm.then_inc(pair_ready[SEAT["S"]].sem, 1)

            def scores_transposed(it, f, par, j, p):
                if p == 0:
                    upto(pe, max_stacked[j], f, 16)
                ps = seat_free(pe, it, "ST", j, p)
                for hh in range(2):
                    for kc in range(2):
                        mm = nc.tensor.matmul(ps[:, hh, kc * W:kc * W + W], ks[:, par, 2 * p + hh, j, kc * C:kc * C + C],
                                              qs[:, par, 2 * p + hh, j, :], start=True, stop=True)
                mm.then_inc(pair_ready[SEAT["ST"]].sem, 1)

            def attend(it, f, par, j, half):
                if half == 0:
                    free(pe, it, "av", j, 0)
                    if j % 2 == 0:
                        ftaken(pe, f, "v", j // 2)
                ps = WK[place[("av", j, 0)][0]]
                seat_taken(pe, it, "ST", j, 2 * half + 1)
                for kc in range(2):
                    keys = C if kc == 0 else TOK - C
                    for g in range(4):
                        hd = 4 * half + g
                        mm = nc.tensor.matmul(ps[32 * g:32 * g + 32, half * W:half * W + W], vaug[0:keys, par, j, kc, hd, :],
                                              probs[0:keys, hd // 2, hd % 2, kc, :], start=(kc == 0), stop=(kc == 1),
                                              skip_group_check=True)
                mm.then_inc(av_half.sem if half == 0 else is_ready("av", j, 0), 1)

            def turn(it, j):
                ps = free(pe, it, "turn", j)
                taken(pe, it, "av", j, 0)
                for qc in range(2):
                    for half in range(2):
                        n = 2 * qc + half
                        mm = nc.tensor.transpose(ps[0:C, n * 128:n * 128 + 128], oraw[:, j % 2, half, qc * C:qc * C + C], ident[:])
                mm.then_inc(is_ready("turn", j), 1)

            def turn_max(f, j):
                ps = ffree(pe, f, "max", j)
                upto(pe, msplit, f, 5 * j + 5)
                for qc in range(2):
                    mm = nc.tensor.transpose(ps[:].bitcast(BF16)[0:PARTS * HEADS, qc * 100:qc * 100 + C],
                                             mparts[:, j, qc].rearrange("p n h -> p (n h)"), identb[0:C, 0:C])
                mm.then_inc(is_fready("max", j), 1)

            def layer_front(f, img, par):
                for piece in range(3):
                    front(f, piece)
                maxima(f, par, range(EARLY))

            def maxima(f, par, images):
                for j in images:
                    for p in range(4):
                        scores(f, par, j, p)
                    turn_max(f, j)

            for it, f, img, next_img, par in steps(pe, layer_front, lambda f, par: maxima(f, par, range(EARLY, G))):
                for step in plan:
                    what, a = step[0], step[1]
                    if what == "front":
                        front(f + 1, a)
                    elif what == "S":
                        scores(f, par, a, step[2])
                    elif what == "next S":
                        scores(f + 1, 1 - par, a, step[2])
                    elif what == "ST":
                        scores_transposed(it, f, par, a, step[2])
                    elif what == "av":
                        attend(it, f, par, a, step[2])
                    elif what == "turn":
                        turn(it, a)
                    elif what == "max":
                        turn_max(f, a)
                    elif what == "next max":
                        turn_max(f + 1, a)
                    elif what == "oT":
                        ps = free(pe, it, "oT", a)
                        for j in (2 * a, 2 * a + 1):
                            taken(pe, it, "turn", j)
                            for c in range(2):
                                mm = nc.tensor.transpose(ps[:, (j % 2) * W + c * C:(j % 2) * W + c * C + C], o[:, j, c, :], ident[0:C, 0:C])
                        mm.then_inc(is_ready("oT", a), 1)
                    elif what == "proj":
                        taken(pe, it, "oT", a)
                        rows(free(pe, it, "proj", a), a, oT, PW, is_ready("proj", a))
                    elif what == "ln2":
                        turn_norm(free(pe, it, "ln2", a), it, 1, a, is_ready("ln2", a))
                    elif what == "f1":
                        hh = step[2]
                        ps = free(pe, it, "f1", a, hh)
                        taken(pe, it, "ln2", a)
                        nc.tensor.matmul(ps[:, 0:2 * W], wts[:, F1W + 128 * hh:F1W + 128 * hh + 128],
                                         yT[:, 1, 2 * a:2 * a + 2, :], start=True, stop=True).then_inc(is_ready("f1", a, hh), 1)
                    elif what == "f2":
                        ps = free(pe, it, "f2", a)
                        taken(pe, it, "f1", a, 0)
                        taken(pe, it, "f1", a, 1)
                        for jj in range(2):
                            for c in range(2):
                                n = jj * 2 + c
                                for hh in range(2):
                                    mm = nc.tensor.matmul(ps[0:C, n * 128:n * 128 + 128], gT[:, a, hh, jj, c * C:c * C + C],
                                                          wts[:, F2W + 128 * hh:F2W + 128 * hh + 128],
                                                          start=(hh == 0), stop=(hh == 1))
                        mm.then_inc(is_ready("f2", a), 1)

        @block.scalar
        def _(act):
            A = nc.scalar

            def front(f, piece):
                if piece == 0:
                    for a in range(G // 2):
                        ps = fready(act, f, "ln1", a)
                        A.activation(flat(yT[:, 0, 2 * a:2 * a + 2, :]), ps[:, 0:2 * W], ACT.Identity,
                                     scale=wts[:, LN1W:LN1W + 1], bias=wts[:, LN1B:LN1B + 1]).then_inc(is_ftaken("ln1", a), 1)
                    return
                a = piece - 1
                for s in stacked:
                    upto(act, s, f, 0)
                for t, (name, b) in enumerate((("q", QB), ("k", KB))):
                    ps = fready(act, f, name, a)
                    A.activation(flat(parts[:, t, 0, 2 * a:2 * a + 2, :]), ps[:, 0:2 * W], ACT.Identity,
                                 bias=wts[:, b:b + 1]).then_inc(high_done.sem, 1)

            def copy_max(f, j):
                ps = fready(act, f, "max", j)
                upto(act, max_stacked[j], f, 0)
                A.copy(mrows[:, j].rearrange("p (q w) -> p q w", q=2),
                       ps[:].bitcast(BF16)[0:PARTS * HEADS, 0:200].rearrange("p (q w) -> p q w", q=2)[:, :, 0:C]
                       ).then_inc(is_ftaken("max", j), 1)

            def layer_front(f, img, par):
                for piece in range(3):
                    front(f, piece)
                for j in range(EARLY):
                    copy_max(f, j)

            def rest_of_front(f, par):
                for j in range(EARLY, G):
                    copy_max(f, j)

            for it, f, img, next_img, par in steps(act, layer_front, rest_of_front):
                for i in range(G + 1):
                    for p in range(4):
                        if i < G:
                            ps = seat_ready(act, it, "ST", i, p)
                            if i >= 1 and p == 0:
                                upto(act, av_half, it, i)
                            if i >= 1 and p == 2:
                                ready(act, it, "av", i - 1, 0)
                            A.activation(probs[:, p].rearrange("p h k w -> p h (k w)"), ps[:, :, 0:2 * W], ACT.Exp,
                                         scale=float(HD) ** -0.5).then_inc(pair_taken[SEAT["ST"]].sem, 1)
                        if p == 0 and i >= 1:
                            ps = ready(act, it, "av", i - 1, 0)
                            if i >= 3:
                                ready(act, it, "turn", i - 3)
                            A.copy(oraw[:, (i - 1) % 2].rearrange("p h w -> p (h w)"), ps[:, 0:2 * W]
                                   ).then_inc(is_taken("av", i - 1, 0), 1)
                        if p == 1 and i in (1, 2):
                            copy_max(f, EARLY + i - 1)
                        if (i, p) in FRONT_AT:
                            front(f + 1, FRONT_AT[i, p])
                for a in range(G // 2):
                    ps = ready(act, it, "oT", a)
                    A.copy(flat(oT[:, 2 * a:2 * a + 2, :]), ps[:, 0:2 * W]).then_inc(is_taken("oT", a), 1)
                for a in range(G // 2):
                    ps = ready(act, it, "ln2", a)
                    A.activation(flat(yT[:, 1, 2 * a:2 * a + 2, :]), ps[:, 0:2 * W], ACT.Identity,
                                 scale=wts[:, LN2W:LN2W + 1], bias=wts[:, LN2B:LN2B + 1]).then_inc(is_taken("ln2", a), 1)
                    for hh in range(2):
                        ps = ready(act, it, "f1", a, hh)
                        A.activation(flat(gT[:, a, hh]), ps[:, 0:2 * W], ACT.Gelu,
                                     bias=wts[:, F1B + hh:F1B + hh + 1]).then_inc(is_taken("f1", a, hh), 1)
                for j in range(EARLY):
                    copy_max(f + 1, j)

        @block.vector
        def _(dve):
            V = nc.vector
            V.memset(ks[STACK:STACK + PARTS], 1.0).then_inc(filled, 1)
            V.memset(vaug[:, :, :, :, :, 0:HD + 1], 1.0).then_inc(filled, 1)
            V.memset(vaug[:, :, :, :, :, HD + 1:32], 0.0).then_inc(filled, 1)
            V.tensor_copy(identb[:], ident[:]).then_inc(filled, 1)

            def statistics(it, img, n):
                for j in range(G):
                    for c in range(2):
                        V.bn_stats(stats[:, n, j, c, :], h[:, img + j, c, :]).then_inc(stats_done[n].sem, 1)
                upto(dve, stats_done[n], it, 2 * G)
                dve.sem_inc(spare, 1)
                for j in range(G):
                    for c in range(2):
                        agg = V.bn_aggr(mv[:, n, j, c, :], stats[:, n, j, c, :])
                agg.then_inc(mv_done[n].sem, 1)

            def normalise(it, img, n):
                upto(dve, rstd_done[n], it, 1)
                for j in range(G):
                    for c in range(2):
                        zz = V.tensor_scalar(z[:, n, j, c, :], h[:, img + j, c, :], mv[:, n, j, c, 0:1],
                                             rstd[:, n, j, c:c + 1], ALU.subtract, ALU.mult)
                    zz.then_inc(z_done[n].sem, 1)

            def front(f, par, a):
                pair = slice(2 * a, 2 * a + 2)
                for t, (name, b) in enumerate((("q", QB), ("k", KB))):
                    n = 2 * a + t
                    upto(dve, high_done, f, n + 1)
                    ps = FR[fplace[(name, a)][0]]
                    part = lambda i: flat(parts[:, t, i, pair, :])
                    rs = flat(rest[:, t])
                    V.scalar_tensor_tensor(rs, ps[:, 0:2 * W], wts[:, b:b + 1], part(0), ALU.add, ALU.subtract
                                           ).then_inc(is_ftaken(name, a), 1)
                    ftaken(dve, f, name, a)
                    V.tensor_copy(part(1), rs).then_inc(mid_done.sem, 1)
                    upto(dve, mid_done, f, n + 1)
                    V.tensor_tensor(part(2), rs, part(1), ALU.subtract).then_inc(low_done.sem, 1)
                    upto(dve, low_done, f, n + 1)
                ps = fready(dve, f, "v", a)
                for jj in range(2):
                    vv = V.tensor_tensor(
                        vaug[:, par, 2 * a + jj, :, :, 0:HD],
                        ps[0:C, jj * 256:jj * 256 + 256].rearrange("p (n h e) -> p n h e", n=2, h=HEADS),
                        wts[0:C, VB:VB + 128].rearrange("p (n h e) -> p n h e", n=1, h=HEADS).to_broadcast([C, 2, HEADS, HD]),
                        ALU.add)
                vv.then_inc(is_ftaken("v", a), 1)

            def layer_front(f, img, par):
                statistics(f, img, 0)
                normalise(f, img, 0)
                for a in range(G // 2):
                    front(f, par, a)
                for j in range(EARLY):
                    maxima(f, j)

            def maxima(f, j, pairs=range(4)):
                for p in pairs:
                    ps = seat_ready(dve, f, "S", j, p)
                    V.tensor_reduce(negmax[:, j, :, 2 * p:2 * p + 2].rearrange("p q h -> p h q"),
                                    ps[:, :, 0:2 * W].rearrange("p h (q k) -> p h q k", q=2)[:, :, :, 0:TOK],
                                    axis=AX.X, op=ALU.max, negate=True).then_inc(pair_taken[SEAT["S"]].sem, 1)

            def rest_of_front(f, par):
                for j in range(EARLY, G):
                    maxima(f, j)

            def add_to_h(it, img, name, n, a):
                if a == 0:
                    upto(dve, bias_added[n], it, 1)
                ps = ready(dve, it, name, a)
                hp = h[:, bass.ds(img + 2 * a, 2), :, :].rearrange("p i c d -> p (i c d)")
                V.tensor_tensor(hp, hp, ps[0:C, :], ALU.add).then_inc(is_taken(name, a), 1)

            for it, f, img, next_img, par in steps(dve, layer_front, rest_of_front):
                dve.sem_inc(spare, 1)
                for j in range(EARLY, G):
                    maxima(f, j)
                statistics(f + 1, next_img, 0)
                for i in range(G):
                    if i >= 1:
                        taken(dve, it, "turn", i - 1)
                    ps = ready(dve, it, "turn", i)
                    pv = ps[0:C, :].rearrange("p (n e) -> p n e", e=32)
                    V.reciprocal(rsum[:].rearrange("p q h g -> p (q h g)"), pv[:, :, HD]).then_inc(rsum_done.sem, 1)
                    upto(dve, rsum_done, it, i + 1)
                    V.tensor_tensor(o[:, i].rearrange("p q (h e) -> p (q h) e", e=HD), pv[:, :, 0:HD],
                                    rsum[:].rearrange("p q h (g o) -> p (q h g) o", o=1).to_broadcast([C, 2 * HEADS, HD]),
                                    ALU.mult).then_inc(is_taken("turn", i), 1)
                    if i == 0:
                        normalise(f + 1, next_img, 0)
                    if i in (1, 2):
                        front(f + 1, 1 - par, i - 1)
                for a in range(G // 2):
                    add_to_h(it, img, "proj", 0, a)
                taken(dve, it, "proj", G // 2 - 1)
                dve.sem_inc(spare, 1)
                statistics(it, img, 1)
                maxima(f + 1, 0, [0, 1])
                normalise(it, img, 1)
                maxima(f + 1, 0, [2, 3])
                maxima(f + 1, 1)
                for a in range(G // 2):
                    add_to_h(it, img, "f2", 1, a)
                taken(dve, it, "f2", G // 2 - 1)
                dve.sem_inc(spare, 1)

        @block.gpsimd
        def _(pool):
            P = nc.gpsimd
            P.memset(neghalf[:], -0.5).then_inc(filled, 1)
            P.memset(rstd[:], 0.0).then_inc(filled, 1)
            pool.wait_ge(filled, 6)

            def deviations(it, n):
                upto(pool, mv_done[n], it, 1)
                pool.sem_inc(spare, 1)
                P.tensor_scalar(rstd[:, n], mv[:, n, :, :, 1], EPS, None, ALU.add).then_inc(veps_done[n].sem, 1)
                upto(pool, veps_done[n], it, 1)
                P.tensor_tensor(rstd[:, n], rstd[:, n], neghalf[:], ALU.pow).then_inc(rstd_done[n].sem, 1)

            def add_bias(img, n, col):
                pool.sem_inc(spare, 1)
                hp = h[:, bass.ds(img, G), :, :].rearrange("p i c d -> p (i c) d")
                P.tensor_tensor(hp, hp, wts[0:C, col:col + 128].rearrange("p (n d) -> p n d", n=1)
                                .to_broadcast([C, 2 * G, DIM]), ALU.add).then_inc(bias_added[n].sem, 1)

            def split_max(f, j):
                seat_taken(pool, f, "S", j, 3)
                pool.sem_inc(spare, 1)
                m = negmax[:, j]
                for n, op in enumerate((lambda: P.tensor_copy(mparts[:, j, :, 0], m),
                                        lambda: P.tensor_tensor(mrest[:, 0], m, mparts[:, j, :, 0], ALU.subtract),
                                        lambda: P.tensor_copy(mparts[:, j, :, 1], mrest[:, 0]),
                                        lambda: P.tensor_tensor(mrest[:, 1], mrest[:, 0], mparts[:, j, :, 1], ALU.subtract),
                                        lambda: P.tensor_copy(mparts[:, j, :, 2], mrest[:, 1]))):
                    op().then_inc(msplit.sem, 1)
                    upto(pool, msplit, f, 5 * j + n + 1)
                    pool.sem_inc(spare, 1)

            def layer_front(f, img, par):
                deviations(f, 0)
                for j in range(EARLY):
                    split_max(f, j)

            def rest_of_front(f, par):
                for j in range(EARLY, G):
                    split_max(f, j)

            for it, f, img, next_img, par in steps(pool, layer_front, rest_of_front):
                upto(pool, z_done[0], f, G)
                add_bias(img, 0, PB)
                rest_of_front(f, par)
                deviations(f + 1, 0)
                deviations(it, 1)
                split_max(f + 1, 0)
                upto(pool, z_done[1], it, G)
                add_bias(img, 1, F2B)
                split_max(f + 1, 1)


def build_norm(nc, B, normw_in, cls_in, h):
    with ExitStack() as ctx:
        sb = lambda name, shape: ctx.enter_context(nc.sbuf_tensor(name, shape, F32))
        sem = lambda name: ctx.enter_context(nc.semaphore(name))
        wb = sb("norm_wb", [C, 2, DIM])
        stats = sb("n_stats", [C, G, 2, 6])
        mv = sb("n_mv", [C, G, 2, 2])
        rstd = sb("n_rstd", [C, G, 2])
        neghalf = sb("n_neghalf", [C, G, 2])
        z = sb("n_z", [C, 2, G, 2, DIM])
        loaded, spare, filled, cls_stored = sem("norm_loaded"), sem("n_spare"), sem("n_filled"), sem("cls_stored")
        stats_done = Count(sem("n_stats_done"), 2 * G)
        mv_done = Count(sem("n_mv_done"), 1)
        veps_done = Count(sem("n_veps_done"), 1)
        rstd_done = Count(sem("n_rstd_done"), 1)
        z_done = Count(sem("n_z_done"), 1)
        scaled = Count(sem("n_scaled"), 1)
        shifted = Count(sem("n_shifted"), 1)
        start(nc)
        block = ctx.enter_context(nc.Block())

        @block.sync
        def _(sp):
            sp.dma_start(wb[:], normw_in).then_inc(loaded, 16)
            sp.wait_ge(shifted.sem, shifted.after(B // G, 0))
            sp.dma_start(h[C - 1:C, :, 1, :], cls_in).then_inc(cls_stored, 16)
            sp.wait_ge(cls_stored, 16)

        @block.vector
        def _(dve):
            def statistics(it, img):
                for j in range(G):
                    for c in range(2):
                        nc.vector.bn_stats(stats[:, j, c, :], h[:, img + j, c, :]).then_inc(stats_done.sem, 1)
                dve.wait_ge(stats_done.sem, stats_done.after(it, 2 * G))
                dve.sem_inc(spare, 1)
                for j in range(G):
                    for c in range(2):
                        agg = nc.vector.bn_aggr(mv[:, j, c, :], stats[:, j, c, :])
                agg.then_inc(mv_done.sem, 1)

            dve.wait_ge(loaded, 16)
            statistics(0, 0)
            with dve.Fori(0, B // G) as it:
                dve.wait_ge(rstd_done.sem, rstd_done.after(it, 1))
                for j in range(G):
                    for c in range(2):
                        zz = nc.vector.tensor_scalar(z[:, 0, j, c, :], h[:, it * G + j, c, :], mv[:, j, c, 0:1],
                                                     rstd[:, j, c:c + 1], ALU.subtract, ALU.mult)
                zz.then_inc(z_done.sem, 1)
                statistics(it + 1, (it + 1) % (B // G) * G)
                dve.wait_ge(z_done.sem, z_done.after(it, 1))
                row = lambda n: wb[:, n:n + 1, :].to_broadcast([C, 2 * G, DIM])
                nc.vector.tensor_tensor(z[:, 1].rearrange("p j c d -> p (j c) d"), z[:, 0].rearrange("p j c d -> p (j c) d"),
                                        row(0), ALU.mult).then_inc(scaled.sem, 1)
                dve.wait_ge(scaled.sem, scaled.after(it, 1))
                nc.vector.tensor_tensor(h[:, bass.ds(it * G, G), :, :].rearrange("p j c d -> p (j c) d"),
                                        z[:, 1].rearrange("p j c d -> p (j c) d"), row(1), ALU.add).then_inc(shifted.sem, 1)
                dve.wait_ge(shifted.sem, shifted.after(it, 1))
                dve.sem_inc(spare, 1)

        @block.gpsimd
        def _(pool):
            nc.gpsimd.memset(neghalf[:], -0.5).then_inc(filled, 1)
            pool.wait_ge(filled, 1)
            with pool.Fori(0, B // G + 1) as it:
                pool.wait_ge(mv_done.sem, mv_done.after(it, 1))
                pool.sem_inc(spare, 1)
                nc.gpsimd.tensor_scalar(rstd[:], mv[:, :, :, 1], EPS, None, ALU.add).then_inc(veps_done.sem, 1)
                pool.wait_ge(veps_done.sem, veps_done.after(it, 1))
                nc.gpsimd.tensor_tensor(rstd[:], rstd[:], neghalf[:], ALU.pow).then_inc(rstd_done.sem, 1)


AQ, AK, AV, AO = 0, 128, 256, 384
AMASK = 640
ANW = 648
TOPK = W // 10
SEG = 2 * HEADS


def build_attention(nc, B, attw_in, h, ident):
    with ExitStack() as ctx:
        sb = lambda name, shape: ctx.enter_context(nc.sbuf_tensor(name, shape, F32))
        sem = lambda name: ctx.enter_context(nc.semaphore(name))
        wts = sb("a_wts", [128, ANW])
        stats = sb("a_stats", [C, 2, 6])
        mv = sb("a_mv", [C, 2, 2])
        rstd = sb("a_rstd", [C, 2])
        neghalf = sb("a_neghalf", [C, 2])
        z = sb("a_z", [C, 2, DIM])
        zT = sb("a_zT", [128, W])
        qm = sb("a_qm", [128, HEADS, W])
        kT = sb("a_kT", [128, W])
        v = sb("a_v", [C, 2, 2, 144])
        mag = sb("a_mag", [C, 2, SEG, W])
        left = sb("a_left", [C, 2, SEG, W])
        total = sb("a_total", [C, 2, SEG])
        top = sb("a_top", [C, SEG, 24])
        small = sb("a_small", [C, 6, SEG])
        wgt = sb("a_wgt", [C, SEG, W])
        wT = sb("a_wT", [C, 2, 2, W])
        oT = sb("a_oT", [128, 2, W])
        SC = [ctx.enter_context(nc.psum_tensor(f"a_SC{i}", [C, 512], F32)) for i in range(2)]
        WT = [ctx.enter_context(nc.psum_tensor(f"a_WT{i}", [C, 512], F32)) for i in range(2)]
        OT = ctx.enter_context(nc.psum_tensor("a_OT", [128, 512], F32))
        PR = ctx.enter_context(nc.psum_tensor("a_PR", [C, 512], F32))
        ZK = ctx.enter_context(nc.psum_tensor("a_ZK", [128, 512], F32))
        QV = ctx.enter_context(nc.psum_tensor("a_QV", [128, 512], F32))
        z_ps, k_ps = ZK[:, 0:W], ZK[:, 256:256 + W]
        q_ps, v_ps = QV[:, 0:W], QV[0:C, 256:512]
        loaded, spare, filled = sem("a_loaded"), sem("a_spare"), sem("a_filled")
        stats_done = Count(sem("a_stats_done"), 2)
        mv_done = Count(sem("a_mv_done"), 1)
        veps_done = Count(sem("a_veps_done"), 1)
        rstd_done = Count(sem("a_rstd_done"), 1)
        z_done = Count(sem("a_z_done"), 1)
        z_turned = Count(sem("a_z_turned"), 1)
        zT_done = Count(sem("a_zT_done"), 1)
        q_ready = Count(sem("a_q_ready"), 1)
        q_taken = Count(sem("a_q_taken"), 1)
        k_ready = Count(sem("a_k_ready"), 1)
        k_taken = Count(sem("a_k_taken"), 1)
        v_ready = Count(sem("a_v_ready"), 1)
        v_taken = Count(sem("a_v_taken"), 1)
        scores_ready = Count(sem("a_scores_ready"), HEADS)
        mag_done = Count(sem("a_mag_done"), HEADS)
        found = Count(sem("a_found"), 3)
        cleared = Count(sem("a_cleared"), 4)
        coef_done = Count(sem("a_coef_done"), 7)
        kept = Count(sem("a_kept"), 1)
        scaled = Count(sem("a_scaled"), 1)
        wT_ready = Count(sem("a_wT_ready"), HEADS)
        wT_taken = Count(sem("a_wT_taken"), HEADS)
        av_done = Count(sem("a_av_done"), HEADS)
        oT_taken = Count(sem("a_oT_taken"), 1)
        proj_ready = Count(sem("a_proj_ready"), 1)
        added = Count(sem("a_added"), 1)
        start(nc)
        block = ctx.enter_context(nc.Block())
        steps = lambda eng: eng.Fori(0, B // 2)

        def upto(eng, count, n, k):
            eng.wait_ge(count.sem, count.after(n, k))

        @block.sync
        def _(sp):
            sp.dma_start(wts[:], attw_in).then_inc(loaded, 16)

        @block.tensor
        def _(pe):
            def front(n):
                upto(pe, z_done, n, 1)
                upto(pe, k_taken, n, 0)
                for c in range(2):
                    mm = nc.tensor.transpose(z_ps[:, c * C:c * C + C], z[:, c, :], ident[0:C, 0:C])
                mm.then_inc(z_turned.sem, 1)
                upto(pe, zT_done, n, 1)
                upto(pe, v_taken, n, 0)
                nc.tensor.matmul(q_ps, wts[:, AQ:AQ + 128], zT[:], start=True, stop=True).then_inc(q_ready.sem, 1)
                nc.tensor.matmul(k_ps, wts[:, AK:AK + 128], zT[:], start=True, stop=True).then_inc(k_ready.sem, 1)
                upto(pe, q_taken, n, 1)
                upto(pe, k_taken, n, 1)
                for hd in range(HEADS):
                    if hd >= 2:
                        upto(pe, mag_done, n, hd - 1)
                    for c in range(2):
                        mm = nc.tensor.matmul(SC[hd % 2][:, c * W:c * W + W], qm[:, hd, c * C:c * C + C], kT[:],
                                              start=True, stop=True)
                    mm.then_inc(scores_ready.sem, 1)

            def values(n):
                for c in range(2):
                    mm = nc.tensor.matmul(v_ps[:, c * 128:c * 128 + 128], zT[:, c * C:c * C + C], wts[:, AV:AV + 128],
                                          start=True, stop=True)
                mm.then_inc(v_ready.sem, 1)

            def turn(n, hd):
                if hd >= 2:
                    upto(pe, wT_taken, n, hd - 1)
                for kc in range(2):
                    for c in range(2):
                        mm = nc.tensor.transpose(WT[hd % 2][:, kc * W + c * C:kc * W + c * C + C],
                                                 wgt[:, c * HEADS + hd, kc * C:kc * C + C], ident[0:C, 0:C])
                mm.then_inc(wT_ready.sem, 1)

            def attend(n, par, hd):
                g, half = hd % 4, hd // 4
                upto(pe, wT_taken, n, hd + 1)
                for kc in range(2):
                    mm = nc.tensor.matmul(OT[32 * g:32 * g + 32, half * W:half * W + W],
                                          v[:, par, kc, HD * hd:HD * hd + 32], wT[:, hd % 2, kc, :],
                                          start=(kc == 0), stop=(kc == 1))
                mm.then_inc(av_done.sem, 1)

            def back(n, par):
                upto(pe, scaled, n, 1)
                upto(pe, v_taken, n, 1)
                upto(pe, oT_taken, n, 0)
                turn(n, 0)
                for hd in range(1, HEADS):
                    turn(n, hd)
                    attend(n, par, hd - 1)
                attend(n, par, HEADS - 1)
                upto(pe, oT_taken, n, 1)
                upto(pe, added, n, 0)
                for c in range(2):
                    for half in range(2):
                        mm = nc.tensor.matmul(PR[:, c * 128:c * 128 + 128], oT[:, half, c * C:c * C + C],
                                              wts[:, AO + 128 * half:AO + 128 * half + 128],
                                              start=(half == 0), stop=(half == 1))
                mm.then_inc(proj_ready.sem, 1)

            pe.wait_ge(loaded, 16)
            for n in range(2):
                front(n)
                values(n)
            with steps(pe) as it:
                for par in range(2):
                    n = it * 2 + par
                    front(n + 2)
                    back(n, par)
                    values(n + 2)

        @block.scalar
        def _(act):
            def front(n, par):
                upto(act, z_turned, n, 1)
                upto(act, v_ready, n, 0)
                nc.scalar.copy(zT[:], z_ps).then_inc(zT_done.sem, 1)
                upto(act, q_ready, n, 1)
                for hd in range(HEADS):
                    cp = nc.scalar.activation(qm[:, hd], q_ps, ACT.Identity, scale=wts[:, AMASK + hd:AMASK + hd + 1])
                cp.then_inc(q_taken.sem, 1)
                upto(act, k_ready, n, 1)
                nc.scalar.copy(kT[:], k_ps).then_inc(k_taken.sem, 1)

            def magnitudes(n, par):
                for hd in range(HEADS):
                    upto(act, scores_ready, n, hd + 1)
                    for c in range(2):
                        seg = c * HEADS + hd
                        ab = nc.scalar.activation(mag[:, par, seg, :], SC[hd % 2][:, c * W:c * W + W], ACT.Abs,
                                                  accum_out=total[:, par, seg:seg + 1])
                    ab.then_inc(mag_done.sem, 1)

            def values(n, par):
                upto(act, v_ready, n, 1)
                nc.scalar.copy(v[:, par, :, 0:DIM], v_ps.rearrange("p (n d) -> p n d", d=DIM)).then_inc(v_taken.sem, 1)

            def back(n):
                for hd in range(HEADS):
                    upto(act, wT_ready, n, hd + 1)
                    if hd >= 2:
                        upto(act, av_done, n, hd - 1)
                    nc.scalar.copy(wT[:, hd % 2].rearrange("p k w -> p (k w)"), WT[hd % 2][:, 0:2 * W]).then_inc(wT_taken.sem, 1)
                upto(act, av_done, n, HEADS)
                upto(act, proj_ready, n, 0)
                act.sem_inc(spare, 1)
                nc.scalar.copy(oT[:].rearrange("p k w -> p (k w)"), OT[:, 0:2 * W]).then_inc(oT_taken.sem, 1)

            act.wait_ge(loaded, 16)
            act.wait_ge(filled, 2)
            for n in range(2):
                front(n, n)
                magnitudes(n, n)
                values(n, n)
            with steps(act) as it:
                for par in range(2):
                    n = it * 2 + par
                    front(n + 2, par)
                    upto(act, kept, n, 1)
                    act.sem_inc(spare, 1)
                    magnitudes(n + 2, par)
                    back(n)
                    values(n + 2, par)

        @block.vector
        def _(dve):
            V = nc.vector

            def statistics(n, img):
                for c in range(2):
                    V.bn_stats(stats[:, c, :], h[:, img, c, :]).then_inc(stats_done.sem, 1)
                upto(dve, stats_done, n, 2)
                dve.sem_inc(spare, 1)
                for c in range(2):
                    agg = V.bn_aggr(mv[:, c, :], stats[:, c, :])
                agg.then_inc(mv_done.sem, 1)

            def normalise(n, img):
                upto(dve, rstd_done, n, 1)
                upto(dve, z_turned, n, 0)
                dve.sem_inc(spare, 1)
                for c in range(2):
                    zz = V.tensor_scalar(z[:, c, :], h[:, img, c, :], mv[:, c, 0:1], rstd[:, c:c + 1], ALU.subtract, ALU.mult)
                zz.then_inc(z_done.sem, 1)

            def find(n, src, r):
                for s in range(SEG):
                    mx = V.max(top[:, s, 8 * r:8 * r + 8], src[:, s, :])
                mx.then_inc(found.sem, 1)
                upto(dve, found, n, r + 1)
                if r == 2:
                    V.memset(top[:, :, TOPK:24], 0.0).then_inc(cleared.sem, 1)
                    upto(dve, cleared, n, 3)
                dve.sem_inc(spare, 1)

            def take_out(n, par, src, r):
                for s in range(SEG):
                    mr = V.match_replace(left[:, par, s, :], top[:, s, 8 * r:8 * r + 8], src[:, s, :], 0.0)
                mr.then_inc(cleared.sem, 1)
                upto(dve, cleared, n, r + 1 + (r == 2))
                dve.sem_inc(spare, 1)

            def coefficients(n, par):
                upto(dve, scaled, n, 0)
                for k, step in enumerate((
                    lambda: V.tensor_reduce(small[:, 0:1, :].rearrange("p o s -> p (o s)"), top[:, :, 0:TOPK], axis=AX.X, op=ALU.add),
                    lambda: V.tensor_scalar(small[:, 1, :], total[:, par, :], 1e-8, None, ALU.add),
                    lambda: V.reciprocal(small[:, 2, :], small[:, 1, :]),
                    lambda: V.tensor_tensor(small[:, 3, :], small[:, 0, :], small[:, 2, :], ALU.mult),
                    lambda: V.tensor_scalar(small[:, 4, :], small[:, 3, :], 1e-8, None, ALU.add),
                    lambda: V.reciprocal(small[:, 1, :], small[:, 4, :]),
                    lambda: V.tensor_tensor(small[:, 5, :], small[:, 1, :], small[:, 2, :], ALU.mult),
                )):
                    step().then_inc(coef_done.sem, 1)
                    upto(dve, coef_done, n, k + 1)

            def pick(n, par, next_img, first=False):
                upto(dve, mag_done, n, HEADS)
                dve.sem_inc(spare, 1)
                find(n, mag[:, par], 0)
                if not first:
                    upto(dve, kept, n - 1, 0)
                    dve.sem_inc(spare, 1)
                take_out(n, par, mag[:, par], 0)
                find(n, left[:, par], 1)
                take_out(n, par, left[:, par], 1)
                find(n, left[:, par], 2)
                statistics(n + 2, next_img)
                take_out(n, par, left[:, par], 2)
                coefficients(n, par)

            V.memset(v[:], 0.0).then_inc(filled, 1)
            dve.wait_ge(filled, 2)
            statistics(0, 0)
            normalise(0, 0)
            statistics(1, 1)
            normalise(1, 1)
            pick(0, 0, 2, first=True)
            with steps(dve) as it:
                for par in range(2):
                    n = it * 2 + par
                    normalise(n + 2, (n + 2) % B)
                    pick(n + 1, 1 - par, (n + 3) % B)
                    upto(dve, proj_ready, n, 1)
                    hp = h[:, bass.ds(n, 1), :, :].rearrange("p i c d -> p (i c d)")
                    V.tensor_tensor(hp, hp, PR[:, 0:2 * DIM], ALU.add).then_inc(added.sem, 1)
                    upto(dve, added, n, 1)
                    dve.sem_inc(spare, 1)

        @block.gpsimd
        def _(pool):
            def deviations(n):
                upto(pool, mv_done, n, 1)
                pool.sem_inc(spare, 1)
                nc.gpsimd.tensor_scalar(rstd[:], mv[:, :, 1], EPS, None, ALU.add).then_inc(veps_done.sem, 1)
                upto(pool, veps_done, n, 1)
                nc.gpsimd.tensor_tensor(rstd[:], rstd[:], neghalf[:], ALU.pow).then_inc(rstd_done.sem, 1)

            def weigh(n, par):
                upto(pool, coef_done, n, 7)
                pool.sem_inc(spare, 1)
                nc.gpsimd.tensor_tensor(wgt[:], mag[:, par], left[:, par], ALU.subtract).then_inc(kept.sem, 1)
                upto(pool, kept, n, 1)
                nc.gpsimd.tensor_tensor(wgt[:], wgt[:], small[:, 5:6, :].rearrange("p o s -> p s o").to_broadcast([C, SEG, W]),
                                        ALU.mult).then_inc(scaled.sem, 1)

            nc.gpsimd.memset(neghalf[:], -0.5).then_inc(filled, 1)
            pool.wait_ge(filled, 2)
            deviations(0)
            deviations(1)
            deviations(2)
            weigh(0, 0)
            with steps(pool) as it:
                for par in range(2):
                    n = it * 2 + par
                    deviations(n + 3)
                    upto(pool, wT_ready, n, HEADS)
                    weigh(n + 1, 1 - par)


FK = 64
TK = 8
NP = 32
TG = 36
GROUPS = ((0, 32), (32, 64), (64, C))
UNIT = 16


def build_ffn(nc, B, ffnq_in, ffnk_in, ffnb_in, iota_in, wdown_in, wup_in, h, ident):
    BF16 = mybir.dt.bfloat16
    U32 = mybir.dt.uint32
    R = SEG * TK
    units = []
    for g, (t0, t1) in enumerate(GROUPS):
        for t in range(t0, t1, UNIT):
            units.append((g, t, min(t + UNIT, t1)))
    per_group = [sum(1 for u in units if u[0] == g) for g in range(len(GROUPS))]
    with ExitStack() as ctx:
        sb = lambda name, shape, dt=F32: ctx.enter_context(nc.sbuf_tensor(name, shape, dt))
        sem = lambda name: ctx.enter_context(nc.semaphore(name))
        bank = lambda name: ctx.enter_context(nc.psum_tensor(name, [128, 512], F32))
        wd = sb("f_wd", [DIM, NP, 128])
        wu = sb("f_wu", [128, NP, DIM])
        wc = sb("f_wc", [128, 2 * HEADS * FK])
        bc = sb("f_bc", [C, 2 * HEADS * FK])
        iota = sb("f_iota", [128, 128, TG], BF16)
        stats = sb("f_stats", [C, 2, 6])
        mv = sb("f_mv", [C, 2, 2])
        rstd = sb("f_rstd", [C, 2])
        neghalf = sb("f_neghalf", [C, 2])
        z = sb("f_z", [C, 2, DIM])
        zT = sb("f_zT", [128, 2, W])
        sc = sb("f_sc", [C, 2, HEADS, 2, FK])
        top = sb("f_top", [C, SEG, 2, TK])
        topi = sb("f_topi", [C, SEG, 2, TK], U32)
        topf = sb("f_topf", [C, SEG, 2, TK])
        pairs = sb("f_pairs", [C, SEG, TK, TK])
        best = sb("f_best", [C, SEG, TK])
        besti = sb("f_besti", [C, SEG, TK], U32)
        rank = sb("f_rank", [C, 2, SEG, TK], U32)
        rankf = sb("f_rankf", [C, 2, SEG, TK])
        pick = sc[:].rearrange("p c h s k -> p (c h s k)").rearrange("p (d s k a) -> p d s k a", d=2, s=SEG, k=TK)
        got = sb("f_got", [C, 2, SEG, TK])
        goti = sb("f_goti", [C, 3, R], U32)
        gotf = sb("f_gotf", [C, 2, R])
        cols = sb("f_cols", [C, 3, R])
        ex = sb("f_ex", [C, 3, SEG, TK])
        esum = sb("f_esum", [C, 2, SEG])
        idx = sb("f_idx", [128, 2, GROUPS[-1][0] + TG], BF16)
        part = sb("f_part", [128, 3, GROUPS[-1][0] + TG], BF16)
        rest = sb("f_rest", [128, 2, GROUPS[-1][0] + TG])
        hotc = sb("f_hotc", [128, 2, NP, TG], BF16)
        outT = sb("f_outT", [128, W])
        WK = [bank(f"f_WK{i}") for i in range(2)]
        IN = [bank(f"f_IN{i}") for i in range(2)]
        AA = [bank(f"f_AA{i}") for i in range(2)]
        OT = bank("f_OT")
        BK = OT[:, 256:512]
        SLOTS = (AA, IN)
        uses = ["z", "s0", "s1", "s2", "s3", "idx"]
        place = {u: (n % 2, n // 2) for n, u in enumerate(uses)}
        work_ready = [Count(sem(f"f_work_ready{b}"), 3) for b in range(2)]
        work_taken = [Count(sem(f"f_work_taken{b}"), 3) for b in range(2)]
        loaded, big_loaded, spare, filled = sem("f_loaded"), sem("f_big_loaded"), sem("f_spare"), sem("f_filled")
        comp_ready, comp_taken = sem("f_comp_ready"), sem("f_comp_taken")
        dve_step = Count(sem("f_dve_step"), 16)
        stats_done = Count(sem("f_stats_done"), 2)
        mv_done = Count(sem("f_mv_done"), 1)
        veps_done = Count(sem("f_veps_done"), 1)
        rstd_done = Count(sem("f_rstd_done"), 1)
        z_done = Count(sem("f_z_done"), 1)
        diff_done = Count(sem("f_diff_done"), 1)
        exp_done = Count(sem("f_exp_done"), 1)
        cols_done = Count(sem("f_cols_done"), 1)
        inner_ready = Count(sem("f_inner_ready"), 16)
        inner_taken = Count(sem("f_inner_taken"), 16)
        hot_done = Count(sem("f_hot_done"), len(GROUPS))
        hotc_done = [Count(sem(f"f_hotc_done{g}"), 1) for g in range(len(GROUPS))]
        hotp_done = [Count(sem(f"f_hotp_done{g}"), 3) for g in range(len(GROUPS))]
        aa_ready = [Count(sem(f"f_aa_ready{i}"), len(units[i::2])) for i in range(2)]
        aa_taken = [Count(sem(f"f_aa_taken{i}"), len(units[i::2])) for i in range(2)]
        out_ready = Count(sem("f_out_ready"), 1)
        out_taken = Count(sem("f_out_taken"), 1)
        back_ready = Count(sem("f_back_ready"), 1)
        added = Count(sem("f_added"), 1)
        start(nc)

        def upto(eng, count, it, k):
            eng.wait_ge(count.sem, count.after(it, k))

        def ready(eng, it, use):
            b, n = place[use]
            upto(eng, work_ready[b], it, n + 1)
            return WK[b]

        def taken(eng, it, use):
            b, n = place[use]
            upto(eng, work_taken[b], it, n + 1)

        def free(eng, it, use):
            b, n = place[use]
            upto(eng, work_taken[b], it, n)
            return WK[b]

        with ExitStack() as c2:
            qt = c2.enter_context(nc.sbuf_tensor("f_qt", [FK, 2 * HEADS, DIM], F32))
            kt = c2.enter_context(nc.sbuf_tensor("f_kt", [FK, 2 * HEADS, FK], F32))
            bt = c2.enter_context(nc.sbuf_tensor("f_bt", [FK, 2 * HEADS, C], F32))
            numbers = c2.enter_context(nc.sbuf_tensor("f_numbers", [128, 128], F32))
            block = c2.enter_context(nc.Block())

            @block.sync
            def _(sp):
                sp.dma_start(qt[:], ffnq_in).then_inc(loaded, 16)
                sp.dma_start(kt[:], ffnk_in).then_inc(loaded, 16)
                sp.dma_start(bt[:], ffnb_in).then_inc(loaded, 16)
                sp.dma_start(numbers[:], iota_in).then_inc(big_loaded, 16)
                sp.dma_start(wd[:], wdown_in).then_inc(big_loaded, 16)
                sp.dma_start(wu[:], wup_in).then_inc(big_loaded, 16)

            @block.tensor
            def _(pe):
                pe.wait_ge(loaded, 48)
                for n in range(2):
                    for s in range(8):
                        mm = nc.tensor.matmul(IN[n][:, s * FK:s * FK + FK], qt[:, 8 * n + s, :], kt[:, 8 * n + s, :],
                                              start=True, stop=True)
                    mm.then_inc(comp_ready, 1)
                for n in range(2):
                    for s in range(8):
                        mm = nc.tensor.matmul(AA[n][0:C, s * FK:s * FK + FK], bt[:, 8 * n + s, :], kt[:, 8 * n + s, :],
                                              start=True, stop=True)
                    mm.then_inc(comp_ready, 1)

            @block.vector
            def _(dve):
                for n in range(4):
                    dve.wait_ge(comp_ready, n + 1)
                    src = (IN + AA)[n]
                    dst = (wc, bc)[n // 2]
                    rows = (128, C)[n // 2]
                    nc.vector.tensor_copy(dst[:, (n % 2) * 512:(n % 2) * 512 + 512], src[0:rows, :]).then_inc(comp_taken, 1)
                dve.wait_ge(big_loaded, 48)
                nc.vector.tensor_copy(iota[:], numbers[:].rearrange("p (i o) -> p i o", o=1).to_broadcast([128, 128, TG]))
                nc.vector.memset(idx[:], 0.0).then_inc(filled, 1)
                nc.vector.memset(part[:], 0.0).then_inc(filled, 1)
                dve.wait_ge(comp_taken, 4)

        hot = sb("f_hot", [128, 2, 128, TG], BF16)
        act_in = sb("f_act", [128, NP, W])
        hotp = sb("f_hotp", [128, 2, 3, NP, TG], BF16)
        block = ctx.enter_context(nc.Block())
        steps = lambda eng: eng.Fori(0, B // 2)

        @block.tensor
        def _(pe):
            def scores(fr, par):
                ps = free(pe, fr, "z")
                upto(pe, z_done, fr, 1)
                for c in range(2):
                    mm = nc.tensor.transpose(ps[:, c * C:c * C + C], z[:, c, :], ident[0:C, 0:C])
                mm.then_inc(work_ready[place["z"][0]].sem, 1)
                taken(pe, fr, "z")
                for k in range(4):
                    ps = free(pe, fr, f"s{k}")
                    c, f = k // 2, k % 2
                    nc.tensor.matmul(ps[0:C, :], zT[:, par, c * C:c * C + C], wc[:, 512 * f:512 * f + 512],
                                     start=True, stop=True).then_inc(work_ready[place[f"s{k}"][0]].sem, 1)

            def turn_cols(fr):
                ps = free(pe, fr, "idx")
                upto(pe, cols_done, fr, 1)
                for k in range(3):
                    mm = nc.tensor.transpose(ps[:, k * C:k * C + C], cols[:, k, :], ident[0:C, 0:C])
                mm.then_inc(work_ready[place["idx"][0]].sem, 1)

            def inner(n, par):
                for k in range(NP // 2):
                    upto(pe, inner_taken, n, max(k - 1, 0))
                    for m in range(2):
                        mm = nc.tensor.matmul(IN[k % 2][:, m * W:m * W + W], wd[:, 2 * k + m, :], zT[:, par, :],
                                              start=True, stop=True)
                    mm.then_inc(inner_ready.sem, 1)

            def weights(n, g):
                upto(pe, hot_done, n, g + 1)
                upto(pe, hotp_done[g], n, 3)
                for u, (gu, t0, t1) in enumerate(units):
                    if gu != g:
                        continue
                    upto(pe, aa_taken[u % 2], n, u // 2)
                    if u == 1:
                        upto(pe, inner_taken, n, NP // 2)
                    for t in range(t0, t1):
                        tt = t - GROUPS[g][0]
                        col = (t - t0) * NP
                        for c in range(2):
                            for pt in range(3):
                                mm = nc.tensor.matmul(SLOTS[u % 2][c][:, col:col + NP], hot[64 * c:64 * c + 64, g % 2, :, tt],
                                                      hotp[64 * c:64 * c + 64, g % 2, pt, :, tt],
                                                      start=(pt == 0), stop=(pt == 2))
                    mm.then_inc(aa_ready[u % 2].sem, 1)

            pe.wait_ge(big_loaded, 48)
            scores(0, 0)
            turn_cols(0)
            with steps(pe) as it:
                for par in range(2):
                    n = it * 2 + par
                    scores(n + 1, 1 - par)
                    inner(n, par)
                    for g in range(len(GROUPS)):
                        weights(n, g)
                    for i in range(2):
                        upto(pe, aa_taken[i], n, aa_taken[i].per)
                    upto(pe, added, n, 0)
                    for k in range(NP):
                        if k == NP // 2:
                            turn_cols(n + 1)
                        mm = nc.tensor.matmul(OT[:, 0:W], wu[:, k, :], act_in[:, k, :], start=(k == 0), stop=(k == NP - 1))
                    mm.then_inc(out_ready.sem, 1)
                    upto(pe, out_taken, n, 1)
                    for c in range(2):
                        mm = nc.tensor.transpose(BK[0:C, c * 128:c * 128 + 128], outT[:, c * C:c * C + C], ident[:])
                    mm.then_inc(back_ready.sem, 1)

        @block.scalar
        def _(act):
            def copy_z(fr, par):
                ps = ready(act, fr, "z")
                nc.scalar.copy(zT[:, par, :], ps[:, 0:W]).then_inc(work_taken[place["z"][0]].sem, 1)

            def exps(fr):
                upto(act, diff_done, fr, 1)
                nc.scalar.activation(ex[:, 1], ex[:, 0], ACT.Exp).then_inc(exp_done.sem, 1)

            copy_z(0, 0)
            exps(0)
            with steps(act) as it:
                for par in range(2):
                    n = it * 2 + par
                    copy_z(n + 1, 1 - par)
                    upto(act, out_ready, n, 0)
                    act.sem_inc(spare, 1)
                    for k in range(NP // 2):
                        upto(act, inner_ready, n, k + 1)
                        nc.scalar.activation(act_in[:, 2 * k:2 * k + 2, :].rearrange("p n w -> p (n w)"), IN[k % 2][:, 0:2 * W],
                                             ACT.Relu).then_inc(inner_taken.sem, 1)
                    exps(n + 1)
                    upto(act, out_ready, n, 1)
                    nc.scalar.copy(outT[:], OT[:, 0:W]).then_inc(out_taken.sem, 1)

        def two_groups_on(eng, n, g):
            done = sum(per_group[:g - 1]) - 1
            upto(eng, aa_ready[done % 2], n, done // 2 + 1)

        @block.vector
        def _(dve):
            V = nc.vector
            segs = [(c, hd, side) for c in range(2) for hd in range(HEADS) for side in range(2)]
            n_step = [0]

            def mark(ins):
                n_step[0] = n_step[0] % dve_step.per + 1
                ins.then_inc(dve_step.sem, 1)

            def met(fr):
                upto(dve, dve_step, fr, n_step[0])
                dve.sem_inc(spare, 1)

            def then(ins, fr):
                mark(ins)
                met(fr)

            def statistics(fr, img):
                for c in range(2):
                    V.bn_stats(stats[:, c, :], h[:, img, c, :]).then_inc(stats_done.sem, 1)
                upto(dve, stats_done, fr, 2)
                dve.sem_inc(spare, 1)
                for c in range(2):
                    agg = V.bn_aggr(mv[:, c, :], stats[:, c, :])
                agg.then_inc(mv_done.sem, 1)

            def normalise(fr, img):
                upto(dve, rstd_done, fr, 1)
                for c in range(2):
                    zz = V.tensor_scalar(z[:, c, :], h[:, img, c, :], mv[:, c, 0:1], rstd[:, c:c + 1], ALU.subtract, ALU.mult)
                zz.then_inc(z_done.sem, 1)

            def copy_scores(fr):
                for k in range(4):
                    c, f = k // 2, k % 2
                    ps = ready(dve, fr, f"s{k}")
                    V.tensor_tensor(sc[:, c, 4 * f:4 * f + 4].rearrange("p h s k -> p (h s k)"), ps[0:C, :],
                                    bc[:, 512 * f:512 * f + 512], ALU.add).then_inc(work_taken[place[f"s{k}"][0]].sem, 1)

            def best_keys(fr):
                taken(dve, fr, "s2")
                taken(dve, fr, "s3")
                dve.sem_inc(spare, 1)
                for c, hd, side in segs:
                    last = V.max(top[:, c * HEADS + hd, side, :], sc[:, c, hd, side, :])
                mark(last)

            def key_numbers(fr):
                met(fr)
                for c, hd, side in segs:
                    last = V.max_index(topi[:, c * HEADS + hd, side, :], top[:, c * HEADS + hd, side, :], sc[:, c, hd, side, :])
                mark(V.tensor_tensor(pairs[:],
                                     top[:, :, 0, :].rearrange("p s (a o) -> p s a o", o=1).to_broadcast([C, SEG, TK, TK]),
                                     top[:, :, 1:2, :].to_broadcast([C, SEG, TK, TK]), ALU.add))

            def best_pairs(fr):
                met(fr)
                V.tensor_copy(topf[:], topi[:])
                for s in range(SEG):
                    last = V.max(best[:, s, :], pairs[:, s].rearrange("p a b -> p (a b)"))
                mark(last)

            def pair_numbers(fr):
                met(fr)
                V.tensor_tensor(ex[:, 0], best[:], best[:, :, 0:1].to_broadcast([C, SEG, TK]), ALU.subtract).then_inc(diff_done.sem, 1)
                for s in range(SEG):
                    last = V.max_index(besti[:, s, :], best[:, s, :], pairs[:, s].rearrange("p a b -> p (a b)"))
                mark(last)

            def ranks(fr):
                met(fr)
                V.tensor_scalar(rank[:, 0], besti[:], 3, None, ALU.logical_shift_right)
                then(V.tensor_scalar(rank[:, 1], besti[:], 7, None, ALU.bitwise_and), fr)
                mark(V.tensor_copy(rankf[:], rank[:]))

            def numbers_at_ranks(fr):
                met(fr)
                for side in range(2):
                    for a in range(TK):
                        last = V.scalar_tensor_tensor(pick[:, side, :, :, a], rankf[:, side], float(a),
                                                      topf[:, :, side, a:a + 1].to_broadcast([C, SEG, TK]),
                                                      ALU.is_equal, ALU.mult)
                mark(last)

            def add_up(fr):
                met(fr)
                mark(V.tensor_reduce(got[:].rearrange("p d s k -> p (d s k)"), pick.rearrange("p d s k a -> p (d s k) a"),
                                     axis=AX.X, op=ALU.add))

            def places(fr):
                met(fr)
                mark(V.tensor_copy(goti[:, 0, :], got[:, 1].rearrange("p s k -> p (s k)")))
                upto(dve, exp_done, fr, 1)
                esums = V.tensor_reduce(esum[:, 0, :], ex[:, 1], axis=AX.X, op=ALU.add)
                mark(esums)
                met(fr)
                V.tensor_scalar(goti[:, 1, :], goti[:, 0, :], 1, None, ALU.logical_shift_right)
                V.tensor_scalar(goti[:, 2, :], goti[:, 0, :], 1, None, ALU.bitwise_and)
                then(V.reciprocal(esum[:, 1, :], esum[:, 0, :]), fr)
                V.tensor_copy(cols[:, 1, :], goti[:, 1, :])
                V.tensor_copy(gotf[:, 0, :], goti[:, 2, :])
                then(V.tensor_tensor(cols[:, 2, :].rearrange("p (s k) -> p s k", k=TK), ex[:, 1],
                                     esum[:, 1, :].rearrange("p (s o) -> p s o", o=1).to_broadcast([C, SEG, TK]),
                                     ALU.mult), fr)
                V.scalar_tensor_tensor(cols[:, 0, :], gotf[:, 0, :], float(FK), got[:, 0].rearrange("p s k -> p (s k)"),
                                       ALU.mult, ALU.add).then_inc(cols_done.sem, 1)

            def split_cols(fr):
                ps = ready(dve, fr, "idx")
                wt = ps[:, 2 * C:3 * C]
                mark(V.tensor_copy(part[:, 0, 0:C], wt))
                V.tensor_copy(idx[:, :, 0:C], ps[:, 0:2 * C].rearrange("p (n t) -> p n t", n=2))
                met(fr)
                then(V.tensor_tensor(rest[:, 0, 0:C], wt, part[:, 0, 0:C], ALU.subtract), fr)
                then(V.tensor_copy(part[:, 1, 0:C], rest[:, 0, 0:C]), fr)
                then(V.tensor_tensor(rest[:, 1, 0:C], rest[:, 0, 0:C], part[:, 1, 0:C], ALU.subtract), fr)
                V.tensor_copy(part[:, 2, 0:C], rest[:, 1, 0:C]).then_inc(work_taken[place["idx"][0]].sem, 1)
                taken(dve, fr, "idx")

            def hot_cols(n, g):
                t0 = GROUPS[g][0]
                V.tensor_tensor(hotc[:, g % 2], idx[:, 1:2, t0:t0 + TG].to_broadcast([128, NP, TG]), iota[:, 0:NP, :],
                                ALU.is_equal).then_inc(hotc_done[g].sem, 1)

            def hot_rows(n, g):
                t0 = GROUPS[g][0]
                if g >= 2:
                    two_groups_on(dve, n, g)
                V.tensor_tensor(hot[:, g % 2], idx[:, 0:1, t0:t0 + TG].to_broadcast([128, 128, TG]), iota[:],
                                ALU.is_equal).then_inc(hot_done.sem, 1)

            def first_hots(n):
                hot_cols(n, 0)
                hot_cols(n, 1)
                hot_rows(n, 0)

            def weigh(n, *which):
                for u in which:
                    _, t0, t1 = units[u]
                    if u == 0:
                        upto(dve, inner_taken, n, NP // 2)
                    upto(dve, aa_ready[u % 2], n, u // 2 + 1)
                    for c in range(2):
                        sl = act_in[:, :, c * C + t0:c * C + t1]
                        last = V.tensor_tensor(sl, sl, SLOTS[u % 2][c][:, 0:(t1 - t0) * NP].rearrange("p (t n) -> p n t", n=NP),
                                               ALU.mult)
                    last.then_inc(aa_taken[u % 2].sem, 1)

            dve.wait_ge(filled, 3)
            dve.wait_ge(big_loaded, 48)
            statistics(0, 0)
            normalise(0, 0)
            copy_scores(0)
            best_keys(0)
            statistics(1, 1)
            normalise(1, 1)
            for stage in (key_numbers, best_pairs, pair_numbers, ranks, numbers_at_ranks, add_up, places, split_cols):
                stage(0)
            first_hots(0)
            assert n_step[0] == dve_step.per, n_step
            with steps(dve) as it:
                for par in range(2):
                    n = it * 2 + par
                    fr = n + 1
                    copy_scores(fr)
                    best_keys(fr)
                    hot_rows(n, 1)
                    upto(dve, hotp_done[0], n, 3)
                    hot_cols(n, 2)
                    key_numbers(fr)
                    statistics(fr + 1, (fr + 1) % B)
                    best_pairs(fr)
                    weigh(n, 0, 1)
                    hot_rows(n, 2)
                    weigh(n, 2)
                    pair_numbers(fr)
                    weigh(n, 3)
                    ranks(fr)
                    normalise(fr + 1, (fr + 1) % B)
                    weigh(n, *range(4, len(units)))
                    numbers_at_ranks(fr)
                    add_up(fr)
                    places(fr)
                    split_cols(fr)
                    first_hots(fr)
                    upto(dve, back_ready, n, 1)
                    hp = h[:, bass.ds(n, 1), :, :].rearrange("p i c d -> p (i c d)")
                    V.tensor_tensor(hp, hp, BK[0:C, 0:2 * DIM], ALU.add).then_inc(added.sem, 1)
                    upto(dve, added, n, 1)
                    dve.sem_inc(spare, 1)

        @block.gpsimd
        def _(pool):
            def deviations(fr):
                upto(pool, mv_done, fr, 1)
                pool.sem_inc(spare, 1)
                nc.gpsimd.tensor_scalar(rstd[:], mv[:, :, 1], EPS, None, ALU.add).then_inc(veps_done.sem, 1)
                upto(pool, veps_done, fr, 1)
                nc.gpsimd.tensor_tensor(rstd[:], rstd[:], neghalf[:], ALU.pow).then_inc(rstd_done.sem, 1)

            def hot_weights(n, g):
                upto(pool, hotc_done[g], n, 1)
                pool.sem_inc(spare, 1)
                t0 = GROUPS[g][0]
                for pt in range(3):
                    nc.gpsimd.tensor_tensor(hotp[:, g % 2, pt], hotc[:, g % 2],
                                            part[:, pt:pt + 1, t0:t0 + TG].to_broadcast([128, NP, TG]),
                                            ALU.mult).then_inc(hotp_done[g].sem, 1)

            nc.gpsimd.memset(neghalf[:], -0.5).then_inc(filled, 1)
            pool.wait_ge(filled, 3)
            deviations(0)
            deviations(1)
            hot_weights(0, 0)
            with steps(pool) as it:
                for par in range(2):
                    n = it * 2 + par
                    hot_weights(n, 1)
                    deviations(n + 2)
                    two_groups_on(pool, n, 2)
                    pool.sem_inc(spare, 1)
                    hot_weights(n, 2)
                    hot_weights(n + 1, 0)


def build(nc, B, DEPTH, x_in, base_in, convw_in, layer_in, ident_in, normw_in, cls_in, attw_in, ffnq_in, ffnk_in, ffnb_in, iota_in, wdown_in, wup_in, out):
    with ExitStack() as ctx:
        h = ctx.enter_context(nc.sbuf_tensor("h", [C, B, 2, DIM], F32))
        ident = ctx.enter_context(nc.sbuf_tensor("ident", [128, 128], F32))
        ident_loaded = ctx.enter_context(nc.semaphore("ident_loaded"))
        with nc.Block() as block:
            @block.sync
            def _(sp):
                sp.dma_start(ident[:], ident_in).then_inc(ident_loaded, 16)
                sp.wait_ge(ident_loaded, 16)
        with ExitStack() as c2:
            build_tower(nc, c2, B, DEPTH, x_in, base_in, convw_in, layer_in, h, ident)
        build_norm(nc, B, normw_in, cls_in, h)
        build_attention(nc, B, attw_in, h, ident)
        build_ffn(nc, B, ffnq_in, ffnk_in, ffnb_in, iota_in, wdown_in, wup_in, h, ident)
        with ExitStack() as c2:
            stored = c2.enter_context(nc.semaphore("stored"))
            block = c2.enter_context(nc.Block())

            @block.sync
            def _(sp):
                first = 2 + C
                sp.dma_start(out[:, 2:first].rearrange("b p d -> p b d"), h[:, :, 0, :]).then_inc(stored, 16)
                sp.dma_start(out[:, first:W].rearrange("b p d -> p b d"), h[0:W - first, :, 1, :]).then_inc(stored, 16)
                for slot, row in ((C - 2, 1), (C - 1, 0)):
                    sp.dma_start(out[:, row:row + 1].rearrange("b p d -> p b d"), h[slot:slot + 1, :, 1, :]).then_inc(stored, 16)
                sp.wait_ge(stored, 64)


def lay_out(inputs, B):
    import numpy as np
    f = np.float32
    x = np.asarray(inputs["x"])[:B]
    x = x.reshape(B, 3, 14, 16, 14, 16).transpose(0, 1, 3, 5, 2, 4).reshape(B, KC, 128, PATCHES)
    x = np.ascontiguousarray(x.transpose(0, 2, 1, 3))
    cw = np.asarray(inputs["L0_tok_conv_w"]).reshape(KC, 128, DIM).transpose(1, 0, 2)
    pos = np.asarray(inputs["L0_tok_pos_embed"])[0]
    base = np.zeros((2, W, DIM), f)
    base[0, :PATCHES] = pos[1:]
    base[0, PATCHES] = pos[0]
    base[1, :PATCHES] = np.asarray(inputs["L0_tok_conv_b"])
    base[1, PATCHES] = np.asarray(inputs["L0_tok_cls_token"])[0, 0]
    base = base.reshape(2, 2, C, DIM).transpose(2, 0, 1, 3)
    g = lambda n: np.asarray(inputs["L0_tok_" + n])
    L = g("qkv_w").shape[0]
    wt = np.zeros((L, 128, NW), f)
    by_dim = np.arange(DIM).reshape(HEADS, HD).T.reshape(-1)
    wt[:, :, QW:QW + 128], wt[:, :, KW:KW + 128] = g("qkv_w")[:, :, by_dim], g("qkv_w")[:, :, DIM + by_dim]
    wt[:, :, QB], wt[:, :, KB] = g("qkv_b")[:, by_dim], g("qkv_b")[:, DIM + by_dim]
    wt[:, :, VW:VW + 128] = g("qkv_w")[:, :, 256:]
    wt[:, :, PW:PW + 128] = g("proj_w")
    wt[:, :, F1W:F1W + 256] = g("fc1_w")
    wt[:, :, F2W:F2W + 256] = g("fc2_w").reshape(L, 2, 128, DIM).transpose(0, 2, 1, 3).reshape(L, 128, 256)
    wt[:, :, VB:VB + 128] = g("qkv_b")[:, None, 256:]
    wt[:, :, PB:PB + 128] = g("proj_b")[:, None]
    wt[:, :, F2B:F2B + 128] = g("fc2_b")[:, None]
    for col, n in ((LN1W, "ln1_w"), (LN1B, "ln1_b"), (LN2W, "ln2_w"), (LN2B, "ln2_b")):
        wt[:, :, col] = g(n)
    wt[:, :, F1B:F1B + 2] = g("fc1_b").reshape(L, 2, 128).transpose(0, 2, 1)
    nw = np.stack([g("norm_w"), g("norm_b")])
    normw = np.ascontiguousarray(np.broadcast_to(nw, (C, 2, DIM)))
    cls = np.ascontiguousarray(np.broadcast_to(np.asarray(inputs["cls_tok"])[0], (B, DIM)))[None]
    a = lambda n: np.asarray(inputs["L0_attn_" + n])
    at = np.zeros((128, ANW), f)
    at[:, AQ:AQ + 128], at[:, AK:AK + 128], at[:, AV:AV + 128] = a("Wq").T, a("Wk").T, a("Wv").T
    for hd in range(HEADS):
        gr, half = hd % 4, hd // 4
        at[32 * gr:32 * gr + HD, AO + 128 * half:AO + 128 * half + 128] = a("Wo").T[HD * hd:HD * hd + HD]
        at[HD * hd:HD * hd + HD, AMASK + hd] = 2.0
    q = lambda n: np.asarray(inputs["L0_ffn_" + n])
    SH = 2 * HEADS
    fq = np.ascontiguousarray(q("Wq").reshape(DIM, SH, FK).transpose(2, 1, 0))
    fk = np.ascontiguousarray(q("keys").reshape(SH, FK, FK).transpose(2, 0, 1))
    fb = np.ascontiguousarray(np.broadcast_to(q("bq").reshape(SH, FK).T[:, :, None], (FK, SH, C)))
    iota = np.ascontiguousarray(np.broadcast_to(np.arange(128, dtype=f), (128, 128)))
    wd = q("w_down").reshape(FK, NP, 2, DIM).transpose(3, 1, 2, 0).reshape(DIM, NP, 128)
    wu = q("w_up").reshape(FK, NP, 2, DIM).transpose(2, 0, 1, 3).reshape(128, NP, DIM)
    return {"ffnq_in": fq, "ffnk_in": fk, "ffnb_in": fb, "iota_in": iota, "wdown_in": np.ascontiguousarray(wd),
            "wup_in": np.ascontiguousarray(wu), "normw_in": normw, "cls_in": cls, "attw_in": at, "x_in": x, "base_in": np.ascontiguousarray(base), "convw_in": np.ascontiguousarray(cw),
            "layer_in": wt, "ident_in": np.eye(128, dtype=f)}


def kernel(**inputs):
    import concourse.bacc as bacc
    from concourse.bass_utils import run_bass_kernel_spmd

    B = inputs["x"].shape[0]
    arrays = lay_out(inputs, B)
    nc = bacc.Bacc("TRN2", target_bir_lowering=False, num_devices=1)
    aps = {name: nc.dram_tensor(name, a.shape, mybir.dt.from_np(a.dtype), kind="ExternalInput").ap()
           for name, a in arrays.items()}
    out = nc.dram_tensor("out", (B, W, DIM), F32, kind="ExternalOutput").ap()
    build(nc, B, inputs["L0_tok_qkv_w"].shape[0], out=out, **aps)
    return run_bass_kernel_spmd(nc, [arrays], core_ids=[0]).results[0]["out"]
```
